# Optimizing a Trainium2 kernel written in Bass

```python
import numpy as np
import jax
import jax.numpy as jnp

def _softmax(x, axis=-1):
    return jax.nn.softmax(x, axis=axis)

def _gelu(x):
    return jax.nn.gelu(x, approximate=True)

def _silu(x):
    return jax.nn.silu(x)

def _sigmoid(x):
    return jax.nn.sigmoid(x)

def _layernorm(x, axis=-1, eps=1e-05):
    m = jnp.mean(x, axis=axis, keepdims=True)
    v = jnp.var(x, axis=axis, keepdims=True)
    return (x - m) / jnp.sqrt(v + eps)

def _scatter_add(tgt, idx, src, axis=0):
    return tgt.at[idx].add(src)

def _segment_sum(src, seg, n):
    return jax.ops.segment_sum(src, seg, n)
kernel_name = 'mk_conv_attn_hybrid_d2_conv_nchw1024_r4_29b6e8'

def setup_inputs(seed: int=0):
    np.random.seed(seed)
    _w = jnp.asarray

    def _rec_inputs():
        import jax
        import jax.numpy as jnp
        _gk = jax.random.key(seed)
        x = -0.0003957 + 1 * jax.random.normal(jax.random.fold_in(_gk, 1), (16, 256, 14, 14), jnp.float32)
        return x
    x = _rec_inputs()

    def _L0_conv_setup():
        import jax, jax.numpy as jnp
        import numpy as np
        EPS = 1e-05

        def _conv(x, w, b, stride, pad):
            y = jax.lax.conv_general_dilated(x, w, window_strides=(stride, stride), padding=[(pad, pad), (pad, pad)], dimension_numbers=('NCHW', 'OIHW', 'NCHW'))
            return y + b.reshape(1, -1, 1, 1)

        def _bn(x, gamma, beta):
            mean = jnp.mean(x, axis=(0, 2, 3), keepdims=True)
            var = jnp.var(x, axis=(0, 2, 3), keepdims=True)
            xn = (x - mean) * jax.lax.rsqrt(var + EPS)
            return gamma.reshape(1, -1, 1, 1) * xn + beta.reshape(1, -1, 1, 1)
        key = jax.random.key(seed)
        ks = jax.random.split(key, 8)
        N, Cin, H, W = (16, 256, 14, 14)
        P = 64
        Cout = P * 4

        def kaiming(k, shape):
            fan_in = shape[1] * shape[2] * shape[3]
            return jax.random.normal(k, shape, jnp.float32) * np.float32(np.sqrt(2.0 / fan_in))
        return {'x': jax.random.normal(ks[0], (N, Cin, H, W), jnp.float32), 'w1': kaiming(ks[1], (P, Cin, 1, 1)), 'b1': jnp.zeros((P,), jnp.float32), 'g1': jnp.ones((P,), jnp.float32), 'be1': jnp.zeros((P,), jnp.float32), 'w2': kaiming(ks[2], (P, P, 3, 3)), 'b2': jnp.zeros((P,), jnp.float32), 'g2': jnp.ones((P,), jnp.float32), 'be2': jnp.zeros((P,), jnp.float32), 'w3': kaiming(ks[3], (Cout, P, 1, 1)), 'b3': jnp.zeros((Cout,), jnp.float32), 'g3': jnp.ones((Cout,), jnp.float32), 'be3': jnp.zeros((Cout,), jnp.float32), 'residual_scale': jnp.zeros((1,), jnp.float32)}
    _L0_conv_all = _L0_conv_setup()
    _L0_conv_in = {k: v for k, v in _L0_conv_all.items() if k in ('w1', 'b1', 'g1', 'be1', 'w2', 'b2', 'g2', 'be2', 'w3', 'b3', 'g3', 'be3', 'residual_scale')}
    del _L0_conv_all

    def _L1_attn_setup():
        import jax, jax.numpy as jnp
        import numpy as np
        HEADS = 16
        DIM_HEAD = 16
        SCALE = DIM_HEAD ** (-0.5)
        key = jax.random.key(seed)
        k1, k2, k3 = jax.random.split(key, 3)
        B, N, D = (4, 2048, 256)
        inner = HEADS * DIM_HEAD
        x = jax.random.normal(k1, (B, N, D), dtype=jnp.float32)
        w_qkv = jax.random.normal(k2, (D, 3 * inner), dtype=jnp.float32) * D ** (-0.5)
        w_out = jax.random.normal(k3, (inner, D), dtype=jnp.float32) * inner ** (-0.5)
        b_out = jnp.zeros((D,), dtype=jnp.float32)
        return {'x': x, 'w_qkv': w_qkv, 'w_out': w_out, 'b_out': b_out}
    _L1_attn_all = _L1_attn_setup()
    _L1_attn_in = {k: v for k, v in _L1_attn_all.items() if k in ('w_qkv', 'w_out', 'b_out')}
    del _L1_attn_all

    def _L1_ffn_setup():
        import jax, jax.numpy as jnp
        import numpy as np
        TOP_K = 2
        key = jax.random.key(seed)
        ks = jax.random.split(key, 7)
        E, D, F = (8, 256, 1024)
        B, S = (4, 512)
        s_in = 1.0 / np.sqrt(D)
        s_ff = 1.0 / np.sqrt(F)
        return {'x': jax.random.normal(ks[0], (B, S, D), jnp.float32), 'gate_w': jax.random.normal(ks[1], (D, E), jnp.float32) * s_in, 'gate_b': jax.random.normal(ks[2], (E,), jnp.float32) * 0.01, 'w1': jax.random.normal(ks[3], (E, D, F), jnp.float32) * s_in, 'b1': jax.random.normal(ks[4], (E, F), jnp.float32) * 0.01, 'w2': jax.random.normal(ks[5], (E, F, D), jnp.float32) * s_ff, 'b2': jax.random.normal(ks[6], (E, D), jnp.float32) * 0.01}
    _L1_ffn_all = _L1_ffn_setup()
    _L1_ffn_in = {k: v for k, v in _L1_ffn_all.items() if k in ('gate_w', 'gate_b', 'w1', 'b1', 'w2', 'b2')}
    del _L1_ffn_all
    return {'x': x, 'L0_conv_w1': _L0_conv_in['w1'], 'L0_conv_b1': _L0_conv_in['b1'], 'L0_conv_g1': _L0_conv_in['g1'], 'L0_conv_be1': _L0_conv_in['be1'], 'L0_conv_w2': _L0_conv_in['w2'], 'L0_conv_b2': _L0_conv_in['b2'], 'L0_conv_g2': _L0_conv_in['g2'], 'L0_conv_be2': _L0_conv_in['be2'], 'L0_conv_w3': _L0_conv_in['w3'], 'L0_conv_b3': _L0_conv_in['b3'], 'L0_conv_g3': _L0_conv_in['g3'], 'L0_conv_be3': _L0_conv_in['be3'], 'L0_conv_residual_scale': _L0_conv_in['residual_scale'], 'L1_attn_w_qkv': _L1_attn_in['w_qkv'], 'L1_attn_w_out': _L1_attn_in['w_out'], 'L1_attn_b_out': _L1_attn_in['b_out'], 'L1_ffn_gate_w': _L1_ffn_in['gate_w'], 'L1_ffn_gate_b': _L1_ffn_in['gate_b'], 'L1_ffn_w1': _L1_ffn_in['w1'], 'L1_ffn_b1': _L1_ffn_in['b1'], 'L1_ffn_w2': _L1_ffn_in['w2'], 'L1_ffn_b2': _L1_ffn_in['b2']}

def reference(x, L0_conv_w1, L0_conv_b1, L0_conv_g1, L0_conv_be1, L0_conv_w2, L0_conv_b2, L0_conv_g2, L0_conv_be2, L0_conv_w3, L0_conv_b3, L0_conv_g3, L0_conv_be3, L0_conv_residual_scale, L1_attn_w_qkv, L1_attn_w_out, L1_attn_b_out, L1_ffn_gate_w, L1_ffn_gate_b, L1_ffn_w1, L1_ffn_b1, L1_ffn_w2, L1_ffn_b2):
    import jax
    import jax.numpy as jnp

    def _L0_conv_ref(x, w1, b1, g1, be1, w2, b2, g2, be2, w3, b3, g3, be3, residual_scale):
        import jax, jax.numpy as jnp
        import numpy as np
        EPS = 1e-05

        def _conv(x, w, b, stride, pad):
            y = jax.lax.conv_general_dilated(x, w, window_strides=(stride, stride), padding=[(pad, pad), (pad, pad)], dimension_numbers=('NCHW', 'OIHW', 'NCHW'))
            return y + b.reshape(1, -1, 1, 1)

        def _bn(x, gamma, beta):
            mean = jnp.mean(x, axis=(0, 2, 3), keepdims=True)
            var = jnp.var(x, axis=(0, 2, 3), keepdims=True)
            xn = (x - mean) * jax.lax.rsqrt(var + EPS)
            return gamma.reshape(1, -1, 1, 1) * xn + beta.reshape(1, -1, 1, 1)
        out = jax.nn.relu(_bn(_conv(x, w1, b1, 1, 0), g1, be1))
        out = jax.nn.relu(_bn(_conv(out, w2, b2, 1, 1), g2, be2))
        out = _bn(_conv(out, w3, b3, 1, 0), g3, be3)
        out = jax.nn.softplus(residual_scale)[0] * out
        out = x + out
        return jax.nn.relu(out)

    def _L1_attn_ref(x, w_qkv, w_out, b_out):
        import jax, jax.numpy as jnp
        import numpy as np
        HEADS = 16
        DIM_HEAD = 16
        SCALE = DIM_HEAD ** (-0.5)
        B, N, D = x.shape
        h, d = (HEADS, DIM_HEAD)
        qkv = x @ w_qkv
        q, k, v = jnp.split(qkv, 3, axis=-1)

        def to_heads(t):
            return t.reshape(B, N, h, d).transpose(0, 2, 1, 3).reshape(B * h, N, d)
        q, k, v = map(to_heads, (q, k, v))
        q = jax.nn.softmax(q * SCALE, axis=-1)
        k = jax.nn.softmax(k, axis=-2)
        context = jnp.einsum('bnd,bne->bde', q, k)
        out = jnp.einsum('bde,bnd->bne', context, v)
        out = out.reshape(B, h, N, d).transpose(0, 2, 1, 3).reshape(B, N, h * d)
        return out @ w_out + b_out

    def _L1_ffn_ref(x, gate_w, gate_b, w1, b1, w2, b2):
        import jax, jax.numpy as jnp
        import numpy as np
        TOP_K = 2
        B, S, D = x.shape
        E = gate_b.shape[0]
        flat = x.reshape(-1, D)
        T = flat.shape[0]
        logits = flat @ gate_w + gate_b
        probs = jax.nn.softmax(logits, axis=-1)
        top_p, top_i = jax.lax.top_k(probs, TOP_K)
        top_w = top_p / (jnp.sum(top_p, axis=-1, keepdims=True) + 1e-09)
        rows = jnp.arange(T)[:, None]
        comb = jnp.zeros((T, E), dtype=flat.dtype).at[rows, top_i].add(top_w)
        out = jnp.zeros_like(flat)
        for e in range(E):
            h = jax.nn.gelu(flat @ w1[e] + b1[e], approximate=False)
            y = h @ w2[e] + b2[e]
            out = out + comb[:, e:e + 1] * y
        return out.reshape(B, S, D)

    def _gn(v, G=32, eps=1e-05):
        B_, C_, H_, W_ = v.shape
        g = v.reshape(B_, G, C_ // G, H_, W_)
        m = jnp.mean(g, axis=(2, 3, 4), keepdims=True)
        s = jnp.var(g, axis=(2, 3, 4), keepdims=True)
        return ((g - m) / jnp.sqrt(s + eps)).reshape(v.shape)

    def _ln_c(v, eps=1e-06):
        m = jnp.mean(v, axis=1, keepdims=True)
        s = jnp.var(v, axis=1, keepdims=True)
        return (v - m) / jnp.sqrt(s + eps)

    def _ln_t(v, eps=1e-05):
        m = jnp.mean(v, axis=-1, keepdims=True)
        s = jnp.var(v, axis=-1, keepdims=True)
        return (v - m) / jnp.sqrt(s + eps)

    def _to_tokens(v):
        B_, C_, H_, W_ = v.shape
        return v.reshape(B_, C_, H_ * W_).transpose(0, 2, 1)

    def _from_tokens(t, like):
        B_, C_, H_, W_ = like.shape
        return t.transpose(0, 2, 1).reshape(B_, C_, H_, W_)
    x = _L0_conv_ref(x, L0_conv_w1, L0_conv_b1, L0_conv_g1, L0_conv_be1, L0_conv_w2, L0_conv_b2, L0_conv_g2, L0_conv_be2, L0_conv_w3, L0_conv_b3, L0_conv_g3, L0_conv_be3, L0_conv_residual_scale)
    t = _to_tokens(x)
    t = t + _L1_attn_ref(_ln_t(t), L1_attn_w_qkv, L1_attn_w_out, L1_attn_b_out)
    t = t + _L1_ffn_ref(_ln_t(t), L1_ffn_gate_w, L1_ffn_gate_b, L1_ffn_w1, L1_ffn_b1, L1_ffn_w2, L1_ffn_b2)
    x = _from_tokens(t, x)
    return x

_drawn_inputs = setup_inputs


def setup_inputs(seed=0):
    import zlib

    import numpy as np

    out = dict(_drawn_inputs(seed))
    spreads = {'L0_conv_b1': (0.0, 0.8),
     'L0_conv_g1': (1.0, 0.2),
     'L0_conv_be1': (0.0, 0.1),
     'L0_conv_b2': (0.0, 0.8),
     'L0_conv_g2': (1.0, 0.2),
     'L0_conv_be2': (0.0, 0.1),
     'L0_conv_b3': (0.0, 0.8),
     'L0_conv_g3': (1.0, 0.2),
     'L0_conv_be3': (0.0, 0.1),
     'L1_attn_b_out': (0.0, 0.1)}
    factors = {'L1_ffn_b1': 8.0, 'L1_ffn_b2': 7.712}
    for name, (base, spread) in spreads.items():
        noise = np.random.default_rng([zlib.crc32(name.encode()), seed]).standard_normal(out[name].shape)
        drawn = base * np.exp(spread * noise) if base else spread * noise
        out[name] = jnp.asarray(drawn.astype(out[name].dtype))
    for name, factor in factors.items():
        out[name] = (out[name] * factor).astype(out[name].dtype)
    return out
```

```python
from contextlib import ExitStack

import concourse.bass as bass
from concourse import mybir

F32 = mybir.dt.float32
I32 = mybir.dt.int32
U32 = mybir.dt.uint32
ALU = mybir.AluOpType
ACT = mybir.ActivationFunctionType
X = mybir.AxisListType.X

B, C, HW, SIDE = 16, 256, 196, 14
TOKENS = B * HW
MID = 64
HALF = HW // 2
TILES = B * 2
CHUNKS = 8
CW = 2 * HW
HEADS, DH = 16, 16
E, FF = 8, 1024
BN_EPS = LN_EPS = 1e-5
CAP = TOKENS + 128
ROW = C + 1 + E
SLOTS = (2 * TOKENS - E) // 128 + E
W2OFF, B1OFF, B2OFF = 2 * FF, 4 * FF, 5 * FF
WSET = 5 * FF + C

STEPS_A = {
    "vec": ["mix0", "mix1", "stat0", "stat1", "agg0", "agg1", "eps", "nr0", "nr1", "nr2", "nr3", "norm0", "norm1"],
    "act": ["relu0", "relu1", "keep", "ln", "exp", "xT"],
    "pe": ["turn", "xT", "q", "k", "v"],
    "pool": ["bias"],
}
STEPS_B = {
    "vec": ["kmax", "kneg", "qmax", "qsub", "qsum", "qrec", "krec", "ctx0", "ctx1", "add"],
    "act": ["kexp0", "kexp1", "qexp", "v", "kT", "proj"],
    "pe": ["kT", "ctx", "proj", "out"],
    "pool": ["q"],
}
STEPS_C = {
    "vec": ["stat0", "stat1", "agg0", "agg1", "eps", "nr0", "nr1", "nr2", "nr3", "norm0", "norm1"],
    "act": ["ln", "exp", "xT"],
    "pe": ["xT", "logits"],
}
STEPS_R = {
    "vec": ["bias", "max", "sub", "sum", "rec", "prob", "top0", "top1", "top2", "top3", "at0", "at1", "at2", "at3",
            "atf", "one1", "one2", "both", "den", "denr", "comb", "scale", "run0", "run1", "run2", "run3",
            "pos", "pos1", "slot1", "pos2", "slot2", "slots"],
    "act": ["exp"],
    "pe": ["rank"],
}


def after(steps, name, i):
    return i * len(steps) + steps.index(name) + 1


def moe_block(nc, x, w1t, b1, g1, be1, w2t, b2, g2, be2, w3t, b3, g3, be3, res_scale,
              wqkv, wout, bout, gate_w, gate_b, ew1, eb1, ew2, eb2, out):
    disp = nc.dram_tensor("dispatch", [E * CAP + 128, ROW], F32, kind="Internal").ap()
    ctx = ExitStack()
    with ctx:
        def sb(name, shape, dt=F32):
            return ctx.enter_context(nc.sbuf_tensor(name, shape, dt))

        def sem(name):
            return ctx.enter_context(nc.semaphore(name))

        img = sb("img", [128, B, 4 * HW])
        pad = sb("pad", [128, B * 256])
        mid2 = sb("mid2", [128, TOKENS])
        w1s = sb("w1s", [128, 2, 128])
        w2s = sb("w2s", [128, 6, MID])
        w3s = sb("w3s", [MID, C])
        vecs = sb("vecs", [128, 3, 4, 2])
        bst = sb("bst", [128, 2, CHUNKS, 6])
        bmv = sb("bmv", [128, 2, 2])
        bn = sb("bn", [128, 8, 2])
        rs = sb("rs", [128, 6])
        coef = sb("coef", [128, 3, 2, 2])
        wq = sb("wq", [128, 2, 3 * C])
        wo = sb("wo", [128, 2, C])
        bo2 = sb("bo2", [HALF, 2, C])
        gw = sb("gw", [128, 2, E])
        gb = sb("gb", [HALF, 4, E])
        ident = sb("ident", [128, 128])
        ones = sb("ones", [HALF, 128])
        upper = sb("upper", [HALF, HALF])
        heads = sb("heads", [128, 128])
        iot = sb("iot", [128, 64], I32)
        expert_id = sb("expert_id", [HALF, 4, E])
        expert_row = sb("expert_row", [HALF, 4, E])
        tokid_i = sb("tokid_i", [HALF, TILES], I32)
        tc = sb("tc", [128, 2, 2, HW])
        xh = sb("xh", [HALF, 2, 2, C])
        xT = sb("xT", [128, 2, 2, HW])
        stt = sb("stt", [HALF, 2, 2, 2, 6])
        mv = sb("mv", [HALF, 2, 2, 2, 2])
        sm = sb("sm", [HALF, 2, 2, 6, 2])
        qe = sb("qe", [HALF, 2, 2 * C])
        qn = sb("qn", [HALF, 2, 2 * C])
        qr = sb("qr", [HALF, 2, 3, 2 * HEADS])
        kx = sb("kx", [128, 2, 4, 2])
        ek = sb("ek", [128, 2, 2, HW])
        vT = sb("vT", [128, 2, 2, HW])
        ekt = sb("ekt", [HALF, 2, 2, C])
        cT = sb("cT", [128, 2, 2, 128])
        pr = sb("pr", [128, 2, 2, C])
        rows = sb("rows", [HALF, 4, 2, ROW])
        xT2 = sb("xT2", [128, 2, 2, HW])
        lg = sb("lg", [HALF, 2, 4, E])
        rt = sb("rt", [HALF, 12, 4, E])
        rv = sb("rv", [HALF, 2, 8, 4])
        top = sb("top", [HALF, 4, 8])
        topi = sb("topi", [HALF, 4, 8], U32)
        topf = sb("topf", [HALF, 4, 2])
        run = sb("run", [HALF, 2, 5, E])
        slot = sb("slot", [HALF, 2, 2, 4], U32)
        cnt = sb("cnt", [128, E])
        cnti = sb("cnti", [128, 3, E], I32)
        ntl = sb("ntl", [128, 3, E])
        padi = sb("padi", [128, E], U32)
        padrow = sb("padrow", [128, ROW])
        lt = sb("lt", [1, E, E])
        big = sb("big", [1, 2, 64, E])
        tb = sb("tb", [1, 8, 64])
        tbi = sb("tbi", [1, 8, 64], I32)
        wset = sb("wset", [128, 2 * WSET])
        xr = sb("xr", [128, 2, ROW])
        xrT = sb("xrT", [128, 2, C])
        hb = pad[:, 0:2 * FF].rearrange("p (a f) -> p a f", a=2)
        hT = pad[:, 2 * FF:4 * FF].rearrange("p (a f) -> p a f", a=2)
        yb = mid2[:, 0:2 * C].rearrange("p (a d) -> p a d", a=2)
        ys = mid2[:, 2 * C:4 * C].rearrange("p (a d) -> p a d", a=2)
        ids = sb("ids", [128, 2, 1], U32)
        meta = sb("meta", [128, 2, 2])

        ps = ctx.enter_context(nc.psum_tensor("ps", [128, 8, 512], F32))
        psT, psX, psQ, psK, psV = (ps[:, n, :] for n in range(5))
        psE, psC, psL = ps[:, 5, :], ps[:, 6, :], ps[:, 7, :]

        s_x = [sem(f"x_loaded{q}") for q in range(4)]
        s_wc = sem("conv_weights_loaded")
        s_wa = sem("attention_weights_loaded")
        s_const = sem("constants_built")
        s_conv = sem("conv_products")
        s_cst = sem("conv_stats")
        s_fin = sem("conv_coefficients")
        s_ca = sem("conv_applied")
        s_sp = sem("softplus_steps")
        A = {k: sem(f"A_{k}") for k in STEPS_A}
        Bs = {k: sem(f"B_{k}") for k in STEPS_B}
        Cs = {k: sem(f"C_{k}") for k in STEPS_C}
        R = {k: sem(f"R_{k}") for k in STEPS_R}
        s_scat = sem("rows_dispatched")
        s_res = sem("residual_written")
        s_padw = sem("padding_written")
        s_cntp = sem("counts_summed")
        s_tab = sem("table_steps")
        s_w = [sem(f"expert_weights{p}") for p in range(2)]
        s_xr = [sem(f"rows_loaded{p}") for p in range(2)]
        s_meta = sem("row_ends_kept")
        s_eT = sem("rows_turned")
        s_eTc = sem("rows_turned_kept")
        s_h = sem("hidden_products")
        s_hb = sem("hidden_biased")
        s_ge = sem("hidden_activated")
        s_hT = sem("hidden_turned")
        s_hTc = sem("hidden_turned_kept")
        s_yp = sem("expert_products")
        s_y1 = sem("expert_biased")
        s_y = sem("expert_rows_ready")
        s_add = sem("rows_added")
        s_go = sem("adding_may_start")

        ps_chunk = lambda c, n=128: ps[0:n, c, 0:CW]
        block = ctx.enter_context(nc.Block())

        def step(stage, steps, engine, name, i, ins):
            ins.then_inc(stage[engine], 1)


        @block.sync
        def _(sp):
            for q in range(4):
                for k in range(2):
                    sp.dma_start(img[:, 4 * q:4 * q + 4, k * HW:(k + 1) * HW],
                                 x[4 * q:4 * q + 4, k * 128:(k + 1) * 128, :].rearrange("b p n -> p b n")
                                 ).then_inc(s_x[q], 16)
                if q == 0:
                    for m in range(2):
                        sp.dma_start(w1s[:, :, m * MID:(m + 1) * MID],
                                     w1t.rearrange("(k p) m -> p k m", p=128)).then_inc(s_wc, 16)
                        lo, hi = m * MID, (m + 1) * MID
                        for n, v in enumerate((b1, g1, be1)):
                            sp.dma_start(vecs[lo:hi, 0, n, 0:1], v.rearrange("(p a) -> p a", a=1)).then_inc(s_wc, 16)
                    for n, v in enumerate((b2, g2, be2)):
                        sp.dma_start(vecs[0:MID, 1, n, 0:1], v.rearrange("(p a) -> p a", a=1)).then_inc(s_wc, 16)
                    for n, v in enumerate((b3, g3, be3)):
                        for k in range(2):
                            sp.dma_start(vecs[:, 2, n, k:k + 1], v[k * 128:(k + 1) * 128].rearrange("(p a) -> p a", a=1)
                                         ).then_inc(s_wc, 16)
                    sp.dma_start(w2s[0:64, 0:3, :], w2t[0].rearrange("d i o -> i d o")).then_inc(s_wc, 16)
                    sp.dma_start(w2s[64:128, 0:3, :], w2t[1].rearrange("d i o -> i d o")).then_inc(s_wc, 16)
                    sp.dma_start(w2s[0:64, 3:6, :], w2t[2].rearrange("d i o -> i d o")).then_inc(s_wc, 16)
                    sp.dma_start(w3s[:, :], w3t).then_inc(s_wc, 16)
                    sp.dma_start(rs[:, 0:1], res_scale.rearrange("(a b) -> a b", a=1).to_broadcast([128, 1])).then_inc(s_wc, 16)
            sp.dma_start(wq[:, :, :], wqkv.rearrange("(k p) n -> p k n", p=128)).then_inc(s_wa, 16)
            sp.dma_start(wo[:, :, :], wout.rearrange("(k p) n -> p k n", p=128)).then_inc(s_wa, 16)
            sp.dma_start(gw[:, :, :], gate_w.rearrange("(k p) n -> p k n", p=128)).then_inc(s_wa, 16)
            for j in range(2):
                sp.dma_start(bo2[:, j, :], bout.rearrange("(a n) -> a n", a=1).to_broadcast([HALF, C])).then_inc(s_wa, 16)
            for j in range(4):
                sp.dma_start(gb[:, j, :], gate_b.rearrange("(a n) -> a n", a=1).to_broadcast([HALF, E])).then_inc(s_wa, 16)

            def load_expert(e):
                p = e % 2
                o = p * WSET
                sp.dma_start(wset[:, o:o + W2OFF].rearrange("p (k f) -> p k f", k=2),
                             ew1[e].rearrange("(k p) f -> p k f", p=128)).then_inc(s_w[p], 16)
                sp.dma_start(wset[:, o + W2OFF:o + B1OFF].rearrange("p (k d) -> p k d", k=8),
                             ew2[e].rearrange("(k p) d -> p k d", p=128)).then_inc(s_w[p], 16)
                sp.dma_start(wset[:, o + B1OFF:o + B2OFF], eb1[e:e + 1, :].to_broadcast([128, FF])).then_inc(s_w[p], 16)
                sp.dma_start(wset[:, o + B2OFF:o + WSET], eb2[e:e + 1, :].to_broadcast([128, C])).then_inc(s_w[p], 16)

            load_expert(0)
            load_expert(1)
            sp.wait_ge(s_const, NCONST)
            sp.dma_start(disp[E * CAP:E * CAP + 128, :], padrow[:, :]).then_inc(s_padw, 16)
            sp.dma_start(out[TOKENS:TOKENS + 128, :], padrow[:, 0:C]).then_inc(s_padw, 16)
            for i in range(B):
                sp.wait_ge(Bs["vec"], after(STEPS_B["vec"], "add", i))
                sp.dma_start(out[i * HW:(i + 1) * HW, :].rearrange("(j p) d -> p j d", p=HALF),
                             img[0:HALF, i, 0:2 * C].rearrange("p (j d) -> p j d", j=2)).then_inc(s_res, 16)
            sp.wait_ge(s_tab, TAB_STEPS)
            ends = [sp.value_load(tbi[0:1, 6, e - 2:e - 1], min_val=1, max_val=SLOTS) for e in range(2, E)]
            for e in range(2, E):
                sp.wait_ge(s_y1, ends[e - 2])
                load_expert(e)

        @block.gpsimd
        def _(pool):
            count = [0]

            def built(ins):
                ins.then_inc(s_const, 1)
                count[0] += 1
                pool.wait_ge(s_const, count[0])

            built(pool.memset(pad[:, :], 0.0))
            built(pool.memset(w2s[64:128, 3:6, :], 0.0))
            for t, v in ((ident, 0.0), (ones, 1.0), (upper, 1.0), (heads, 1.0), (padrow, 0.0)):
                built(pool.memset(t[:, :], v))
            built(pool.memset(run[:, :, :, :], 0.0))
            built(pool.memset(lt[:, :, :], 1.0))
            built(pool.iota(tokid_i[:, :], pattern=[[HALF, TILES]], base=0, channel_multiplier=1))
            built(pool.iota(iot[:, :], pattern=[[1, 64]], base=0, channel_multiplier=0))
            built(pool.affine_select(out=ident[:, :], in_=ident[:, :], compare_op=ALU.not_equal, fill=1.0,
                                     base=0, pattern=[[-1, 128]], channel_multiplier=1))
            built(pool.affine_select(out=upper[:, :], in_=upper[:, :], compare_op=ALU.is_gt, fill=0.0,
                                     base=0, pattern=[[1, HALF]], channel_multiplier=-1))
            hv = heads[:, :].rearrange("p (h d) -> p h d", d=DH)
            built(pool.affine_select(out=hv, in_=hv, compare_op=ALU.is_ge, fill=0.0,
                                     base=0, pattern=[[-DH, 8], [0, DH]], channel_multiplier=1))
            built(pool.affine_select(out=hv, in_=hv, compare_op=ALU.is_ge, fill=0.0,
                                     base=DH - 1, pattern=[[DH, 8], [0, DH]], channel_multiplier=-1))
            built(pool.affine_select(out=lt[:, :, :], in_=lt[:, :, :], compare_op=ALU.is_ge, fill=0.0,
                                     base=0, pattern=[[1, E], [-1, E]], channel_multiplier=0))
            built(pool.iota(cnti[:, 0, :], pattern=[[0, E]], base=TOKENS, channel_multiplier=1))
            built(pool.iota(cnti[:, 1, :], pattern=[[CAP, E]], base=0, channel_multiplier=1))
            built(pool.tensor_copy(padrow[:, C:C + 1], cnti[:, 0, 0:1]))
            for j in range(4):
                built(pool.tensor_copy(expert_id[:, j, :], iot[0:HALF, 0:E]))
            built(pool.tensor_copy(ntl[:, 2, :], cnti[:, 1, :]))
            for j in range(4):
                built(pool.tensor_scalar(expert_row[:, j, :], expert_id[:, j, :], float(CAP), None, ALU.mult))
            assert count[0] == NCONST

            def stage_a(i):
                pool.wait_ge(s_wa, 9 * 16)
                pool.wait_ge(A["vec"], after(STEPS_A["vec"], "norm1", i))
                t = img[0:HALF, i, 0:2 * C]
                pool.tensor_tensor(t, t, bo2[:, :, :].rearrange("p j d -> p (j d)"), ALU.add).then_inc(A["pool"], 1)

            def stage_b(i):
                p = i % 2
                pool.wait_ge(Bs["vec"], after(STEPS_B["vec"], "qrec", i))
                if i >= 2:
                    pool.wait_ge(Bs["pe"], after(STEPS_B["pe"], "ctx", i - 2))
                pool.tensor_tensor(qn[:, p, :].rearrange("p (g d) -> p g d", d=DH),
                                   qe[:, p, :].rearrange("p (g d) -> p g d", d=DH),
                                   qr[:, p, 2, :].unsqueeze(2).to_broadcast([HALF, 2 * HEADS, DH]),
                                   ALU.mult).then_inc(Bs["pool"], 1)

            sent = [0]

            def scatter(g):
                pool.wait_ge(R["vec"], after(STEPS_R["vec"], "slots", g))
                if g == 0:
                    pool.wait_ge(s_padw, 32)
                for t in range(4):
                    for k in range(2):
                        if sent[0]:
                            pool.wait_ge(s_scat, 16 * sent[0])
                        pool.indirect_dma_start(
                            disp, bass.IndirectOffsetOnAxis(slot[:, g % 2, k, t:t + 1], 0),
                            rows[:, (2 * g + t // 2) % 4, t % 2, :], None).then_inc(s_scat, 16)
                        sent[0] += 1

            for n in range(B + 2):
                if 1 <= n <= B:
                    stage_b(n - 1)
                if n < B:
                    stage_a(n)
                if n >= 4 and n % 2 == 0:
                    scatter((n - 4) // 2)
            scatter(B // 2 - 1)
            pool.wait_ge(s_tab, TAB_PAD)
            for e in range(E):
                pool.wait_ge(s_scat, 16 * sent[0])
                pool.indirect_dma_start(disp, bass.IndirectOffsetOnAxis(padi[:, e:e + 1], 0),
                                        padrow[:, :], None).then_inc(s_scat, 16)
                sent[0] += 1
            pool.wait_ge(s_res, 16 * B)

            def add_rows(i, p, first=False):
                pool.wait_ge(s_y, i + 1)
                if not first:
                    pool.wait_ge(s_add, i * 16)
                    pool.sem_inc(s_go, 1)
                pool.indirect_dma_start(out, bass.IndirectOffsetOnAxis(ids[:, p, :], 0), ys[:, p, :], None,
                                        compute_op=ALU.add).then_inc(s_add, 16)

            add_rows(0, 0, True)
            add_rows(1, 1)
            with pool.Fori(1, SLOTS // 2) as g:
                for p in range(2):
                    add_rows(2 * g + p, p)
            pool.wait_ge(s_add, 16 * SLOTS)

        @block.scalar
        def _(act):
            act.wait_ge(s_sp, 1)
            act.activation(rs[:, 2:3], rs[:, 1:2], ACT.Exp, scale=-1.0).then_inc(s_sp, 1)
            act.wait_ge(s_sp, 3)
            act.activation(rs[:, 4:5], rs[:, 3:4], ACT.Ln).then_inc(s_sp, 1)
            pv = pad[:, :].rearrange("p (b r c) -> p b r c", b=B, c=16)
            act.wait_ge(s_const, 1)
            act.wait_ge(s_fin, 1)
            for c in range(CHUNKS):
                src = ps_chunk(c).rearrange("p (b r c) -> p b r c", b=2, c=SIDE)
                for h in range(2):
                    q = slice(64 * h, 64 * h + 64)
                    dst = pv[q, 2 * c:2 * c + 2, 1 - h:15 - h, 1:15]
                    for b in range(2):
                        last = act.activation(dst[:, b], src[q, b], ACT.Relu, bias=coef[q, 0, 1, 0:1], scale=coef[q, 0, 0, 0:1])
                last.then_inc(s_ca, 1)
            act.wait_ge(s_fin, 2)
            for c in range(CHUNKS):
                act.activation(mid2[0:MID, c * CW:(c + 1) * CW], ps_chunk(c, MID), ACT.Relu,
                               bias=coef[0:MID, 1, 1, 0:1], scale=coef[0:MID, 1, 0, 0:1]).then_inc(s_ca, 1)
            for c in range(CHUNKS):
                for h in range(2):
                    act.wait_ge(s_conv, 2 * CHUNKS + 2 * c + h + 1)
                    act.copy(img[:, 2 * c:2 * c + 2, (2 + h) * HW:(3 + h) * HW],
                             ps_chunk((2 * c + h) % 8).rearrange("p (b n) -> p b n", b=2)).then_inc(s_ca, 1)

            def inv_sqrt(stage, steps, i, which):
                act.wait_ge(stage["vec"], after(steps["vec"], "eps", i))
                w = sm[:, which, i % 2]
                act.activation(w[:, 1, :], w[:, 0, :], ACT.Ln).then_inc(stage["act"], 1)
                act.wait_ge(stage["act"], after(steps["act"], "ln", i))
                act.activation(w[:, 2, :], w[:, 1, :], ACT.Exp, scale=-0.5).then_inc(stage["act"], 1)

            def a_relu(i):
                p = i % 2
                for k in range(2):
                    act.wait_ge(A["vec"], after(STEPS_A["vec"], f"mix{k}", i))
                    act.activation(tc[:, p, k, :], tc[:, p, k, :], ACT.Relu, bias=coef[:, 2, 1, k:k + 1]).then_inc(A["act"], 1)

            def a_keep(i):
                act.wait_ge(A["pe"], after(STEPS_A["pe"], "turn", i))
                act.copy(img[0:HALF, i, 0:2 * C], psT[0:HALF, :]).then_inc(A["act"], 1)

            def a_xT(i):
                act.wait_ge(A["pe"], after(STEPS_A["pe"], "xT", i))
                if i >= 2:
                    act.wait_ge(A["pe"], after(STEPS_A["pe"], "v", i - 2))
                act.copy(xT[:, i % 2, :, :].rearrange("p k n -> p (k n)"), psX[:, 0:CW]).then_inc(A["act"], 1)

            def b_exps(i):
                p = i % 2
                act.wait_ge(Bs["vec"], after(STEPS_B["vec"], "kneg", i))
                if i >= 2:
                    act.wait_ge(Bs["pe"], after(STEPS_B["pe"], "kT", i - 2))
                for h in range(2):
                    act.activation(ek[:, p, h, :], psK[:, h * HW:(h + 1) * HW], ACT.Exp, bias=kx[:, p, 1, h:h + 1],
                                   accum_out=kx[:, p, 2, h:h + 1]).then_inc(Bs["act"], 1)
                act.wait_ge(Bs["vec"], after(STEPS_B["vec"], "qsub", i))
                act.activation(qe[:, p, :], qe[:, p, :], ACT.Exp, scale=float(DH) ** -0.5).then_inc(Bs["act"], 1)

            def b_copies(i):
                p = i % 2
                act.wait_ge(A["pe"], after(STEPS_A["pe"], "v", i))
                if i >= 2:
                    act.wait_ge(Bs["pe"], after(STEPS_B["pe"], "out", i - 2))
                act.copy(vT[:, p, :, :].rearrange("p k n -> p (k n)"), psV[:, 0:CW]).then_inc(Bs["act"], 1)
                act.wait_ge(Bs["pe"], after(STEPS_B["pe"], "kT", i))
                act.copy(ekt[:, p, :, :].rearrange("p j d -> p (j d)"), psE[0:HALF, :]).then_inc(Bs["act"], 1)

            def b_proj(i):
                act.wait_ge(Bs["pe"], after(STEPS_B["pe"], "proj", i))
                act.copy(pr[:, i % 2, :, :].rearrange("p k d -> p (k d)"), psE[:, :]).then_inc(Bs["act"], 1)

            def c_xT(i):
                act.wait_ge(Cs["pe"], after(STEPS_C["pe"], "xT", i))
                act.copy(xT2[:, i % 2, :, :].rearrange("p k n -> p (k n)"), psL[:, 0:CW]).then_inc(Cs["act"], 1)

            def r_exp(g):
                act.wait_ge(R["vec"], after(STEPS_R["vec"], "sub", g))
                act.activation(rt[:, 0], rt[:, 0], ACT.Exp).then_inc(R["act"], 1)

            for n in range(B + 2):
                a, b, c = n, n - 1, n - 2
                if a < B:
                    a_relu(a)
                if 0 <= b < B:
                    b_exps(b)
                if a < B:
                    a_keep(a)
                if 0 <= b < B:
                    b_copies(b)
                if c >= 0:
                    inv_sqrt(Cs, STEPS_C, c, 1)
                if a < B:
                    inv_sqrt(A, STEPS_A, a, 0)
                if c >= 0:
                    c_xT(c)
                if a < B:
                    a_xT(a)
                if 0 <= b < B:
                    b_proj(b)
                if c >= 0 and c % 2:
                    r_exp(c // 2)

            act.wait_ge(s_tab, TAB_STEPS)
            act.wait_ge(s_scat, 16 * (4 * B + E))

            def load_rows(i, p, row):
                act.dma_start(xr[:, p, :], disp[bass.ds(row, 128), :]).then_inc(s_xr[p], 16)

            def turned(i, p):
                act.wait_ge(s_eT, i + 1)
                act.copy(xrT[:, p, :], ps[:, 0, 0:C]).then_inc(s_eTc, 1)

            def gelu(i, p):
                for h in range(2):
                    act.wait_ge(s_hb, 2 * i + h + 1)
                    act.activation(hb[:, p, h * 512:(h + 1) * 512], hb[:, p, h * 512:(h + 1) * 512],
                                   ACT.Gelu).then_inc(s_ge, 1)

            def turned_hidden(i, p):
                act.wait_ge(s_hT, 2 * i + 1)
                act.copy(hT[:, p, 0:512], ps[:, 3, :]).then_inc(s_hTc, 1)

            def act_slot(m, p):
                if not isinstance(m, int) or m + 1 < SLOTS:
                    row = act.value_load(tbi[0:1, 1, bass.ds(m + 1, 1)], min_val=0, max_val=E * CAP)
                    if not isinstance(m, int) or m >= 1:
                        act.wait_ge(s_meta, m)
                        act.wait_ge(s_eT, m)
                    load_rows(m + 1, 1 - p, row)
                if not isinstance(m, int) or 0 <= m - 2 < SLOTS:
                    turned_hidden(m - 2, p)
                if not isinstance(m, int) or 0 <= m - 1 < SLOTS:
                    gelu(m - 1, 1 - p)
                if not isinstance(m, int) or m < SLOTS:
                    turned(m, p)

            load_rows(0, 0, act.value_load(tbi[0:1, 1, 0:1], min_val=0, max_val=E * CAP))
            act_slot(0, 0)
            act_slot(1, 1)
            act_slot(2, 0)
            act_slot(3, 1)
            with act.Fori(2, SLOTS // 2 - 1) as g:
                for p in range(2):
                    act_slot(2 * g + p, p)
            act_slot(SLOTS - 2, 0)
            act_slot(SLOTS - 1, 1)
            act_slot(SLOTS, 0)
            act_slot(SLOTS + 1, 1)

        @block.tensor
        def _(pe):
            pe.wait_ge(s_wc, 16 * NCW)
            for c in range(CHUNKS):
                if c % 2 == 0:
                    pe.wait_ge(s_x[c // 2], 32)
                for k in range(2):
                    last = pe.matmul(ps_chunk(c), w1s[:, k, :], img[:, 2 * c:2 * c + 2, k * HW:(k + 1) * HW],
                                     start=(k == 0), stop=(k == 1))
                last.then_inc(s_conv, 1)
            pv = pad[:, :].rearrange("p (b r c) -> p b r c", b=B, c=16)
            pe.wait_ge(s_const, 2)
            for c in range(CHUNKS):
                pe.wait_ge(s_ca, c + 1)
                for t in range(6):
                    r, d = (0, t) if t < 3 else (2, t - 3)
                    for b in range(2):
                        last = pe.matmul(ps[0:MID, c, b * HW:(b + 1) * HW], w2s[:, t, :],
                                         pv[:, 2 * c + b, r:r + SIDE, d:d + SIDE],
                                         start=(t == 0 and b == 0), stop=(t == 5), skip_group_check=True)
                last.then_inc(s_conv, 1)
            for c in range(CHUNKS):
                for h in range(2):
                    n = 2 * c + h
                    pe.wait_ge(s_ca, CHUNKS + n + 1 if n < 8 else 2 * CHUNKS + n - 7)
                    pe.matmul(ps_chunk(n % 8), w3s[:, h * 128:(h + 1) * 128], mid2[0:MID, c * CW:(c + 1) * CW],
                              start=True, stop=True).then_inc(s_conv, 1)
            pe.wait_ge(s_wa, 9 * 16)
            pe.wait_ge(s_const, NCONST)
            pe.wait_ge(s_ca, 4 * CHUNKS)

            def a_turn(i):
                p = i % 2
                pe.wait_ge(A["act"], after(STEPS_A["act"], "relu1", i))
                if i >= 1:
                    pe.wait_ge(A["act"], after(STEPS_A["act"], "keep", i - 1))
                for j in range(2):
                    for k in range(2):
                        last = pe.transpose(psT[0:HALF, j * C + k * 128:j * C + (k + 1) * 128],
                                            tc[:, p, k, j * HALF:(j + 1) * HALF], ident[:, :])
                last.then_inc(A["pe"], 1)

            def a_xT(i):
                p = i % 2
                pe.wait_ge(A["vec"], after(STEPS_A["vec"], "norm1", i))
                if i >= 1:
                    pe.wait_ge(A["act"], after(STEPS_A["act"], "xT", i - 1))
                for k in range(2):
                    for j in range(2):
                        last = pe.transpose(psX[:, k * HW + j * HALF:k * HW + (j + 1) * HALF],
                                            xh[:, p, j, k * 128:(k + 1) * 128], ident[0:HALF, 0:HALF])
                last.then_inc(A["pe"], 1)

            def a_qkv(i):
                p = i % 2
                pe.wait_ge(A["act"], after(STEPS_A["act"], "xT", i))
                if i >= 1:
                    pe.wait_ge(Bs["vec"], after(STEPS_B["vec"], "qsub", i - 1))
                for j in range(2):
                    for k in range(2):
                        last = pe.matmul(psQ[0:HALF, j * C:(j + 1) * C], xT[:, p, k, j * HALF:(j + 1) * HALF],
                                         wq[:, k, 0:C], start=(k == 0), stop=(k == 1))
                last.then_inc(A["pe"], 1)
                for what, dst, off, free in (("k", psK, C, "kexp1"), ("v", psV, 2 * C, "v")):
                    if i >= 1:
                        pe.wait_ge(Bs["act"], after(STEPS_B["act"], free, i - 1))
                    for h in range(2):
                        for k in range(2):
                            last = pe.matmul(dst[:, h * HW:(h + 1) * HW], wq[:, k, off + h * 128:off + (h + 1) * 128],
                                             xT[:, p, k, :], start=(k == 0), stop=(k == 1))
                    last.then_inc(A["pe"], 1)

            def b_kT(i):
                p = i % 2
                pe.wait_ge(Bs["act"], after(STEPS_B["act"], "kexp1", i))
                if i >= 1:
                    pe.wait_ge(Bs["act"], after(STEPS_B["act"], "proj", i - 1))
                for j in range(2):
                    for h in range(2):
                        last = pe.transpose(psE[0:HALF, j * C + h * 128:j * C + (h + 1) * 128],
                                            ek[:, p, h, j * HALF:(j + 1) * HALF], ident[:, :])
                last.then_inc(Bs["pe"], 1)

            def b_ctx(i):
                p = i % 2
                pe.wait_ge(Bs["act"], after(STEPS_B["act"], "kT", i))
                pe.wait_ge(Bs["pool"], after(STEPS_B["pool"], "q", i))
                if i >= 1:
                    pe.wait_ge(Bs["vec"], after(STEPS_B["vec"], "add", i - 1))
                for h in range(2):
                    for j in range(2):
                        last = pe.matmul(psC[:, h * 128:(h + 1) * 128], ekt[:, p, j, h * 128:(h + 1) * 128],
                                         qn[:, p, j * C + h * 128:j * C + (h + 1) * 128], start=(j == 0), stop=(j == 1))
                last.then_inc(Bs["pe"], 1)

            def b_proj(i):
                p = i % 2
                pe.wait_ge(Bs["vec"], after(STEPS_B["vec"], "ctx1", i))
                for h in range(2):
                    last = pe.matmul(psE[:, h * C:(h + 1) * C], cT[:, p, h, :], wo[:, h, :], start=True, stop=True)
                last.then_inc(Bs["pe"], 1)

            def b_out(i):
                p = i % 2
                pe.wait_ge(Bs["act"], after(STEPS_B["act"], "proj", i))
                for j in range(2):
                    for h in range(2):
                        last = pe.matmul(psC[0:HALF, j * C:(j + 1) * C], vT[:, p, h, j * HALF:(j + 1) * HALF],
                                         pr[:, p, h, :], start=(h == 0), stop=(h == 1))
                last.then_inc(Bs["pe"], 1)

            def c_xT(i):
                pe.wait_ge(Cs["vec"], after(STEPS_C["vec"], "norm1", i))
                if i >= 2 and i % 2 == 0:
                    pe.wait_ge(R["vec"], after(STEPS_R["vec"], "pos", i // 2 - 1))
                if i % 2:
                    pe.wait_ge(Cs["act"], after(STEPS_C["act"], "xT", i - 1))
                for k in range(2):
                    for j in range(2):
                        last = pe.transpose(psL[:, k * HW + j * HALF:k * HW + (j + 1) * HALF],
                                            rows[:, i % 4, j, k * 128:(k + 1) * 128], ident[0:HALF, 0:HALF])
                last.then_inc(Cs["pe"], 1)

            def c_logits(i):
                pe.wait_ge(Cs["act"], after(STEPS_C["act"], "xT", i))
                for j in range(2):
                    at = CW + ((i % 2) * 2 + j) * E
                    for k in range(2):
                        last = pe.matmul(psL[0:HALF, at:at + E], xT2[:, i % 2, k, j * HALF:(j + 1) * HALF],
                                         gw[:, k, :], start=(k == 0), stop=(k == 1))
                last.then_inc(Cs["pe"], 1)

            def r_rank(g):
                pe.wait_ge(R["vec"], after(STEPS_R["vec"], "run3", g))
                pe.matmul(psL[0:HALF, CW + 32:CW + 64], upper[:, :], rt[:, 4].rearrange("p t e -> p (t e)"),
                          start=True, stop=False)
                pe.matmul(psL[0:HALF, CW + 32:CW + 64], ones[:, 0:HALF],
                          run[:, g % 2, 0:4, :].rearrange("p t e -> p (t e)"), start=False, stop=True).then_inc(R["pe"], 1)

            for n in range(B + 2):
                a, b, c = n, n - 1, n - 2
                if a < B:
                    a_turn(a)
                if 0 <= b < B:
                    b_kT(b)
                if c >= 0:
                    c_xT(c)
                if a < B:
                    a_xT(a)
                if 0 <= b < B:
                    b_ctx(b)
                if c >= 0:
                    c_logits(c)
                if 0 <= b < B:
                    b_proj(b)
                if a < B:
                    a_qkv(a)
                if 0 <= b < B:
                    b_out(b)
                if c >= 0 and c % 2:
                    r_rank(c // 2)
            pe.wait_ge(R["vec"], after(STEPS_R["vec"], "slots", B // 2 - 1))
            pe.matmul(ps[:, 0, 0:E], ones[:, :], run[:, (B // 2) % 2, 0, :], start=True, stop=True).then_inc(s_cntp, 1)

            def x_turn(i, p, late):
                pe.wait_ge(s_xr[p], (i // 2 + 1) * 16 if isinstance(i, int) else late)
                if not isinstance(i, int) or i >= 1:
                    pe.wait_ge(s_eTc, i)
                for k in range(2):
                    last = pe.transpose(ps[:, 0, k * 128:(k + 1) * 128], xr[:, p, k * 128:(k + 1) * 128], ident[:, :])
                last.then_inc(s_eT, 1)

            def hidden(i, p):
                off = pe.value_load(tbi[0:1, 2, bass.ds(i, 1)], min_val=0, max_val=WSET)
                need = [pe.value_load(tbi[0:1, 3 + q, bass.ds(i, 1)], min_val=64, max_val=64 * E) for q in range(2)]
                pe.wait_ge(s_eTc, i + 1)
                for q in range(2):
                    pe.wait_ge(s_w[q], need[q])
                for h in range(2):
                    if not isinstance(i, int) or i >= 1:
                        pe.wait_ge(s_hb, 2 * i - 1 + h)
                    for k in range(2):
                        last = pe.matmul(ps[:, 1 + h, :], xrT[:, p, k * 128:(k + 1) * 128],
                                         wset[:, bass.ds(off + k * FF + h * 512, 512)], start=(k == 0), stop=(k == 1))
                    last.then_inc(s_h, 1)

            def h_turn(i, p):
                for h in range(2):
                    pe.wait_ge(s_ge, 2 * i + h + 1)
                    if not isinstance(i, int) or i >= 1:
                        pe.wait_ge(s_hTc, 2 * i - 1 + h)
                    for k in range(4):
                        last = pe.transpose(ps[:, 3 + h, k * 128:(k + 1) * 128],
                                            hb[:, p, h * 512 + k * 128:h * 512 + (k + 1) * 128], ident[:, :])
                    last.then_inc(s_hT, 1)

            def expert_out(i, p):
                off = pe.value_load(tbi[0:1, 2, bass.ds(i, 1)], min_val=0, max_val=WSET)
                pe.wait_ge(s_hTc, 2 * i + 2)
                if not isinstance(i, int) or i >= 1:
                    pe.wait_ge(s_y1, i)
                for k in range(8):
                    last = pe.matmul(ps[:, 5, 0:C], hT[:, p, k * 128:(k + 1) * 128],
                                     wset[:, bass.ds(off + W2OFF + k * C, C)], start=(k == 0), stop=(k == 7))
                last.then_inc(s_yp, 1)

            pe.wait_ge(s_tab, TAB_STEPS)

            def pe_slot(m, p, late=None):
                st = isinstance(m, int)
                if not st or 0 <= m - 2 < SLOTS:
                    h_turn(m - 2, p)
                if not st or 0 <= m - 1 < SLOTS:
                    hidden(m - 1, 1 - p)
                if not st or m < SLOTS:
                    x_turn(m, p, late)
                if not st or 0 <= m - 2 < SLOTS:
                    expert_out(m - 2, p)

            for m in range(4):
                pe_slot(m, m % 2)
            with pe.Fori(2, SLOTS // 2) as g:
                for p in range(2):
                    pe_slot(2 * g + p, p, g * 16 + 16)
            pe_slot(SLOTS, 0)
            pe_slot(SLOTS + 1, 1)

        @block.vector
        def _(dve):
            V, I = nc.vector, s_sp
            dve.wait_ge(s_wc, 16 * NCW)
            V.scalar_tensor_tensor(out=rs[:, 1:2], in0=rs[:, 0:1], scalar=-1.0, in1=rs[:, 0:1], op0=ALU.mult,
                                   op1=ALU.max).then_inc(s_sp, 1)
            dve.wait_ge(s_sp, 2)
            V.tensor_scalar(rs[:, 3:4], rs[:, 2:3], 1.0, None, ALU.add).then_inc(s_sp, 1)
            dve.wait_ge(s_sp, 4)
            V.scalar_tensor_tensor(out=rs[:, 5:6], in0=rs[:, 0:1], scalar=0.0, in1=rs[:, 4:5], op0=ALU.max,
                                   op1=ALU.add).then_inc(s_sp, 1)
            done = [0]

            def chain(ins):
                ins.then_inc(s_cst, 1)
                done[0] += 1
                dve.wait_ge(s_cst, done[0])

            def coefficients(m, parts, halves, mult=None):
                P = slice(0, parts)
                for h in range(halves):
                    chain(V.bn_aggr(bmv[P, h, :], bst[P, h, :, :].rearrange("p c s -> p (c s)")))
                H = slice(0, halves)
                mean, var = bmv[P, H, 0], bmv[P, H, 1]
                chain(V.tensor_scalar(bn[P, 0, H], var, BN_EPS, None, ALU.add))
                chain(V.tensor_scalar(bn[P, 1, H].bitcast(I32), bn[P, 0, H].bitcast(I32), 1, None, ALU.logical_shift_right))
                chain(V.tensor_scalar(bn[P, 1, H].bitcast(I32), bn[P, 1, H].bitcast(I32), -1, None, ALU.bitwise_xor))
                chain(V.tensor_scalar(bn[P, 1, H].bitcast(I32), bn[P, 1, H].bitcast(I32), MAGIC, None, ALU.add))
                for _ in range(4):
                    chain(V.tensor_tensor(bn[P, 2, H], bn[P, 1, H], bn[P, 1, H], ALU.mult))
                    chain(V.tensor_tensor(bn[P, 2, H], bn[P, 2, H], bn[P, 0, H], ALU.mult))
                    chain(V.tensor_scalar(bn[P, 2, H], bn[P, 2, H], -0.5, 1.5, ALU.mult, ALU.add))
                    chain(V.tensor_tensor(bn[P, 1, H], bn[P, 1, H], bn[P, 2, H], ALU.mult))
                chain(V.tensor_tensor(coef[P, m, 0, H], bn[P, 1, H], vecs[P, m, 1, H], ALU.mult))
                chain(V.tensor_tensor(bn[P, 3, H], mean, vecs[P, m, 0, H], ALU.add))
                chain(V.tensor_tensor(bn[P, 4, H], vecs[P, m, 0, H], bn[P, 3, H], ALU.subtract))
                chain(V.tensor_tensor(bn[P, 4, H], bn[P, 4, H], coef[P, m, 0, H], ALU.mult))
                chain(V.tensor_tensor(coef[P, m, 1, H], bn[P, 4, H], vecs[P, m, 2, H], ALU.add))
                if mult is not None:
                    chain(V.tensor_scalar(coef[P, m, 0, H], coef[P, m, 0, H], mult, None, ALU.mult))
                    chain(V.tensor_scalar(coef[P, m, 1, H], coef[P, m, 1, H], mult, None, ALU.mult))
                V.tensor_copy(bn[P, 5, H], coef[P, m, 0, H]).then_inc(s_fin, 1)

            for c in range(CHUNKS):
                dve.wait_ge(s_conv, c + 1)
                chain(V.bn_stats(bst[:, 0, c, :], ps_chunk(c)))
            coefficients(0, 128, 1)
            for c in range(CHUNKS):
                dve.wait_ge(s_conv, CHUNKS + c + 1)
                chain(V.bn_stats(bst[0:MID, 0, c, :], ps_chunk(c, MID)))
            coefficients(1, MID, 1)
            for c in range(CHUNKS):
                for h in range(2):
                    dve.wait_ge(s_ca, 2 * CHUNKS + 2 * c + h + 1)
                    chain(V.bn_stats(bst[:, h, c, :], img[:, 2 * c:2 * c + 2, (2 + h) * HW:(3 + h) * HW]))
            dve.wait_ge(s_sp, 5)
            coefficients(2, 128, 2, rs[:, 5:6])
            dve.wait_ge(s_const, NCONST)

            def mix(i):
                p = i % 2
                for k in range(2):
                    if i >= 2:
                        dve.wait_ge(A["pe"], after(STEPS_A["pe"], "turn", i - 2))
                    V.scalar_tensor_tensor(out=tc[:, p, k, :], in0=img[:, i, (2 + k) * HW:(3 + k) * HW],
                                           scalar=coef[:, 2, 0, k:k + 1], in1=img[:, i, k * HW:(k + 1) * HW],
                                           op0=ALU.mult, op1=ALU.add).then_inc(A["vec"], 1)

            def stats(stage, steps, i, which):
                p = i % 2
                S = steps["vec"]
                for j in range(2):
                    V.bn_stats(stt[:, which, p, j, :], img[0:HALF, i, j * C:(j + 1) * C]).then_inc(stage["vec"], 1)
                for j in range(2):
                    dve.wait_ge(stage["vec"], after(S, f"stat{j}", i))
                    V.bn_aggr(mv[:, which, p, j, :], stt[:, which, p, j, :]).then_inc(stage["vec"], 1)
                dve.wait_ge(stage["vec"], after(S, "agg1", i))
                V.tensor_scalar(sm[:, which, p, 0, :], mv[:, which, p, :, 1], LN_EPS, None, ALU.add).then_inc(stage["vec"], 1)

            def normalise(stage, steps, i, which, out):
                p = i % 2
                S = steps["vec"]
                w = sm[:, which, p]
                dve.wait_ge(stage["act"], after(steps["act"], "exp", i))
                V.tensor_tensor(w[:, 3, :], w[:, 2, :], w[:, 2, :], ALU.mult).then_inc(stage["vec"], 1)
                dve.wait_ge(stage["vec"], after(S, "nr0", i))
                V.tensor_tensor(w[:, 3, :], w[:, 3, :], w[:, 0, :], ALU.mult).then_inc(stage["vec"], 1)
                dve.wait_ge(stage["vec"], after(S, "nr1", i))
                V.tensor_scalar(w[:, 3, :], w[:, 3, :], -0.5, 1.5, ALU.mult, ALU.add).then_inc(stage["vec"], 1)
                dve.wait_ge(stage["vec"], after(S, "nr2", i))
                V.tensor_tensor(w[:, 4, :], w[:, 3, :], w[:, 2, :], ALU.mult).then_inc(stage["vec"], 1)
                dve.wait_ge(stage["vec"], after(S, "nr3", i))
                for j in range(2):
                    V.tensor_scalar(out[j], img[0:HALF, i, j * C:(j + 1) * C], mv[:, which, p, j, 0:1],
                                    w[:, 4, j:j + 1], ALU.subtract, ALU.mult).then_inc(stage["vec"], 1)

            def a_stats(i):
                dve.wait_ge(A["act"], after(STEPS_A["act"], "keep", i))
                stats(A, STEPS_A, i, 0)

            def a_norm(i):
                if i >= 2:
                    dve.wait_ge(A["pe"], after(STEPS_A["pe"], "xT", i - 2))
                normalise(A, STEPS_A, i, 0, [xh[:, i % 2, j, :] for j in range(2)])

            def b_maxes(i):
                p = i % 2
                S = STEPS_B["vec"]
                dve.wait_ge(A["pe"], after(STEPS_A["pe"], "k", i))
                V.tensor_reduce(kx[:, p, 0, :], psK[:, 0:CW].rearrange("p (h n) -> p h n", h=2), X, ALU.max).then_inc(Bs["vec"], 1)
                dve.wait_ge(Bs["vec"], after(S, "kmax", i))
                V.tensor_scalar(kx[:, p, 1, :], kx[:, p, 0, :], -1.0, None, ALU.mult).then_inc(Bs["vec"], 1)
                q = psQ[0:HALF, :].rearrange("p (g d) -> p g d", d=DH)
                V.tensor_reduce(qr[:, p, 0, :], q, X, ALU.max).then_inc(Bs["vec"], 1)
                dve.wait_ge(Bs["vec"], after(S, "qmax", i))
                if i >= 2:
                    dve.wait_ge(Bs["pool"], after(STEPS_B["pool"], "q", i - 2))
                V.tensor_tensor(qe[:, p, :].rearrange("p (g d) -> p g d", d=DH), q,
                                qr[:, p, 0, :].unsqueeze(2).to_broadcast([HALF, 2 * HEADS, DH]),
                                ALU.subtract).then_inc(Bs["vec"], 1)

            def b_sums(i):
                p = i % 2
                S = STEPS_B["vec"]
                dve.wait_ge(Bs["act"], after(STEPS_B["act"], "qexp", i))
                V.tensor_reduce(qr[:, p, 1, :], qe[:, p, :].rearrange("p (g d) -> p g d", d=DH), X, ALU.add).then_inc(Bs["vec"], 1)
                dve.wait_ge(Bs["vec"], after(S, "qsum", i))
                V.reciprocal(qr[:, p, 2, :], qr[:, p, 1, :]).then_inc(Bs["vec"], 1)
                V.reciprocal(kx[:, p, 3, :], kx[:, p, 2, :]).then_inc(Bs["vec"], 1)

            def b_ctx(i):
                p = i % 2
                dve.wait_ge(Bs["vec"], after(STEPS_B["vec"], "krec", i))
                dve.wait_ge(Bs["pe"], after(STEPS_B["pe"], "ctx", i))
                for h in range(2):
                    V.scalar_tensor_tensor(out=cT[:, p, h, :], in0=psC[:, h * 128:(h + 1) * 128],
                                           scalar=kx[:, p, 3, h:h + 1], in1=heads[:, :],
                                           op0=ALU.mult, op1=ALU.mult).then_inc(Bs["vec"], 1)

            def b_add(i):
                dve.wait_ge(Bs["pe"], after(STEPS_B["pe"], "out", i))
                dve.wait_ge(A["pool"], after(STEPS_A["pool"], "bias", i))
                V.tensor_tensor(img[0:HALF, i, 0:2 * C], psC[0:HALF, :], img[0:HALF, i, 0:2 * C],
                                ALU.add).then_inc(Bs["vec"], 1)

            def c_stats(i):
                dve.wait_ge(Bs["vec"], after(STEPS_B["vec"], "add", i))
                stats(Cs, STEPS_C, i, 1)

            def c_norm(i):
                if i >= 4:
                    dve.wait_ge(s_scat, 16 * 8 * (i // 2 - 1))
                normalise(Cs, STEPS_C, i, 1, [rows[:, i % 4, j, 0:C] for j in range(2)])

            def route(g):
                S = STEPS_R["vec"]
                L = rt[:, 0]
                n = [g * len(S)]

                def to(ins, wait=True):
                    ins.then_inc(R["vec"], 1)
                    n[0] += 1
                    if wait:
                        dve.wait_ge(R["vec"], n[0])

                bc = lambda v, k=E: v.unsqueeze(2).to_broadcast([HALF, 4, k])
                v = rv[:, g % 2]
                dve.wait_ge(Cs["pe"], after(STEPS_C["pe"], "logits", 2 * g + 1))
                to(V.tensor_tensor(L, psL[0:HALF, CW:CW + 32].rearrange("p (t e) -> p t e", e=E), gb[:, :, :], ALU.add))
                to(V.tensor_reduce(v[:, 0, :], L, X, ALU.max))
                to(V.tensor_tensor(L, L, bc(v[:, 0, :]), ALU.subtract))
                dve.wait_ge(R["act"], after(STEPS_R["act"], "exp", g))
                to(V.tensor_reduce(v[:, 1, :], L, X, ALU.add))
                to(V.reciprocal(v[:, 2, :], v[:, 1, :]))
                to(V.tensor_tensor(L, L, bc(v[:, 2, :]), ALU.mult))
                for t in range(4):
                    to(V.max(top[:, t, :], L[:, t, :]), t == 3)
                for t in range(4):
                    to(V.max_index(topi[:, t, :], top[:, t, :], L[:, t, :]), t == 3)
                to(V.tensor_copy(topf[:, :, :], topi[:, :, 0:2]))
                one1, one2, both, comb = rt[:, 2], rt[:, 3], rt[:, 4], rt[:, 5]
                to(V.tensor_tensor(one1, expert_id[:, :, :], bc(topf[:, :, 0]), ALU.is_equal), False)
                to(V.tensor_tensor(one2, expert_id[:, :, :], bc(topf[:, :, 1]), ALU.is_equal))
                if g >= 1:
                    dve.wait_ge(R["pe"], after(STEPS_R["pe"], "rank", g - 1))
                to(V.tensor_tensor(both, one1, one2, ALU.add))
                to(V.scalar_tensor_tensor(out=v[:, 3, :], in0=top[:, :, 0], scalar=1e-9, in1=top[:, :, 1],
                                          op0=ALU.add, op1=ALU.add))
                to(V.reciprocal(v[:, 4, :], v[:, 3, :]))
                to(V.tensor_tensor(comb, L, both, ALU.mult))
                if g >= 2:
                    dve.wait_ge(s_scat, 16 * 8 * (g - 1))
                rw = rows[:, (2 * g) % 4:(2 * g) % 4 + 2, :, :].rearrange("p i j r -> p (i j) r")
                to(V.tensor_tensor(rw[:, :, C + 1:ROW], comb, bc(v[:, 4, :]), ALU.mult), False)
                for t in range(4):
                    dst = run[:, g % 2, t + 1, :] if t < 3 else run[:, (g + 1) % 2, 0, :]
                    to(V.tensor_tensor(dst, run[:, g % 2, t, :], both[:, t, :], ALU.add))
                dve.wait_ge(R["pe"], after(STEPS_R["pe"], "rank", g))
                pos = rt[:, 6]
                to(V.tensor_tensor(pos, psL[0:HALF, CW + 32:CW + 64].rearrange("p (t e) -> p t e", e=E),
                                   expert_row[:, :, :], ALU.add))
                for k, one in enumerate((one1, one2)):
                    to(V.tensor_tensor(rt[:, 7 + k], pos, one, ALU.mult))
                    to(V.tensor_reduce(v[:, 5 + k, :], rt[:, 7 + k], X, ALU.add), k == 1)
                to(V.tensor_copy(slot[:, g % 2, :, :], v[:, 5:7, :]), False)

            for n in range(B + 2):
                a, b, c = n, n - 1, n - 2
                if a < B:
                    mix(a)
                if 0 <= b < B:
                    b_maxes(b)
                if c >= 0:
                    c_stats(c)
                if a < B:
                    a_stats(a)
                if 0 <= b < B:
                    b_sums(b)
                if c >= 0:
                    c_norm(c)
                    V.tensor_copy(rows[:, c % 4, :, C], tokid_i[:, 2 * c:2 * c + 2])
                if a < B:
                    a_norm(a)
                if 0 <= b < B:
                    b_ctx(b)
                    b_add(b)
                if c >= 0 and c % 2:
                    route(c // 2)

            tab = [0]

            def link(ins):
                ins.then_inc(s_tab, 1)
                tab[0] += 1
                dve.wait_ge(s_tab, tab[0])

            dve.wait_ge(s_cntp, 1)
            link(V.tensor_copy(cnt[:, :], ps[:, 0, 0:E]))
            link(V.tensor_tensor(padi[:, :], cnt[:, :], ntl[:, 2, :], ALU.add))
            assert tab[0] == TAB_PAD
            link(V.tensor_scalar(cnti[:, 0, :], cnt[:, :], 127.0, None, ALU.add))
            link(V.tensor_scalar(cnti[:, 0, :], cnti[:, 0, :], 7, None, ALU.logical_shift_right))
            link(V.tensor_scalar(ntl[:, 0, :], cnti[:, 0, :], 1.0, None, ALU.max))
            lo = lambda t: t[0:1]
            link(V.tensor_tensor(big[:, 0, 0:E, :], lt[:, :, :], ntl[0:1, 0, :].unsqueeze(1).to_broadcast([1, E, E]), ALU.mult))
            link(V.tensor_reduce(ntl[0:1, 1, :], big[:, 0, 0:E, :], X, ALU.add))
            link(V.tensor_copy(tbi[:, 6, 0:E], ntl[0:1, 1, :]))
            link(V.tensor_copy(tb[:, 0, :], iot[0:1, :]))
            link(V.tensor_tensor(big[:, 0], tb[:, 0, :].unsqueeze(2).to_broadcast([1, 64, E]),
                                 ntl[0:1, 1, :].unsqueeze(1).to_broadcast([1, 64, E]), ALU.is_ge))
            link(V.tensor_reduce(tb[:, 1, :], big[:, 0], X, ALU.add))
            link(V.tensor_tensor(big[:, 1], big[:, 0], ntl[0:1, 0, :].unsqueeze(1).to_broadcast([1, 64, E]), ALU.mult))
            link(V.tensor_reduce(tb[:, 2, :], big[:, 1], X, ALU.add))
            link(V.tensor_tensor(tb[:, 3, :], tb[:, 0, :], tb[:, 2, :], ALU.subtract))
            link(V.tensor_scalar(tb[:, 3, :], tb[:, 3, :], 128.0, None, ALU.mult))
            link(V.scalar_tensor_tensor(out=tb[:, 3, :], in0=tb[:, 1, :], scalar=float(CAP), in1=tb[:, 3, :],
                                        op0=ALU.mult, op1=ALU.add))
            link(V.tensor_scalar(tbi[:, 1, :], tb[:, 3, :], float(E * CAP), None, ALU.min))
            link(V.tensor_scalar(tbi[:, 0, :], tb[:, 1, :], float(E - 1), None, ALU.min))
            link(V.tensor_scalar(tbi[:, 5, :], tbi[:, 0, :], 1, None, ALU.bitwise_and))
            link(V.tensor_scalar(tbi[:, 2, :], tbi[:, 5, :], float(WSET), None, ALU.mult))
            link(V.tensor_scalar(tbi[:, 7, :], tbi[:, 0, :], 1, None, ALU.logical_shift_right))
            link(V.tensor_scalar(tbi[:, 3, :], tbi[:, 7, :], 64.0, 64.0, ALU.mult, ALU.add))
            link(V.tensor_tensor(tb[:, 4, :], tbi[:, 7, :], tbi[:, 5, :], ALU.add))
            link(V.tensor_scalar(tbi[:, 4, :], tb[:, 4, :], 1.0, 64.0, ALU.max, ALU.mult))
            assert tab[0] == TAB_STEPS, tab[0]

            def turned_hidden(i, p):
                dve.wait_ge(s_hT, 2 * i + 2)
                dve.wait_ge(s_hTc, 2 * i + 1)
                V.tensor_copy(hT[:, p, 512:1024], ps[:, 4, :]).then_inc(s_hTc, 1)

            def bias_hidden(i, p):
                off = dve.value_load(tbi[0:1, 2, bass.ds(i, 1)], min_val=0, max_val=WSET)
                need = [dve.value_load(tbi[0:1, 3 + q, bass.ds(i, 1)], min_val=64, max_val=64 * E) for q in range(2)]
                for q in range(2):
                    dve.wait_ge(s_w[q], need[q])
                for h in range(2):
                    dve.wait_ge(s_h, 2 * i + h + 1)
                    V.tensor_tensor(hb[:, p, h * 512:(h + 1) * 512], ps[:, 1 + h, :],
                                    wset[:, bass.ds(off + B1OFF + h * 512, 512)], ALU.add).then_inc(s_hb, 1)

            def finish(i, p):
                off = dve.value_load(tbi[0:1, 2, bass.ds(i, 1)], min_val=0, max_val=WSET)
                dve.wait_ge(s_yp, i + 1)
                V.tensor_tensor(yb[:, p, :], ps[:, 5, 0:C], wset[:, bass.ds(off + B2OFF, C)], ALU.add).then_inc(s_y1, 1)
                if not isinstance(i, int) or i >= 2:
                    dve.wait_ge(s_add, i * 16 - 16)
                dve.wait_ge(s_y1, i + 1)
                dve.wait_ge(s_meta, i + 1)
                V.tensor_copy(ids[:, p, :], meta[:, p, 0:1])
                V.tensor_scalar(ys[:, p, :], yb[:, p, :], meta[:, p, 1:2], None, ALU.mult).then_inc(s_y, 1)

            def keep_row_ends(i, p, late):
                e = dve.value_load(tbi[0:1, 0, bass.ds(i, 1)], min_val=0, max_val=E - 1)
                dve.wait_ge(s_xr[p], (i // 2 + 1) * 16 if isinstance(i, int) else late)
                if not isinstance(i, int) or i >= 2:
                    dve.wait_ge(s_y, i - 1)
                V.tensor_copy(meta[:, p, 0:1], xr[:, p, C:C + 1])
                V.tensor_copy(meta[:, p, 1:2], xr[:, p, bass.ds(e + (C + 1), 1)]).then_inc(s_meta, 1)

            def vec_slot(m, p, late=None):
                st = isinstance(m, int)
                if not st or 0 <= m - 2 < SLOTS:
                    turned_hidden(m - 2, p)
                if not st or 0 <= m - 1 < SLOTS:
                    bias_hidden(m - 1, 1 - p)
                if not st or 0 <= m - 2 < SLOTS:
                    finish(m - 2, p)
                if not st or m < SLOTS:
                    keep_row_ends(m, p, late)

            for m in range(4):
                vec_slot(m, m % 2)
            with dve.Fori(2, SLOTS // 2) as g:
                for p in range(2):
                    vec_slot(2 * g + p, p, g * 16 + 16)
            vec_slot(SLOTS, 0)
            vec_slot(SLOTS + 1, 1)


NCONST = 28
NCW = 2 + 6 + 3 + 6 + 3 + 1 + 1
MAGIC = 0x5F3759DF + 1
TAB_PAD = 2
TAB_STEPS = 24


_NAMES = ["x", "w1t", "b1", "g1", "be1", "w2t", "b2", "g2", "be2", "w3t", "b3", "g3", "be3", "res_scale",
          "wqkv", "wout", "bout", "gate_w", "gate_b", "ew1", "eb1", "ew2", "eb2"]


def kernel(x, L0_conv_w1, L0_conv_b1, L0_conv_g1, L0_conv_be1, L0_conv_w2, L0_conv_b2, L0_conv_g2, L0_conv_be2,
           L0_conv_w3, L0_conv_b3, L0_conv_g3, L0_conv_be3, L0_conv_residual_scale, L1_attn_w_qkv, L1_attn_w_out,
           L1_attn_b_out, L1_ffn_gate_w, L1_ffn_gate_b, L1_ffn_w1, L1_ffn_b1, L1_ffn_w2, L1_ffn_b2):
    import numpy as np
    import concourse.bacc as bacc
    from concourse.bass_utils import run_bass_kernel_spmd

    values = [
        np.asarray(x).reshape(B, C, HW),
        np.asarray(L0_conv_w1).reshape(MID, C).T, L0_conv_b1, L0_conv_g1, L0_conv_be1,
        np.asarray(L0_conv_w2).transpose(2, 3, 1, 0), L0_conv_b2, L0_conv_g2, L0_conv_be2,
        np.asarray(L0_conv_w3).reshape(C, MID).T, L0_conv_b3, L0_conv_g3, L0_conv_be3,
        L0_conv_residual_scale, L1_attn_w_qkv, L1_attn_w_out, L1_attn_b_out,
        L1_ffn_gate_w, L1_ffn_gate_b, L1_ffn_w1, L1_ffn_b1, L1_ffn_w2, L1_ffn_b2,
    ]
    nc = bacc.Bacc("TRN2", target_bir_lowering=False, num_devices=1)
    arrays, args = {}, []
    for name, value in zip(_NAMES, values):
        a = np.ascontiguousarray(value)
        arrays[f"in_{name}"] = a
        args.append(nc.dram_tensor(f"in_{name}", a.shape, mybir.dt.from_np(a.dtype), kind="ExternalInput").ap())
    args.append(nc.dram_tensor("out_0", (TOKENS + 128, C), F32, kind="ExternalOutput").ap())
    moe_block(nc, *args)
    r = run_bass_kernel_spmd(nc, [arrays], core_ids=[0])
    tokens = np.asarray(r.results[0]["out_0"])[:TOKENS]
    return np.ascontiguousarray(tokens.reshape(B, HW, C).transpose(0, 2, 1)).reshape(B, C, SIDE, SIDE)
```

```python
from contextlib import ExitStack

import concourse.bass as bass
from concourse import mybir

F32 = mybir.dt.float32
I32 = mybir.dt.int32
FR = mybir.dt.float32r
U32 = mybir.dt.uint32
ALU = mybir.AluOpType
ACT = mybir.ActivationFunctionType
X = mybir.AxisListType.X

B, C, HW, SIDE = 16, 256, 196, 14
TOKENS = B * HW
MID = 64
HALF = HW // 2
TILES = B * 2
CHUNKS = 8
CW = 2 * HW
HEADS, DH = 16, 16
E, FF = 8, 1024
BN_EPS = LN_EPS = 1e-5
COLS = -(-TOKENS // 128)
NONE = E * COLS
ROW = C + E
SLOTS = (2 * TOKENS - E) // 128 + E
W1HI, W1LO, W2HI, W2LO = 0, 2 * FF, 4 * FF, 6 * FF
WSET = 8 * FF
BSET = FF + C
UNITS = 2 * E
UW = 2 * FF
EARLY = 4

LAG = {"in": 0, "norm": 1, "qkv": 2, "soft": 3, "ctx": 4, "out": 5, "norm2": 6}
STEPS = {
    "in": {"vec": ["mix0", "mix1"], "act": ["relu0", "relu1", "keep"], "pe": ["turn"]},
    "norm": {"vec": ["stat0", "stat1", "agg0", "agg1"], "act": ["norm0", "norm1", "xT"], "pe": ["xT"], "pool": ["bias"]},
    "qkv": {"pe": ["v", "q", "k"]},
    "soft": {"vec": ["kmax", "kneg", "qmax", "qsub", "qsum", "qrec", "krec"],
             "act": ["v", "kexp0", "kexp1", "qexp", "kT"], "pe": ["kT"], "pool": ["q"]},
    "ctx": {"vec": ["ctx0", "ctx1"], "act": ["proj"], "pe": ["ctx", "proj"]},
    "out": {"vec": ["add"], "pe": ["out"]},
    "norm2": {"vec": ["stat0", "stat1", "agg0", "agg1"], "act": ["norm0", "norm1", "xT"], "pe": ["xT", "logits"]},
    "root": {"vec": ["eps", "seed", "guess"] + [f"newton{k}{m}" for k in range(3) for m in range(3)] + ["shift"]},
    "route": {"vec": ["bias", "max", "sub", "sum", "rec", "prob", "top0", "top1", "top2", "top3",
                      "at0", "at1", "at2", "at3", "atf", "one1", "one2", "both", "den", "denr", "comb", "scale",
                      "run0", "run1", "run2", "run3", "pos", "pos1", "slot1", "pos2", "slot2", "slots",
                      "column", "row", "places"],
              "act": ["exp"], "pe": ["rank"]},
}
ROUTE_LAG = 8
SLOTS_A = B + 9
HOT_LAG = 11
POOL_HALVES = B - 2
RING = 6


def after(stage, engine, name, i):
    steps = STEPS[stage][engine]
    return i * len(steps) + steps.index(name) + 1


def moe_block(nc, x, w1t, w2t, w3t, norms, res_scale, wqkv, wout, bout, gate_w, gate_b, ew1, ew2, eb, out):
    split_w = nc.dram_tensor("split_weights", [E, 128, 2, 2 * UW], F32, kind="Internal").ap()
    norm_rows = nc.dram_tensor("normalised_rows", [TOKENS + 128, ROW], F32, kind="Internal").ap()
    ctx = ExitStack()
    with ctx:
        def sb(name, shape, dt=F32):
            return ctx.enter_context(nc.sbuf_tensor(name, shape, dt))

        def sem(name):
            return ctx.enter_context(nc.semaphore(name))

        img = sb("img", [128, B, 4 * HW])
        vecs = sb("vecs", [128, 3, 3, 2])
        bst = sb("bst", [128, 2, CHUNKS, 6])
        bmv = sb("bmv", [128, 2, 2])
        bn = sb("bn", [128, 8, 2])
        rs = sb("rs", [128, 6])
        coef = sb("coef", [128, 3, 2, 2])
        wq = sb("wq", [128, 2, 3 * C])
        wo = sb("wo", [128, 2, C])
        bo2 = sb("bo2", [HALF, 2, C])
        gw = sb("gw", [128, 2, E])
        gb = sb("gb", [HALF, 4, E])
        ident = sb("ident", [128, 128])
        ones = sb("ones", [HALF, 128])
        upper = sb("upper", [HALF, HALF])
        heads = sb("heads", [128, 128])
        iotf = sb("iotf", [128, NONE])
        expert_id = sb("expert_id", [HALF, 4, E])
        expert_row = sb("expert_row", [HALF, 4, E])
        tokid_i = sb("tokid_i", [HALF, TILES], I32)
        tokid = sb("tokid", [HALF, TILES])
        tc = sb("tc", [128, 2, 2, HW])
        xT = sb("xT", [128, 2, 2, HW])
        stt = sb("stt", [HALF, 2, 2, 2, 6])
        mv = sb("mv", [HALF, 2, 2, 2, 2])
        sm = sb("sm", [HALF, 2, 4, 2, 2])
        qr = sb("qr", [HALF, 2, 3, 2 * HEADS])
        kx = sb("kx", [128, 2, 4, 2])
        rows = sb("rows", [HALF, RING, 2, ROW])
        lg = sb("lg", [HALF, 2, 4, E])
        rt = sb("rt", [HALF, 12, 4, E])
        rv = sb("rv", [HALF, 2, 8, 4])
        top = sb("top", [HALF, 4, 8])
        topi = sb("topi", [HALF, 4, 8], U32)
        topf = sb("topf", [HALF, 4, 2])
        run = sb("run", [HALF, 2, 5, E])
        slot = sb("slot", [HALF, 3, 2, 4], I32)
        place = sb("place", [HALF, 2, 2, 2, 4])
        hot_row = sb("hot_row", [HALF, 4, 128], FR)
        hot_col = sb("hot_col", [HALF, 4, NONE], FR)
        table = sb("table", [128, NONE + 1])
        table_ids = sb("table_ids", [128, NONE + 1], U32)
        cnti = sb("cnti", [128, E], I32)
        ntl = sb("ntl", [128, 2, E])
        spare = sb("spare", [128, 1])
        lt = sb("lt", [128, E, E])
        big = sb("big", [128, 2, 64, E])
        iot = big[:, 0].rearrange("p a e -> p (a e)")[:, 0:NONE].bitcast(I32)
        tb = sb("tb", [128, 5, 64])
        tbi = sb("tbi", [128, 2, 64], I32)
        packed = sb("packed", [128, 2, SLOTS // 4])
        packedi = sb("packedi", [128, SLOTS // 4], I32)
        last_tile = sb("last_tile", [128, E], I32)
        is_expert = big[:, 1]
        wset = sb("wset", [128, 2 * WSET], FR)
        bset = sb("bset", [128, 2 * BSET])
        xr = sb("xr", [128, 2, ROW])
        ids = sb("ids", [128, 4, 1], U32)
        ids_add = sb("ids_add", [128, 2, 1], U32)
        wsel = sb("wsel", [128, E])
        meta = sb("meta", [128, 2])

        raw = [wset[:, a * 3 * UW:a * 3 * UW + UW].bitcast(F32) for a in range(2)]
        part_hi = [wset[:, a * 3 * UW + UW:a * 3 * UW + 2 * UW] for a in range(2)]
        part_lo = [wset[:, a * 3 * UW + 2 * UW:(a + 1) * 3 * UW] for a in range(2)]
        with ExitStack() as scope:
            pad = scope.enter_context(nc.sbuf_tensor("pad", [128, B * 256], F32))
            mid2 = scope.enter_context(nc.sbuf_tensor("mid2", [MID, TOKENS], F32))
            w1s = scope.enter_context(nc.sbuf_tensor("w1s", [128, 2, 128], F32))
            w2s = scope.enter_context(nc.sbuf_tensor("w2s", [128, 6, MID], F32))
            w3s = scope.enter_context(nc.sbuf_tensor("w3s", [MID, C], F32))
            padrow = scope.enter_context(nc.sbuf_tensor("padrow", [128, ROW], F32))
        with ExitStack() as scope:
            def mem(name, shape):
                return scope.enter_context(nc.sbuf_tensor(name, shape, F32))
            xh = mem("xh", [HALF, 2, 2, C])
            qe = mem("qe", [HALF, 2, 2 * C])
            qn = mem("qn", [HALF, 2, 2 * C])
            ek = mem("ek", [128, 2, 2, HW])
            vT = mem("vT", [128, 3, 2, HW])
            ekt = mem("ekt", [HALF, 2, 2, C])
            cT = mem("cT", [128, 2, 2, 128])
            pr = mem("pr", [128, 2, 2, C])
            xT2 = mem("xT2", [128, 2, 2, HW])
        xrTh = sb("xrTh", [128, 2, C], FR)
        xrTl = sb("xrTl", [128, 2, C], FR)
        hb = sb("hb", [128, 2, FF])
        hTh = sb("hTh", [128, 2, FF], FR)
        hTl = sb("hTl", [128, 2, FF], FR)
        table_pad = sb("table_pad", [128, NONE + 1])
        yb = sb("yb", [128, 2, C])
        ys = sb("ys", [128, 2, C])

        ps = ctx.enter_context(nc.psum_tensor("ps", [128, 8, 512], F32))
        psT, psX, psQ, psK, psV = (ps[:, n, :] for n in range(5))
        psE, psC, psL = ps[:, 5, :], ps[:, 6, :], ps[:, 7, :]

        s_x = [sem(f"x_loaded{q}") for q in range(4)]
        s_w1 = sem("conv1_weights_loaded")
        s_wc = sem("conv_weights_loaded")
        s_wa = sem("attention_weights_loaded")
        s_const = sem("constants_built")
        s_conv = sem("conv_products")
        s_cst = sem("conv_stats")
        s_fin = sem("conv_coefficients")
        s_ca = sem("conv_applied")
        s_sp = sem("softplus_steps")
        S = {st: {en: sem(f"{st}_steps_of_{en}") for en in STEPS[st]} for st in STEPS}
        s_rows = [sem(f"normalised_rows_written{a}") for a in range(RING // 2)]
        s_hot = sem("one_hot_tables")
        s_tmm = sem("table_products")
        s_tadd = sem("table_added")
        s_ids = sem("row_numbers_picked")
        s_kept = sem("row_numbers_kept")
        s_res = sem("residual_written")
        s_padw = sem("padding_written")
        s_cntp = sem("counts_summed")
        s_tab = sem("table_steps")
        s_raw = [sem(f"matrix_loaded{a}") for a in range(2)]
        s_hi = sem("leading_part_made")
        s_lo = sem("rest_made")
        s_split = [sem(f"matrix_split{a}") for a in range(2)]
        s_w = sem("expert_weights_loaded")
        s_xr = [sem(f"rows_loaded{p}") for p in range(2)]
        s_ws = sem("weight_picked")
        s_meta = sem("row_ends_kept")
        s_eT = sem("rows_turned")
        s_xhi = sem("turned_rows_leading")
        s_xlo = sem("turned_rows_rest")
        s_h = sem("hidden_products")
        s_hb = sem("hidden_biased")
        s_ge = sem("hidden_activated")
        s_hT = sem("hidden_turned")
        s_hhi = sem("turned_hidden_leading")
        s_hlo = sem("turned_hidden_rest")
        s_yp = sem("expert_products")
        s_y1 = sem("expert_biased")
        s_y = sem("expert_rows_ready")
        s_add = sem("rows_added")
        s_go = sem("adding_may_start")

        ps_chunk = lambda c, n=128: ps[0:n, c, 0:CW]
        block = ctx.enter_context(nc.Block())

        def wait_for(eng, stage, engine, name, i):
            if i >= 0:
                eng.wait_ge(S[stage][engine], after(stage, engine, name, i))


        def one_hot(eng, q):
            g, k = q // 2, q % 2
            wait_for(eng, "route", "vec", "places", g)
            if q:
                eng.wait_ge(s_tmm, q)
            for t in range(4):
                eng.tensor_scalar(hot_row[:, t, :], iotf[0:HALF, 0:128], place[:, g % 2, 1, k, t:t + 1], None,
                                  ALU.is_equal).then_inc(s_hot, 1)
                eng.tensor_scalar(hot_col[:, t, :], iotf[0:HALF, :], place[:, g % 2, 0, k, t:t + 1],
                                  tokid[:, 4 * g + t:4 * g + t + 1], ALU.is_equal, ALU.mult).then_inc(s_hot, 1)

        @block.sync
        def _(sp):
            for q in range(4):
                for k in range(2):
                    sp.dma_start(img[:, 4 * q:4 * q + 4, k * HW:(k + 1) * HW],
                                 x[4 * q:4 * q + 4, k * 128:(k + 1) * 128, :].rearrange("b p n -> p b n")
                                 ).then_inc(s_x[q], 16)
                if q == 0:
                    for m in range(2):
                        sp.dma_start(w1s[:, :, m * MID:(m + 1) * MID],
                                     w1t.rearrange("(k p) m -> p k m", p=128)).then_inc(s_w1, 16)
            sp.dma_start(vecs[:, :, :, :], norms).then_inc(s_wc, 16)
            sp.dma_start(w2s[0:64, 0:3, :], w2t[0].rearrange("d i o -> i d o")).then_inc(s_wc, 16)
            sp.dma_start(w2s[64:128, 0:3, :], w2t[1].rearrange("d i o -> i d o")).then_inc(s_wc, 16)
            sp.dma_start(w2s[0:64, 3:6, :], w2t[2].rearrange("d i o -> i d o")).then_inc(s_wc, 16)
            sp.dma_start(w3s[:, :], w3t).then_inc(s_wc, 16)
            sp.dma_start(rs[:, 0:1], res_scale.rearrange("(a b) -> a b", a=1).to_broadcast([128, 1])).then_inc(s_wc, 16)

            def load_matrix(u):
                if u >= 2:
                    sp.wait_ge(s_lo, u - 1)
                src = ew1[u // 2] if u % 2 == 0 else ew2[u // 2]
                sp.dma_start(raw[u % 2].rearrange("p (k f) -> p k f", k=2 if u % 2 == 0 else 8),
                             src.rearrange("(k p) f -> p k f", p=128)).then_inc(s_raw[u % 2], 16)

            def store_parts(u):
                sp.wait_ge(s_hi, u + 1)
                sp.wait_ge(s_lo, u + 1)
                sp.dma_start(split_w[u // 2, :, u % 2, :],
                             wset[:, (u % 2) * 3 * UW + UW:(u % 2 + 1) * 3 * UW].bitcast(F32)).then_inc(s_split[u % 2], 16)

            load_matrix(0)
            load_matrix(1)
            sp.dma_start(wq[:, :, :], wqkv.rearrange("(k p) n -> p k n", p=128)).then_inc(s_wa, 16)
            sp.dma_start(wo[:, :, :], wout.rearrange("(k p) n -> p k n", p=128)).then_inc(s_wa, 16)
            sp.dma_start(gw[:, :, :], gate_w.rearrange("(k p) n -> p k n", p=128)).then_inc(s_wa, 16)
            for j in range(2):
                sp.dma_start(bo2[:, j, :], bout.rearrange("(a n) -> a n", a=1).to_broadcast([HALF, C])).then_inc(s_wa, 16)
            for j in range(4):
                sp.dma_start(gb[:, j, :], gate_b.rearrange("(a n) -> a n", a=1).to_broadcast([HALF, E])).then_inc(s_wa, 16)

            def load_part(e, n):
                p, w = e % 2, WSET // WPARTS
                if n or e:
                    sp.wait_ge(s_w, LOAD_E * e + 16 * n)
                if n < WPARTS:
                    sp.dma_start(wset[:, p * WSET + n * w:p * WSET + (n + 1) * w].bitcast(F32),
                                 split_w[e].rearrange("p m n -> p (m n)")[:, n * w:(n + 1) * w]).then_inc(s_w, 16)
                else:
                    sp.dma_start(bset[:, p * BSET:(p + 1) * BSET],
                                 eb[e:e + 1, :].to_broadcast([128, BSET])).then_inc(s_w, 16)

            def load_expert(e):
                for n in range(WPARTS + 1):
                    load_part(e, n)

            sp.wait_ge(s_const, NCONST)
            sp.dma_start(norm_rows[TOKENS:TOKENS + 128, :], padrow[:, :]).then_inc(s_padw, 16)
            sp.dma_start(out[TOKENS:TOKENS + 128, :], padrow[:, 0:C]).then_inc(s_padw, 16)

            def split_step(u):
                store_parts(u)
                if u + 2 < UNITS:
                    load_matrix(u + 2)

            for u in range(EARLY):
                split_step(u)
            for n in range(SLOTS_A):
                if n + EARLY < UNITS:
                    split_step(n + EARLY)
                i = n - LAG["out"]
                if 0 <= i < B:
                    wait_for(sp, "out", "vec", "add", i)
                    sp.dma_start(out[i * HW:(i + 1) * HW, :].rearrange("(j p) d -> p j d", p=HALF),
                                 img[0:HALF, i, 0:2 * C].rearrange("p (j d) -> p j d", j=2)).then_inc(s_res, 16)
                if n > ROUTE_LAG and n % 2:
                    g = (n - ROUTE_LAG) // 2
                    wait_for(sp, "route", "vec", "scale", g)
                    wait_for(sp, "norm2", "act", "norm1", 2 * g + 1)
                    at = (2 * g) % RING
                    sp.dma_start(norm_rows[2 * g * HW:(2 * g + 2) * HW, :].rearrange("(j p) d -> p j d", p=HALF),
                                 rows[:, at:at + 2, :, :].rearrange("p i j d -> p (i j) d")
                                 ).then_inc(s_rows[g % (RING // 2)], 16)
                if n == UNITS - EARLY:
                    for a in range(2):
                        sp.wait_ge(s_split[a], 16 * UNITS // 2)
                if UNITS - EARLY <= n <= UNITS - EARLY + WPARTS:
                    load_part(0, n - UNITS + EARLY)
            load_expert(1)
            sp.wait_ge(s_tab, TAB_STEPS)
            ends = [sp.value_load(last_tile[0:1, e - 2:e - 1], min_val=1, max_val=SLOTS) for e in range(2, E)]
            for e in range(2, E):
                sp.wait_ge(s_y1, ends[e - 2])
                load_expert(e)

        @block.gpsimd
        def _(pool):
            count = [0]

            def built(ins):
                ins.then_inc(s_const, 1)
                count[0] += 1
                pool.wait_ge(s_const, count[0])

            built(pool.memset(pad[:, :], 0.0))
            built(pool.memset(w2s[64:128, 3:6, :], 0.0))
            for t, v in ((ident, 0.0), (ones, 1.0), (upper, 1.0), (heads, 1.0), (padrow, 0.0)):
                built(pool.memset(t[:, :], v))
            built(pool.memset(run[:, :, :, :], 0.0))
            built(pool.memset(lt[:, :, :], 1.0))
            built(pool.iota(tokid_i[:, :], pattern=[[HALF, TILES]], base=1, channel_multiplier=1))
            built(pool.iota(iot, pattern=[[1, NONE]], base=0, channel_multiplier=0))
            built(pool.affine_select(out=ident[:, :], in_=ident[:, :], compare_op=ALU.not_equal, fill=1.0,
                                     base=0, pattern=[[-1, 128]], channel_multiplier=1))
            built(pool.affine_select(out=upper[:, :], in_=upper[:, :], compare_op=ALU.is_gt, fill=0.0,
                                     base=0, pattern=[[1, HALF]], channel_multiplier=-1))
            hv = heads[:, :].rearrange("p (h d) -> p h d", d=DH)
            built(pool.affine_select(out=hv, in_=hv, compare_op=ALU.is_ge, fill=0.0,
                                     base=0, pattern=[[-DH, 8], [0, DH]], channel_multiplier=1))
            built(pool.affine_select(out=hv, in_=hv, compare_op=ALU.is_ge, fill=0.0,
                                     base=DH - 1, pattern=[[DH, 8], [0, DH]], channel_multiplier=-1))
            built(pool.affine_select(out=lt[:, :, :], in_=lt[:, :, :], compare_op=ALU.is_ge, fill=0.0,
                                     base=0, pattern=[[1, E], [-1, E]], channel_multiplier=0))
            built(pool.iota(cnti[:, :], pattern=[[0, E]], base=TOKENS + 1, channel_multiplier=1))
            built(pool.tensor_copy(spare[:, :], cnti[:, 0:1]))
            built(pool.tensor_copy(tokid[:, :], tokid_i[:, :]))
            built(pool.tensor_copy(iotf[:, :], iot))
            built(pool.memset(table[:, :], 0.0))
            for j in range(4):
                built(pool.tensor_copy(expert_id[:, j, :], iot[0:HALF, 0:E]))
            for j in range(4):
                built(pool.tensor_scalar(expert_row[:, j, :], expert_id[:, j, :], float(128 * COLS), None, ALU.mult))
            assert count[0] == NCONST

            def split_rest(u):
                a = u % 2
                pool.wait_ge(s_hi, u + 1)
                pool.tensor_tensor(part_lo[a], raw[a], part_hi[a].bitcast(F32), ALU.subtract).then_inc(s_lo, 1)

            for u in range(EARLY):
                split_rest(u)

            def norm_bias(i):
                wait_for(pool, "norm", "act", "norm1", i)
                t = img[0:HALF, i, 0:2 * C]
                pool.tensor_tensor(t, t, bo2[:, :, :].rearrange("p j d -> p (j d)"), ALU.add).then_inc(S["norm"]["pool"], 1)

            def soft_q(i):
                p = i % 2
                wait_for(pool, "soft", "vec", "qrec", i)
                wait_for(pool, "ctx", "pe", "ctx", i - 2)
                pool.tensor_tensor(qn[:, p, :].rearrange("p (g d) -> p g d", d=DH),
                                   qe[:, p, :].rearrange("p (g d) -> p g d", d=DH),
                                   qr[:, p, 2, :].unsqueeze(2).to_broadcast([HALF, 2 * HEADS, DH]),
                                   ALU.mult).then_inc(S["soft"]["pool"], 1)

            pool.wait_ge(s_wa, 9 * 16)
            for n in range(SLOTS_A):
                if 0 <= n - HOT_LAG < POOL_HALVES:
                    one_hot(pool, n - HOT_LAG)
                if 0 <= n - LAG["norm"] < B:
                    norm_bias(n - LAG["norm"])
                if 0 <= n - LAG["soft"] < B:
                    soft_q(n - LAG["soft"])
                if n + EARLY < UNITS:
                    split_rest(n + EARLY)
            pool.wait_ge(s_res, 16 * B)
            for a in range(RING // 2):
                pool.wait_ge(s_rows[a], 16 * len(range(a, B // 2, RING // 2)))
            pool.wait_ge(s_padw, 32)

            def gather(i, r):
                pool.wait_ge(s_ids, i + 1)
                if not isinstance(i, int) or i >= 2:
                    pool.wait_ge(s_meta, i - 1)
                    pool.wait_ge(s_eT, i - 1)
                    pool.sem_inc(s_go, 1)
                pool.indirect_dma_start(xr[:, r % 2, :], None, norm_rows,
                                        bass.IndirectOffsetOnAxis(ids[:, r % 4, :], 0)).then_inc(s_xr[r % 2], 16)

            def add_rows(i, r):
                pool.wait_ge(s_y, i + 1)
                pool.wait_ge(s_kept, i + 1)
                if not isinstance(i, int) or i >= 1:
                    pool.wait_ge(s_add, i * 16)
                pool.sem_inc(s_go, 1)
                pool.indirect_dma_start(out, bass.IndirectOffsetOnAxis(ids_add[:, r % 2, :], 0), ys[:, r % 2, :], None,
                                        compute_op=ALU.add).then_inc(s_add, 16)

            def pool_slot(m, r):
                if not isinstance(m, int) or m + 1 < SLOTS:
                    gather(m + 1, r + 1)
                if not isinstance(m, int) or 0 <= m - 2 < SLOTS:
                    add_rows(m - 2, r + 2)

            gather(0, 0)
            for m in range(4):
                pool_slot(m, m)
            with pool.Fori(1, SLOTS // 4 - 1) as g:
                for r in range(4):
                    pool_slot(4 * g + r, r)
            for m in range(SLOTS - 4, SLOTS + 2):
                pool_slot(m, m % 4)
            pool.wait_ge(s_add, 16 * SLOTS)

        @block.scalar
        def _(act):
            def split_leading(u):
                a = u % 2
                act.wait_ge(s_raw[a], 16 * (u // 2 + 1))
                if u >= 2:
                    act.wait_ge(s_split[a], 16 * (u // 2))
                act.copy(part_hi[a], raw[a]).then_inc(s_hi, 1)

            pv = pad[:, :].rearrange("p (b r c) -> p b r c", b=B, c=16)
            act.wait_ge(s_const, 1)
            for u in range(2):
                split_leading(u)
            act.wait_ge(s_fin, 1)
            for c in range(CHUNKS):
                src = ps_chunk(c).rearrange("p (b r c) -> p b r c", b=2, c=SIDE)
                for h in range(2):
                    q = slice(64 * h, 64 * h + 64)
                    dst = pv[q, 2 * c:2 * c + 2, 1 - h:15 - h, 1:15]
                    for b in range(2):
                        last = act.activation(dst[:, b], src[q, b], ACT.Relu, bias=coef[q, 0, 1, 0:1], scale=coef[q, 0, 0, 0:1])
                last.then_inc(s_ca, 1)
            act.wait_ge(s_sp, 1)
            act.activation(rs[:, 2:3], rs[:, 1:2], ACT.Exp, scale=-1.0).then_inc(s_sp, 1)
            act.wait_ge(s_sp, 3)
            act.activation(rs[:, 4:5], rs[:, 3:4], ACT.Ln).then_inc(s_sp, 1)
            for u in range(2, 4):
                split_leading(u)
            act.wait_ge(s_fin, 2)
            for c in range(CHUNKS):
                act.activation(mid2[0:MID, c * CW:(c + 1) * CW], ps_chunk(c, MID), ACT.Relu,
                               bias=coef[0:MID, 1, 1, 0:1], scale=coef[0:MID, 1, 0, 0:1]).then_inc(s_ca, 1)
            for c in range(CHUNKS):
                for h in range(2):
                    act.wait_ge(s_conv, 2 * CHUNKS + 2 * c + h + 1)
                    act.copy(img[:, 2 * c:2 * c + 2, (2 + h) * HW:(3 + h) * HW],
                             ps_chunk((2 * c + h) % 8).rearrange("p (b n) -> p b n", b=2)).then_inc(s_ca, 1)

            def in_relu(i):
                p = i % 2
                for k in range(2):
                    wait_for(act, "in", "vec", f"mix{k}", i)
                    act.activation(tc[:, p, k, :], tc[:, p, k, :], ACT.Relu,
                                   bias=coef[:, 2, 1, k:k + 1]).then_inc(S["in"]["act"], 1)

            def in_keep(i):
                wait_for(act, "in", "pe", "turn", i)
                act.copy(img[0:HALF, i, 0:2 * C], psT[0:HALF, :]).then_inc(S["in"]["act"], 1)

            def normalise(stage, which, i, n, out):
                act.wait_ge(S["root"]["vec"], n * len(STEPS["root"]["vec"]))
                for j in range(2):
                    act.activation(out[j], img[0:HALF, i, j * C:(j + 1) * C], ACT.Identity,
                                   scale=sm[:, n % 2, 1, which, j:j + 1],
                                   bias=sm[:, n % 2, 3, which, j:j + 1]).then_inc(S[stage]["act"], 1)

            def norm_norm(i, n):
                wait_for(act, "norm", "pe", "xT", i - 2)
                normalise("norm", 0, i, n, [xh[:, i % 2, j, :] for j in range(2)])

            def norm2_norm(i, n):
                if i >= RING:
                    g = (i - RING) // 2
                    act.wait_ge(s_rows[g % (RING // 2)], 16 * (g // (RING // 2) + 1))
                normalise("norm2", 1, i, n, [rows[:, i % RING, j, 0:C] for j in range(2)])

            def norm_xT(i):
                wait_for(act, "norm", "pe", "xT", i)
                wait_for(act, "qkv", "pe", "k", i - 2)
                act.copy(xT[:, i % 2, :, :].rearrange("p k n -> p (k n)"), psX[:, 0:CW]).then_inc(S["norm"]["act"], 1)

            def soft_v(i):
                wait_for(act, "qkv", "pe", "v", i)
                wait_for(act, "out", "pe", "out", i - 3)
                act.copy(vT[:, i % 3, :, :].rearrange("p k n -> p (k n)"), psV[:, 0:CW]).then_inc(S["soft"]["act"], 1)

            def soft_exps(i):
                p = i % 2
                wait_for(act, "soft", "vec", "kneg", i)
                wait_for(act, "soft", "pe", "kT", i - 2)
                for h in range(2):
                    act.activation(ek[:, p, h, :], psK[:, h * HW:(h + 1) * HW], ACT.Exp, bias=kx[:, p, 1, h:h + 1],
                                   accum_out=kx[:, p, 2, h:h + 1]).then_inc(S["soft"]["act"], 1)
                wait_for(act, "soft", "vec", "qsub", i)
                act.activation(qe[:, p, :], qe[:, p, :], ACT.Exp, scale=float(DH) ** -0.5).then_inc(S["soft"]["act"], 1)

            def soft_kT(i):
                p = i % 2
                wait_for(act, "soft", "pe", "kT", i)
                wait_for(act, "ctx", "pe", "ctx", i - 2)
                act.copy(ekt[:, p, :, :].rearrange("p j d -> p (j d)"), psE[0:HALF, :]).then_inc(S["soft"]["act"], 1)

            def ctx_proj(i):
                wait_for(act, "ctx", "pe", "proj", i)
                wait_for(act, "out", "pe", "out", i - 2)
                act.copy(pr[:, i % 2, :, :].rearrange("p k d -> p (k d)"), psE[:, :]).then_inc(S["ctx"]["act"], 1)

            def norm2_xT(i):
                wait_for(act, "norm2", "pe", "xT", i)
                wait_for(act, "norm2", "pe", "logits", i - 2)
                act.copy(xT2[:, i % 2, :, :].rearrange("p k n -> p (k n)"), psL[:, 0:CW]).then_inc(S["norm2"]["act"], 1)

            def route_exp(g):
                wait_for(act, "route", "vec", "sub", g)
                act.activation(rt[:, 0], rt[:, 0], ACT.Exp).then_inc(S["route"]["act"], 1)

            for n in range(SLOTS_A):
                for stage, do in (("soft", soft_v), ("soft", soft_exps), ("in", in_relu),
                                  ("norm", lambda i: norm_norm(i, n)), ("norm2", lambda i: norm2_norm(i, n)),
                                  ("soft", soft_kT), ("in", in_keep), ("ctx", ctx_proj)):
                    if 0 <= n - LAG[stage] < B:
                        do(n - LAG[stage])
                if n >= ROUTE_LAG and n % 2 == 0 and (n - ROUTE_LAG) // 2 < B // 2:
                    route_exp((n - ROUTE_LAG) // 2)
                for stage, do in (("norm", norm_xT), ("norm2", norm2_xT)):
                    if 0 <= n - LAG[stage] < B:
                        do(n - LAG[stage])
                if n + EARLY < UNITS:
                    split_leading(n + EARLY)

            act.wait_ge(s_tab, TAB_STEPS)

            def pick_ids(i, r):
                column = act.value_load(tbi[0:1, 1, bass.ds(i, 1)], min_val=0, max_val=NONE)
                act.copy(ids[:, r % 4, :], table_ids[:, bass.ds(column, 1)]).then_inc(s_ids, 1)

            def keep_ids(i, r):
                act.wait_ge(s_ids, i + 1)
                if not isinstance(i, int) or i >= 2:
                    act.wait_ge(s_add, 16 * i - 16)
                act.copy(ids_add[:, r % 2, :], ids[:, r % 4, :]).then_inc(s_kept, 1)

            def turned(i, p):
                act.wait_ge(s_eT, i + 1)
                act.copy(xrTh[:, p, :], ps[:, 0, 0:C]).then_inc(s_xhi, 1)

            def gelu(i, p):
                for h in range(2):
                    act.wait_ge(s_hb, 2 * i + h + 1)
                    act.activation(hb[:, p, h * 512:(h + 1) * 512], hb[:, p, h * 512:(h + 1) * 512],
                                   ACT.Gelu).then_inc(s_ge, 1)

            def turned_hidden(i, p):
                for h in range(2):
                    act.wait_ge(s_hT, 2 * i + h + 1)
                    act.copy(hTh[:, p, h * 512:(h + 1) * 512], ps[:, 3 + h, :]).then_inc(s_hhi, 1)

            def act_slot(m, r):
                st = isinstance(m, int)
                p = r % 2
                if not st or 0 <= m - 2 < SLOTS:
                    turned_hidden(m - 2, p)
                if not st or m < SLOTS:
                    turned(m, p)
                if not st or m + 2 < SLOTS:
                    if not st or m >= 2:
                        act.wait_ge(s_kept, m - 1)
                    pick_ids(m + 2, r + 2)
                if not st or 0 <= m - 1 < SLOTS:
                    gelu(m - 1, 1 - p)
                    keep_ids(m - 1, r + 3)

            pick_ids(0, 0)
            pick_ids(1, 1)
            for m in range(4):
                act_slot(m, m)
            with act.Fori(1, SLOTS // 4 - 1) as g:
                for r in range(4):
                    act_slot(4 * g + r, r)
            for m in range(SLOTS - 4, SLOTS + 2):
                act_slot(m, m % 4)

        @block.tensor
        def _(pe):
            pe.wait_ge(s_w1, 32)
            for c in range(CHUNKS):
                if c % 2 == 0:
                    pe.wait_ge(s_x[c // 2], 32)
                for k in range(2):
                    last = pe.matmul(ps_chunk(c), w1s[:, k, :], img[:, 2 * c:2 * c + 2, k * HW:(k + 1) * HW],
                                     start=(k == 0), stop=(k == 1))
                last.then_inc(s_conv, 1)
            pv = pad[:, :].rearrange("p (b r c) -> p b r c", b=B, c=16)
            pe.wait_ge(s_const, 2)
            pe.wait_ge(s_wc, 16 * NCW)
            for c in range(CHUNKS):
                pe.wait_ge(s_ca, c + 1)
                for t in range(6):
                    r, d = (0, t) if t < 3 else (2, t - 3)
                    for b in range(2):
                        last = pe.matmul(ps[0:MID, c, b * HW:(b + 1) * HW], w2s[:, t, :],
                                         pv[:, 2 * c + b, r:r + SIDE, d:d + SIDE],
                                         start=(t == 0 and b == 0), stop=(t == 5), skip_group_check=True)
                last.then_inc(s_conv, 1)
            for c in range(CHUNKS):
                for h in range(2):
                    n = 2 * c + h
                    pe.wait_ge(s_ca, CHUNKS + n + 1 if n < 8 else 2 * CHUNKS + n - 7)
                    pe.matmul(ps_chunk(n % 8), w3s[:, h * 128:(h + 1) * 128], mid2[0:MID, c * CW:(c + 1) * CW],
                              start=True, stop=True).then_inc(s_conv, 1)
            pe.wait_ge(s_wa, 9 * 16)
            pe.wait_ge(s_const, NCONST)
            pe.wait_ge(s_ca, 4 * CHUNKS)

            def in_turn(i):
                p = i % 2
                wait_for(pe, "in", "act", "relu1", i)
                wait_for(pe, "in", "act", "keep", i - 1)
                if i > HOT_LAG:
                    pe.wait_ge(s_tadd, i - HOT_LAG)
                for j in range(2):
                    for k in range(2):
                        last = pe.transpose(psT[0:HALF, j * C + k * 128:j * C + (k + 1) * 128],
                                            tc[:, p, k, j * HALF:(j + 1) * HALF], ident[:, :])
                last.then_inc(S["in"]["pe"], 1)

            def norm_xT(i):
                p = i % 2
                wait_for(pe, "norm", "act", "norm1", i)
                wait_for(pe, "norm", "act", "xT", i - 1)
                for k in range(2):
                    for j in range(2):
                        last = pe.transpose(psX[:, k * HW + j * HALF:k * HW + (j + 1) * HALF],
                                            xh[:, p, j, k * 128:(k + 1) * 128], ident[0:HALF, 0:HALF])
                last.then_inc(S["norm"]["pe"], 1)

            def qkv_q(i):
                p = i % 2
                wait_for(pe, "norm", "act", "xT", i)
                wait_for(pe, "soft", "vec", "qsub", i - 1)
                for j in range(2):
                    for k in range(2):
                        last = pe.matmul(psQ[0:HALF, j * C:(j + 1) * C], xT[:, p, k, j * HALF:(j + 1) * HALF],
                                         wq[:, k, 0:C], start=(k == 0), stop=(k == 1))
                last.then_inc(S["qkv"]["pe"], 1)

            def qkv_kv(i, dst, off, free):
                p = i % 2
                wait_for(pe, "norm", "act", "xT", i)
                wait_for(pe, "soft", "act", free, i - 1)
                for h in range(2):
                    for k in range(2):
                        last = pe.matmul(dst[:, h * HW:(h + 1) * HW], wq[:, k, off + h * 128:off + (h + 1) * 128],
                                         xT[:, p, k, :], start=(k == 0), stop=(k == 1))
                last.then_inc(S["qkv"]["pe"], 1)

            def soft_kT(i):
                p = i % 2
                wait_for(pe, "soft", "act", "kexp1", i)
                wait_for(pe, "ctx", "act", "proj", i - 2)
                for j in range(2):
                    for h in range(2):
                        last = pe.transpose(psE[0:HALF, j * C + h * 128:j * C + (h + 1) * 128],
                                            ek[:, p, h, j * HALF:(j + 1) * HALF], ident[:, :])
                last.then_inc(S["soft"]["pe"], 1)

            def ctx_ctx(i):
                p = i % 2
                wait_for(pe, "soft", "act", "kT", i)
                wait_for(pe, "soft", "pool", "q", i)
                wait_for(pe, "out", "vec", "add", i - 1)
                for h in range(2):
                    for j in range(2):
                        last = pe.matmul(psC[:, h * 128:(h + 1) * 128], ekt[:, p, j, h * 128:(h + 1) * 128],
                                         qn[:, p, j * C + h * 128:j * C + (h + 1) * 128], start=(j == 0), stop=(j == 1))
                last.then_inc(S["ctx"]["pe"], 1)

            def ctx_proj(i):
                p = i % 2
                wait_for(pe, "ctx", "vec", "ctx1", i)
                wait_for(pe, "soft", "act", "kT", min(i + 1, B - 1))
                for h in range(2):
                    last = pe.matmul(psE[:, h * C:(h + 1) * C], cT[:, p, h, :], wo[:, h, :], start=True, stop=True)
                last.then_inc(S["ctx"]["pe"], 1)

            def out_out(i):
                wait_for(pe, "ctx", "act", "proj", i)
                for j in range(2):
                    for h in range(2):
                        last = pe.matmul(psC[0:HALF, j * C:(j + 1) * C], vT[:, i % 3, h, j * HALF:(j + 1) * HALF],
                                         pr[:, i % 2, h, :], start=(h == 0), stop=(h == 1))
                last.then_inc(S["out"]["pe"], 1)

            def norm2_xT(i):
                wait_for(pe, "norm2", "act", "norm1", i)
                wait_for(pe, "norm2", "act", "xT", i - 1)
                if i % 2 == 0:
                    wait_for(pe, "route", "vec", "bias", i // 2 - 1)
                for k in range(2):
                    for j in range(2):
                        last = pe.transpose(psL[:, k * HW + j * HALF:k * HW + (j + 1) * HALF],
                                            rows[:, i % RING, j, k * 128:(k + 1) * 128], ident[0:HALF, 0:HALF])
                last.then_inc(S["norm2"]["pe"], 1)

            def norm2_logits(i):
                wait_for(pe, "norm2", "act", "xT", i)
                wait_for(pe, "route", "vec", "bias", i // 2 - 1)
                for j in range(2):
                    at = CW + ((i % 2) * 2 + j) * E
                    for k in range(2):
                        last = pe.matmul(psL[0:HALF, at:at + E], xT2[:, i % 2, k, j * HALF:(j + 1) * HALF],
                                         gw[:, k, :], start=(k == 0), stop=(k == 1))
                last.then_inc(S["norm2"]["pe"], 1)

            def route_rank(g):
                wait_for(pe, "route", "vec", "run3", g)
                wait_for(pe, "norm2", "act", "xT", min(2 * g + 3, B - 1))
                pe.matmul(psL[0:HALF, CW + 32:CW + 64], upper[:, :], rt[:, 4].rearrange("p t e -> p (t e)"),
                          start=True, stop=False)
                pe.matmul(psL[0:HALF, CW + 32:CW + 64], ones[:, 0:HALF],
                          run[:, g % 2, 0:4, :].rearrange("p t e -> p (t e)"),
                          start=False, stop=True).then_inc(S["route"]["pe"], 1)

            def table_half(q):
                wait_for(pe, "in", "act", "keep", min(q + HOT_LAG, B - 1))
                if q:
                    pe.wait_ge(s_tadd, q)
                for t in range(4):
                    pe.wait_ge(s_hot, 8 * q + 2 * t + 2)
                    last = pe.matmul(psT[:, 0:NONE], hot_row[:, t, :], hot_col[:, t, :], start=(t == 0), stop=(t == 3))
                last.then_inc(s_tmm, 1)

            for n in range(SLOTS_A + 3):
                if n > HOT_LAG:
                    table_half(n - HOT_LAG - 1)
                if n == SLOTS_A - 1:
                    wait_for(pe, "route", "vec", "run3", B // 2 - 1)
                    pe.matmul(psX[:, 0:E], ones[:, :], run[:, (B // 2) % 2, 0, :], start=True, stop=True).then_inc(s_cntp, 1)
                for stage, do in (("out", out_out), ("qkv", lambda i: qkv_kv(i, psV, 2 * C, "v"))):
                    if 0 <= n - LAG[stage] < B:
                        do(n - LAG[stage])
                if n >= ROUTE_LAG + 2 and n % 2 == 0 and n < SLOTS_A:
                    route_rank((n - ROUTE_LAG - 2) // 2)
                for stage, lag, do in (("norm2", 1, norm2_logits), ("ctx", 0, ctx_ctx), ("soft", 0, soft_kT),
                                       ("in", 0, in_turn), ("qkv", 0, qkv_q), ("ctx", 0, ctx_proj),
                                       ("qkv", 0, lambda i: qkv_kv(i, psK, C, "kexp1")),
                                       ("norm", 0, norm_xT), ("norm2", 0, norm2_xT)):
                    if 0 <= n - LAG[stage] - lag < B:
                        do(n - LAG[stage] - lag)
            def x_turn(i, p, late):
                pe.wait_ge(s_xr[p], (i // 2 + 1) * 16 if isinstance(i, int) else late)
                if not isinstance(i, int) or i >= 1:
                    pe.wait_ge(s_xlo, i)
                for k in range(2):
                    last = pe.transpose(ps[:, 0, k * 128:(k + 1) * 128], xr[:, p, k * 128:(k + 1) * 128], ident[:, :])
                last.then_inc(s_eT, 1)

            def products(dst, hi, lo, parts, column, to_rest, width):
                for k in range(parts):
                    for n, (rows_k, rest) in enumerate(((hi, 0), (hi, to_rest), (lo, 0))):
                        last = pe.matmul(dst, rows_k[:, k * 128:(k + 1) * 128], wset[:, bass.ds(column(k) + rest, width)],
                                         start=(k == 0 and n == 0), stop=(k == parts - 1 and n == 2))
                return last

            def expert_of(i):
                return pe.value_load(tbi[0:1, 0, bass.ds(i, 1)], min_val=0, max_val=E - 1)

            def experts_of(g):
                six = pe.value_load(packedi[0:1, bass.ds(g, 1)], min_val=0, max_val=8 ** 6 - 1)
                return [(six >> (3 * n)) & (E - 1) for n in range(6)]

            def hidden(i, p, e):
                off = (e & 1) * WSET
                pe.wait_ge(s_xlo, i + 1)
                for h in range(2):
                    if not isinstance(i, int) or i >= 1:
                        pe.wait_ge(s_hb, 2 * i - 1 + h)
                    products(ps[:, 1 + h, :], xrTh[:, p, :], xrTl[:, p, :], 2,
                             lambda k: off + W1HI + k * FF + h * 512, W1LO - W1HI, 512).then_inc(s_h, 1)

            def h_turn(i, p):
                for h in range(2):
                    pe.wait_ge(s_ge, 2 * i + h + 1)
                    if not isinstance(i, int) or i >= 1:
                        pe.wait_ge(s_hlo, 2 * i - 1 + h)
                    for k in range(4):
                        last = pe.transpose(ps[:, 3 + h, k * 128:(k + 1) * 128],
                                            hb[:, p, h * 512 + k * 128:h * 512 + (k + 1) * 128], ident[:, :])
                    last.then_inc(s_hT, 1)

            def expert_out(i, p, e):
                off = (e & 1) * WSET
                pe.wait_ge(s_hlo, 2 * i + 2)
                if not isinstance(i, int) or i >= 1:
                    pe.wait_ge(s_y1, i)
                products(ps[:, 5, 0:C], hTh[:, p, :], hTl[:, p, :], 8,
                         lambda k: off + W2HI + k * C, W2LO - W2HI, C).then_inc(s_yp, 1)

            pe.wait_ge(s_tab, TAB_STEPS)

            def pe_slot(m, p, before=None, e=None, late=None):
                st = isinstance(m, int)
                if st:
                    e = expert_of(m - 1) if 0 <= m - 1 < SLOTS else None
                    before = expert_of(m - 2) if m >= 2 else None
                if not st or 0 <= m - 2 < SLOTS:
                    h_turn(m - 2, p)
                if not st or m < SLOTS:
                    x_turn(m, p, late)
                if e is not None:
                    hidden(m - 1, 1 - p, e)
                if not st or 0 <= m - 2 < SLOTS:
                    expert_out(m - 2, p, before)

            for m in range(4):
                pe_slot(m, m % 2)
            with pe.Fori(1, SLOTS // 4) as g:
                of = experts_of(g)
                for q in range(4):
                    pe_slot(4 * g + q, q % 2, of[q], of[q + 1], g * 32 + (q // 2) * 16 + 16)
            pe_slot(SLOTS, 0)
            pe_slot(SLOTS + 1, 1)

        @block.vector
        def _(dve):
            V, I = nc.vector, s_sp
            done = [0]

            def chain(ins):
                ins.then_inc(s_cst, 1)
                done[0] += 1
                dve.wait_ge(s_cst, done[0])

            def coefficients(m, parts, halves, mult=None):
                P, H = slice(0, parts), slice(0, halves)
                for h in range(halves):
                    chain(V.bn_aggr(bmv[P, h, :], bst[P, h, :, :].rearrange("p c s -> p (c s)")))
                mean, var = bmv[P, H, 0], bmv[P, H, 1]
                v, y, t, d = (bn[P, n, H] for n in range(4))
                chain(V.tensor_scalar(v, var, BN_EPS, None, ALU.add))
                chain(V.tensor_scalar(y.bitcast(I32), v.bitcast(I32), 1, -1, ALU.logical_shift_right, ALU.bitwise_xor))
                chain(V.tensor_tensor(d, mean, vecs[P, m, 0, H], ALU.add))
                chain(V.tensor_scalar(y.bitcast(I32), y.bitcast(I32), MAGIC, None, ALU.add))
                for n in range(3):
                    chain(V.tensor_tensor(t, y, y, ALU.mult))
                    chain(V.scalar_tensor_tensor(out=t, in0=t, scalar=-0.5, in1=v, op0=ALU.mult, op1=ALU.mult))
                    chain(V.scalar_tensor_tensor(out=y, in0=t, scalar=1.5, in1=y, op0=ALU.add, op1=ALU.mult))
                V.tensor_tensor(d, vecs[P, m, 0, H], d, ALU.subtract)
                chain(V.tensor_tensor(coef[P, m, 0, H], y, vecs[P, m, 1, H], ALU.mult))
                chain(V.tensor_tensor(d, d, coef[P, m, 0, H], ALU.mult))
                last = V.tensor_tensor(coef[P, m, 1, H], d, vecs[P, m, 2, H], ALU.add)
                if mult is not None:
                    chain(last)
                    last = V.tensor_scalar(coef[P, m, :, :], coef[P, m, :, :], mult, None, ALU.mult)
                last.then_inc(s_fin, 1)

            for c in range(CHUNKS):
                dve.wait_ge(s_conv, c + 1)
                chain(V.bn_stats(bst[:, 0, c, :], ps_chunk(c)))
            dve.wait_ge(s_wc, 16 * NCW)
            coefficients(0, 128, 1)
            V.scalar_tensor_tensor(out=rs[:, 1:2], in0=rs[:, 0:1], scalar=-1.0, in1=rs[:, 0:1], op0=ALU.mult,
                                   op1=ALU.max).then_inc(s_sp, 1)
            for c in range(CHUNKS):
                dve.wait_ge(s_conv, CHUNKS + c + 1)
                chain(V.bn_stats(bst[0:MID, 0, c, :], ps_chunk(c, MID)))
                if c == 0:
                    dve.wait_ge(s_sp, 2)
                    V.tensor_scalar(rs[:, 3:4], rs[:, 2:3], 1.0, None, ALU.add).then_inc(s_sp, 1)
            coefficients(1, MID, 1)
            for c in range(CHUNKS):
                for h in range(2):
                    dve.wait_ge(s_ca, 2 * CHUNKS + 2 * c + h + 1)
                    chain(V.bn_stats(bst[:, h, c, :], img[:, 2 * c:2 * c + 2, (2 + h) * HW:(3 + h) * HW]))
            dve.wait_ge(s_sp, 4)
            V.scalar_tensor_tensor(out=rs[:, 5:6], in0=rs[:, 0:1], scalar=0.0, in1=rs[:, 4:5], op0=ALU.max,
                                   op1=ALU.add).then_inc(s_sp, 1)
            dve.wait_ge(s_sp, 5)
            coefficients(2, 128, 2, rs[:, 5:6])
            dve.wait_ge(s_fin, 3)
            dve.wait_ge(s_const, NCONST)

            roots = [iter(())]

            def in_mix(i):
                p = i % 2
                wait_for(dve, "in", "pe", "turn", i - 2)
                for k in range(2):
                    V.scalar_tensor_tensor(out=tc[:, p, k, :], in0=img[:, i, (2 + k) * HW:(3 + k) * HW],
                                           scalar=coef[:, 2, 0, k:k + 1], in1=img[:, i, k * HW:(k + 1) * HW],
                                           op0=ALU.mult, op1=ALU.add).then_inc(S["in"]["vec"], 1)
                    next(roots[0], None)

            def stats(stage, which, i, n):
                p = n % 2
                for j in range(2):
                    V.bn_stats(stt[:, which, p, j, :], img[0:HALF, i, j * C:(j + 1) * C]).then_inc(S[stage]["vec"], 1)
                for j in range(2):
                    wait_for(dve, stage, "vec", f"stat{j}", i)
                    V.bn_aggr(mv[:, which, p, j, :], stt[:, which, p, j, :]).then_inc(S[stage]["vec"], 1)
                wait_for(dve, stage, "vec", "agg1", i)

            def inverse_roots(n, lo, hi):
                def root(ins):
                    ins.then_inc(S["root"]["vec"], 1)
                    r[0] += 1
                W, q = slice(lo, hi), n % 2
                v, y, t, m = (sm[:, q, a, W, :] for a in range(4))
                if n >= 3:
                    wait_for(dve, "norm", "act", "norm1", min(n - 3, B - 1))
                    wait_for(dve, "norm2", "act", "norm1", n - 2 - LAG["norm2"])
                root(V.tensor_scalar(v, mv[:, W, q, :, 1], LN_EPS, None, ALU.add))
                yield
                dve.wait_ge(S["root"]["vec"], r[0])
                root(V.tensor_scalar(y.bitcast(I32), v.bitcast(I32), 1, -1, ALU.logical_shift_right, ALU.bitwise_xor))
                yield
                dve.wait_ge(S["root"]["vec"], r[0])
                root(V.tensor_scalar(y.bitcast(I32), y.bitcast(I32), MAGIC, None, ALU.add))
                for _ in range(3):
                    yield
                    dve.wait_ge(S["root"]["vec"], r[0])
                    root(V.tensor_tensor(t, y, y, ALU.mult))
                    yield
                    dve.wait_ge(S["root"]["vec"], r[0])
                    root(V.scalar_tensor_tensor(out=t, in0=t, scalar=-0.5, in1=v, op0=ALU.mult, op1=ALU.mult))
                    yield
                    dve.wait_ge(S["root"]["vec"], r[0])
                    root(V.scalar_tensor_tensor(out=y, in0=t, scalar=1.5, in1=y, op0=ALU.add, op1=ALU.mult))
                yield
                dve.wait_ge(S["root"]["vec"], r[0])
                root(V.scalar_tensor_tensor(out=m, in0=mv[:, W, q, :, 0], scalar=-1.0, in1=y,
                                            op0=ALU.mult, op1=ALU.mult))

            def soft_maxes(i):
                p = i % 2
                wait_for(dve, "qkv", "pe", "k", i)
                V.tensor_reduce(kx[:, p, 0, :], psK[:, 0:CW].rearrange("p (h n) -> p h n", h=2), X,
                                ALU.max).then_inc(S["soft"]["vec"], 1)
                next(roots[0], None)
                wait_for(dve, "soft", "vec", "kmax", i)
                V.tensor_scalar(kx[:, p, 1, :], kx[:, p, 0, :], -1.0, None, ALU.mult).then_inc(S["soft"]["vec"], 1)
                next(roots[0], None)
                q = psQ[0:HALF, :].rearrange("p (g d) -> p g d", d=DH)
                V.tensor_reduce(qr[:, p, 0, :], q, X, ALU.max).then_inc(S["soft"]["vec"], 1)
                next(roots[0], None)
                wait_for(dve, "soft", "vec", "qmax", i)
                wait_for(dve, "soft", "pool", "q", i - 2)
                V.tensor_tensor(qe[:, p, :].rearrange("p (g d) -> p g d", d=DH), q,
                                qr[:, p, 0, :].unsqueeze(2).to_broadcast([HALF, 2 * HEADS, DH]),
                                ALU.subtract).then_inc(S["soft"]["vec"], 1)
                next(roots[0], None)

            def soft_sums(i):
                p = i % 2
                wait_for(dve, "soft", "act", "qexp", i)
                V.tensor_reduce(qr[:, p, 1, :], qe[:, p, :].rearrange("p (g d) -> p g d", d=DH), X,
                                ALU.add).then_inc(S["soft"]["vec"], 1)
                next(roots[0], None)
                wait_for(dve, "soft", "vec", "qsum", i)
                V.reciprocal(qr[:, p, 2, :], qr[:, p, 1, :]).then_inc(S["soft"]["vec"], 1)
                next(roots[0], None)
                V.reciprocal(kx[:, p, 3, :], kx[:, p, 2, :]).then_inc(S["soft"]["vec"], 1)

            def ctx_ctx(i):
                p = i % 2
                wait_for(dve, "soft", "vec", "krec", i)
                wait_for(dve, "ctx", "pe", "ctx", i)
                for h in range(2):
                    V.scalar_tensor_tensor(out=cT[:, p, h, :], in0=psC[:, h * 128:(h + 1) * 128],
                                           scalar=kx[:, p, 3, h:h + 1], in1=heads[:, :],
                                           op0=ALU.mult, op1=ALU.mult).then_inc(S["ctx"]["vec"], 1)

            def out_add(i):
                wait_for(dve, "out", "pe", "out", i)
                wait_for(dve, "norm", "pool", "bias", i)
                V.tensor_tensor(img[0:HALF, i, 0:2 * C], psC[0:HALF, :], img[0:HALF, i, 0:2 * C],
                                ALU.add).then_inc(S["out"]["vec"], 1)

            done_r, r = [0], [0]

            def to(ins, wait=True):
                ins.then_inc(S["route"]["vec"], 1)
                done_r[0] += 1
                next(roots[0], None)
                if wait:
                    dve.wait_ge(S["route"]["vec"], done_r[0])

            def over(v, k=E):
                return v.unsqueeze(2).to_broadcast([HALF, 4, k])

            L, one1, one2, both, comb, pos = (rt[:, n] for n in (0, 2, 3, 4, 5, 6))

            def route_choose(g):
                v = rv[:, g % 2]
                wait_for(dve, "norm2", "pe", "logits", 2 * g + 1)
                to(V.tensor_tensor(L, psL[0:HALF, CW:CW + 32].rearrange("p (t e) -> p t e", e=E), gb[:, :, :], ALU.add))
                to(V.tensor_reduce(v[:, 0, :], L, X, ALU.max))
                to(V.tensor_tensor(L, L, over(v[:, 0, :]), ALU.subtract))

            def route_top(g):
                v = rv[:, g % 2]
                wait_for(dve, "route", "act", "exp", g)
                to(V.tensor_reduce(v[:, 1, :], L, X, ALU.add))
                to(V.reciprocal(v[:, 2, :], v[:, 1, :]))
                to(V.tensor_tensor(L, L, over(v[:, 2, :]), ALU.mult))
                for t in range(4):
                    to(V.max(top[:, t, :], L[:, t, :]), t == 3)
                for t in range(4):
                    to(V.max_index(topi[:, t, :], top[:, t, :], L[:, t, :]), t == 3)
                to(V.tensor_copy(topf[:, :, :], topi[:, :, 0:2]))

            def route_count(g):
                v = rv[:, g % 2]
                to(V.tensor_tensor(one1, expert_id[:, :, :], over(topf[:, :, 0]), ALU.is_equal), False)
                to(V.tensor_tensor(one2, expert_id[:, :, :], over(topf[:, :, 1]), ALU.is_equal))
                wait_for(dve, "route", "pe", "rank", g - 1)
                to(V.tensor_tensor(both, one1, one2, ALU.add))
                to(V.scalar_tensor_tensor(out=v[:, 3, :], in0=top[:, :, 0], scalar=1e-9, in1=top[:, :, 1],
                                          op0=ALU.add, op1=ALU.add))
                to(V.reciprocal(v[:, 4, :], v[:, 3, :]))
                to(V.tensor_tensor(comb, L, both, ALU.mult))
                rw = rows[:, (2 * g) % RING:(2 * g) % RING + 2, :, :].rearrange("p i j r -> p (i j) r")
                to(V.tensor_tensor(rw[:, :, C:ROW], comb, over(v[:, 4, :]), ALU.mult), False)
                for t in range(4):
                    dst = run[:, g % 2, t + 1, :] if t < 3 else run[:, (g + 1) % 2, 0, :]
                    to(V.tensor_tensor(dst, run[:, g % 2, t, :], both[:, t, :], ALU.add))

            def route_slots(g):
                v = rv[:, g % 2]
                wait_for(dve, "route", "pe", "rank", g)
                wait_for(dve, "norm2", "pe", "logits", min(2 * g + 3, B - 1))
                to(V.tensor_tensor(pos, psL[0:HALF, CW + 32:CW + 64].rearrange("p (t e) -> p t e", e=E),
                                   expert_row[:, :, :], ALU.add))
                for k, one in enumerate((one1, one2)):
                    to(V.tensor_tensor(rt[:, 7 + k], pos, one, ALU.mult))
                    to(V.tensor_reduce(v[:, 5 + k, :], rt[:, 7 + k], X, ALU.add), k == 1)
                to(V.tensor_copy(slot[:, 0], v[:, 5:7, :]))
                to(V.tensor_scalar(slot[:, 1], slot[:, 0], 7, None, ALU.logical_shift_right), False)
                to(V.tensor_scalar(slot[:, 2], slot[:, 0], 127, None, ALU.bitwise_and))
                if g >= 2:
                    dve.wait_ge(s_hot, 16 * (g - 1))
                to(V.tensor_copy(place[:, g % 2], slot[:, 1:3]), False)

            def add_table(q):
                dve.wait_ge(s_tmm, q + 1)
                if q:
                    dve.wait_ge(s_tadd, q)
                V.tensor_tensor(table[:, 0:NONE], psT[:, 0:NONE], table[:, 0:NONE], ALU.add).then_inc(s_tadd, 1)

            for n in range(SLOTS_A):
                i = {stage: n - LAG[stage] for stage in LAG}
                on = {stage: 0 <= i[stage] < B for stage in LAG}
                g = (n - ROUTE_LAG) // 2
                if on["norm"]:
                    wait_for(dve, "in", "act", "keep", i["norm"])
                    stats("norm", 0, i["norm"], n)
                if on["norm2"]:
                    wait_for(dve, "out", "vec", "add", i["norm2"])
                    stats("norm2", 1, i["norm2"], n)
                roots[0] = iter(())
                if on["norm"] or on["norm2"]:
                    roots[0] = inverse_roots(n, 0 if on["norm"] else 1, 2 if on["norm2"] else 1)
                    next(roots[0])
                if on["soft"]:
                    soft_maxes(i["soft"])
                if on["out"]:
                    out_add(i["out"])
                    next(roots[0], None)
                if n > HOT_LAG:
                    add_table(n - HOT_LAG - 1)
                    next(roots[0], None)
                if on["in"]:
                    in_mix(i["in"])
                for _ in roots[0]:
                    pass
                if on["ctx"]:
                    ctx_ctx(i["ctx"])
                if n % 2 == 0 and g >= 1:
                    route_slots(g - 1)
                if n % 2 == 0 and 0 <= g < B // 2:
                    route_choose(g)
                if on["soft"]:
                    soft_sums(i["soft"])
                if n % 2 == 0 and 0 <= g < B // 2:
                    route_top(g)
                if n % 2 == 1 and 0 <= g < B // 2:
                    route_count(g)

            tab = [0]

            def link(ins):
                ins.then_inc(s_tab, 1)
                tab[0] += 1
                dve.wait_ge(s_tab, tab[0])

            dve.wait_ge(s_cntp, 1)
            link(V.tensor_scalar(cnti[:, :], psX[:, 0:E], 127.0, None, ALU.add))
            link(V.tensor_scalar(cnti[:, :], cnti[:, :], 7, None, ALU.logical_shift_right))
            link(V.tensor_scalar(ntl[:, 0, :], cnti[:, :], 1.0, None, ALU.max))
            link(V.tensor_tensor(big[:, 0, 0:E, :], lt[:, :, :], ntl[:, 0, :].unsqueeze(1).to_broadcast([128, E, E]), ALU.mult))
            link(V.tensor_reduce(ntl[:, 1, :], big[:, 0, 0:E, :], X, ALU.add))
            link(V.tensor_copy(last_tile[:, :], ntl[:, 1, :]))
            link(V.tensor_tensor(big[:, 0], iotf[:, 0:64].unsqueeze(2).to_broadcast([128, 64, E]),
                                 ntl[:, 1, :].unsqueeze(1).to_broadcast([128, 64, E]), ALU.is_ge))
            link(V.tensor_reduce(tb[:, 1, :], big[:, 0], X, ALU.add))
            link(V.tensor_tensor(big[:, 1], big[:, 0], ntl[:, 0, :].unsqueeze(1).to_broadcast([128, 64, E]), ALU.mult))
            link(V.tensor_reduce(tb[:, 2, :], big[:, 1], X, ALU.add))
            link(V.tensor_tensor(tb[:, 3, :], iotf[:, 0:64], tb[:, 2, :], ALU.subtract))
            link(V.scalar_tensor_tensor(out=tb[:, 3, :], in0=tb[:, 1, :], scalar=float(COLS), in1=tb[:, 3, :],
                                        op0=ALU.mult, op1=ALU.add))
            link(V.tensor_scalar(tbi[:, 1, :], tb[:, 3, :], float(NONE), None, ALU.min))
            link(V.tensor_scalar(tb[:, 4, :], tb[:, 1, :], float(E - 1), None, ALU.min))
            link(V.tensor_copy(tbi[:, 0, :], tb[:, 4, :]))
            link(V.tensor_copy(tb[:, 0, 2:SLOTS + 2], tb[:, 4, 0:SLOTS]))
            t5 = tb[:, 0, 0:SLOTS + 4].rearrange("p (g t) -> p g t", t=4)
            N4 = SLOTS // 4
            link(V.tensor_copy(packed[:, 0, 1:N4], t5[:, 1:N4, 0]))
            for n in range(1, 6):
                src = t5[:, 1:N4, n] if n < 4 else t5[:, 2:N4 + 1, n - 4]
                link(V.scalar_tensor_tensor(out=packed[:, n % 2, 1:N4], in0=src, scalar=float(8 ** n),
                                            in1=packed[:, (n + 1) % 2, 1:N4], op0=ALU.mult, op1=ALU.add))
            link(V.tensor_copy(packedi[:, 1:N4], packed[:, 1, 1:N4]))
            link(V.tensor_tensor(is_expert, tb[:, 4, :].unsqueeze(2).to_broadcast([128, 64, E]),
                                 iotf[:, 0:E].unsqueeze(1).to_broadcast([128, 64, E]), ALU.is_equal))
            for q in range(SLOTS_A - HOT_LAG - 1, B):
                if q >= POOL_HALVES:
                    one_hot(dve, q)
                add_table(q)

            dve.wait_ge(s_tadd, B)
            link(V.tensor_scalar(table_pad[:, :], table[:, :], 0.0, spare[:, 0:1], ALU.is_equal, ALU.mult))
            link(V.scalar_tensor_tensor(out=table_ids[:, :], in0=table_pad[:, :], scalar=-1.0, in1=table[:, :],
                                        op0=ALU.add, op1=ALU.add))
            assert tab[0] == TAB_STEPS, tab[0]

            def turned_hidden(i, p):
                for h in range(2):
                    dve.wait_ge(s_hhi, 2 * i + h + 1)
                    part = slice(h * 512, (h + 1) * 512)
                    V.tensor_tensor(hTl[:, p, part], ps[:, 3 + h, :], hTh[:, p, part].bitcast(F32),
                                    ALU.subtract).then_inc(s_hlo, 1)

            def turned(i, p, e):
                dve.wait_ge(s_w, e * LOAD_E + LOAD_E)
                dve.wait_ge(s_xhi, i + 1)
                V.tensor_tensor(xrTl[:, p, :], ps[:, 0, 0:C], xrTh[:, p, :].bitcast(F32), ALU.subtract).then_inc(s_xlo, 1)

            def expert_of(i):
                return dve.value_load(tbi[0:1, 0, bass.ds(i, 1)], min_val=0, max_val=E - 1)

            def experts_of(g):
                six = dve.value_load(packedi[0:1, bass.ds(g, 1)], min_val=0, max_val=8 ** 6 - 1)
                return [(six >> (3 * n)) & (E - 1) for n in range(6)]

            def bias_hidden(i, p, e):
                off = (e & 1) * BSET
                for h in range(2):
                    dve.wait_ge(s_h, 2 * i + h + 1)
                    V.tensor_tensor(hb[:, p, h * 512:(h + 1) * 512], ps[:, 1 + h, :],
                                    bset[:, bass.ds(off + h * 512, 512)], ALU.add).then_inc(s_hb, 1)

            def finish(i, p, e):
                off = (e & 1) * BSET
                dve.wait_ge(s_yp, i + 1)
                V.tensor_tensor(yb[:, p, :], ps[:, 5, 0:C], bset[:, bass.ds(off + FF, C)], ALU.add).then_inc(s_y1, 1)
                if not isinstance(i, int) or i >= 2:
                    dve.wait_ge(s_add, i * 16 - 16)
                dve.wait_ge(s_y1, i + 1)
                dve.wait_ge(s_meta, i + 1)
                V.tensor_scalar(ys[:, p, :], yb[:, p, :], meta[:, p:p + 1], None, ALU.mult).then_inc(s_y, 1)

            def keep_row_ends(i, p, late):
                dve.wait_ge(s_xr[p], (i // 2 + 1) * 16 if isinstance(i, int) else late)
                if not isinstance(i, int) or i >= 2:
                    dve.wait_ge(s_y, i - 1)
                if not isinstance(i, int) or i >= 1:
                    dve.wait_ge(s_meta, i)
                V.tensor_tensor(wsel[:, :], xr[:, p, C:ROW],
                                is_expert[:, bass.ds(i, 1), :].rearrange("p a e -> p (a e)"), ALU.mult).then_inc(s_ws, 1)
                dve.wait_ge(s_ws, i + 1)
                V.tensor_reduce(meta[:, p:p + 1], wsel[:, :], X, ALU.add).then_inc(s_meta, 1)

            def vec_slot(m, p, before=None, e=None, now=None, late=None):
                st = isinstance(m, int)
                if st:
                    e = expert_of(m - 1) if 0 <= m - 1 < SLOTS else None
                    before = expert_of(m - 2) if m >= 2 else None
                    now = expert_of(m) if m < SLOTS else None
                if not st or 0 <= m - 2 < SLOTS:
                    turned_hidden(m - 2, p)
                if not st or m < SLOTS:
                    turned(m, p, now)
                if e is not None:
                    bias_hidden(m - 1, 1 - p, e)
                if not st or 0 <= m - 2 < SLOTS:
                    finish(m - 2, p, before)
                if not st or m < SLOTS:
                    keep_row_ends(m, p, late)

            for m in range(4):
                vec_slot(m, m % 2)
            with dve.Fori(1, SLOTS // 4) as g:
                of = experts_of(g)
                for q in range(4):
                    vec_slot(4 * g + q, q % 2, of[q], of[q + 1], of[q + 2], g * 32 + (q // 2) * 16 + 16)
            vec_slot(SLOTS, 0)
            vec_slot(SLOTS + 1, 1)


NCONST = 29
WPARTS = 8
LOAD_E = 16 * (WPARTS + 1)
NCW = 6
MAGIC = 0x5F3759DF + 1
TAB_STEPS = 26


_NAMES = ["x", "w1t", "w2t", "w3t", "norms", "res_scale", "wqkv", "wout", "bout", "gate_w", "gate_b", "ew1", "ew2", "eb"]


def kernel(x, L0_conv_w1, L0_conv_b1, L0_conv_g1, L0_conv_be1, L0_conv_w2, L0_conv_b2, L0_conv_g2, L0_conv_be2,
           L0_conv_w3, L0_conv_b3, L0_conv_g3, L0_conv_be3, L0_conv_residual_scale, L1_attn_w_qkv, L1_attn_w_out,
           L1_attn_b_out, L1_ffn_gate_w, L1_ffn_gate_b, L1_ffn_w1, L1_ffn_b1, L1_ffn_w2, L1_ffn_b2):
    import numpy as np
    import concourse.bacc as bacc
    from concourse.bass_utils import run_bass_kernel_spmd

    vectors = [[L0_conv_b1, L0_conv_g1, L0_conv_be1], [L0_conv_b2, L0_conv_g2, L0_conv_be2],
               [L0_conv_b3, L0_conv_g3, L0_conv_be3]]
    norms = np.zeros((128, 3, 3, 2), np.float32)
    for n, v in enumerate(vectors[0]):
        norms[0:MID, 0, n, 0] = norms[MID:128, 0, n, 0] = np.asarray(v)
    for n, v in enumerate(vectors[1]):
        norms[0:MID, 1, n, 0] = np.asarray(v)
    for n, v in enumerate(vectors[2]):
        norms[:, 2, n, :] = np.asarray(v).reshape(2, 128).T
    values = [
        np.asarray(x).reshape(B, C, HW),
        np.asarray(L0_conv_w1).reshape(MID, C).T,
        np.asarray(L0_conv_w2).transpose(2, 3, 1, 0),
        np.asarray(L0_conv_w3).reshape(C, MID).T, norms,
        L0_conv_residual_scale, L1_attn_w_qkv, L1_attn_w_out, L1_attn_b_out,
        L1_ffn_gate_w, L1_ffn_gate_b, L1_ffn_w1, L1_ffn_w2,
        np.concatenate([np.asarray(L1_ffn_b1), np.asarray(L1_ffn_b2)], axis=1),
    ]
    nc = bacc.Bacc("TRN2", target_bir_lowering=False, num_devices=1)
    arrays, args = {}, []
    for name, value in zip(_NAMES, values):
        a = np.ascontiguousarray(value)
        arrays[f"in_{name}"] = a
        args.append(nc.dram_tensor(f"in_{name}", a.shape, mybir.dt.from_np(a.dtype), kind="ExternalInput").ap())
    args.append(nc.dram_tensor("out_0", (TOKENS + 128, C), F32, kind="ExternalOutput").ap())
    moe_block(nc, *args)
    r = run_bass_kernel_spmd(nc, [arrays], core_ids=[0])
    tokens = np.asarray(r.results[0]["out_0"])[:TOKENS]
    return np.ascontiguousarray(tokens.reshape(B, HW, C).transpose(0, 2, 1)).reshape(B, C, SIDE, SIDE)
```

```python
from contextlib import ExitStack

import concourse.bass as bass
from concourse import mybir

F32 = mybir.dt.float32
I32 = mybir.dt.int32
FR = mybir.dt.float32r
U32 = mybir.dt.uint32
ALU = mybir.AluOpType
ACT = mybir.ActivationFunctionType
X = mybir.AxisListType.X

B, C, HW, SIDE = 16, 256, 196, 14
TOKENS = B * HW
MID = 64
HALF = HW // 2
TILES = B * 2
CHUNKS = 8
CW = 2 * HW
HEADS, DH = 16, 16
E, FF = 8, 1024
BN_EPS = LN_EPS = 1e-5
COLS = -(-TOKENS // 128)
NONE = E * COLS
ROW = C + E
SLOTS = (2 * TOKENS - E) // 128 + E
W1HI, W1LO, W2HI, W2LO = 0, 2 * FF, 4 * FF, 6 * FF
WSET = 8 * FF
BSET = FF + C
UNITS = 2 * E
UW = 2 * FF
EARLY = 4

LAG = {"in": 0, "norm": 1, "qkv": 2, "soft": 3, "ctx": 4, "out": 5, "norm2": 6}
STEPS = {
    "in": {"vec": ["mix0", "mix1"], "act": ["relu0", "relu1", "keep"], "pe": ["turn"]},
    "norm": {"vec": ["stat0", "stat1", "agg0", "agg1"], "act": ["norm0", "norm1", "xT"], "pe": ["xT"], "pool": ["bias"]},
    "qkv": {"pe": ["v", "q", "k"]},
    "soft": {"vec": ["kmax", "kneg", "qmax", "qsub", "qsum", "qrec", "krec"],
             "act": ["v", "kexp0", "kexp1", "qexp", "kT"], "pe": ["kT"], "pool": ["q"]},
    "ctx": {"vec": ["ctx0", "ctx1"], "act": ["proj"], "pe": ["ctx", "proj"]},
    "out": {"vec": ["add"], "pe": ["out"]},
    "norm2": {"vec": ["stat0", "stat1", "agg0", "agg1"], "act": ["norm0", "norm1", "xT"], "pe": ["xT", "logits"]},
    "root": {"vec": ["eps", "seed", "guess"] + [f"newton{k}{m}" for k in range(3) for m in range(3)] + ["shift"]},
    "route": {"vec": ["bias", "max", "sub", "sum", "rec", "prob", "top0", "top1", "top2", "top3",
                      "at0", "at1", "at2", "at3", "den", "atf", "denr", "one1", "one2", "both", "run0", "comb",
                      "run1", "scale", "run2", "run3", "pos", "pos1", "pos2", "slot1", "slot2", "slots",
                      "column", "row", "places"],
              "act": ["exp"], "pe": ["rank"]},
}
ROUTE_LAG = 8
SLOTS_A = B + 9
HOT_LAG = 11
POOL_HALVES = 14
RING = 6


def after(stage, engine, name, i):
    steps = STEPS[stage][engine]
    return i * len(steps) + steps.index(name) + 1


def moe_block(nc, x, w1t, w2t, w3t, norms, res_scale, wqkv, wout, bout, gate_w, gate_b, ew1, ew2, eb, out):
    split_w = nc.dram_tensor("split_weights", [E, 128, 2, 2 * UW], F32, kind="Internal").ap()
    norm_rows = nc.dram_tensor("normalised_rows", [TOKENS + 128, ROW], F32, kind="Internal").ap()
    ctx = ExitStack()
    with ctx:
        def sb(name, shape, dt=F32):
            return ctx.enter_context(nc.sbuf_tensor(name, shape, dt))

        def sem(name):
            return ctx.enter_context(nc.semaphore(name))

        img = sb("img", [128, B, 4 * HW])
        vecs = sb("vecs", [128, 3, 3, 2])
        bst = sb("bst", [128, 2, CHUNKS, 6])
        bmv = sb("bmv", [128, 2, 2])
        bn = sb("bn", [128, 8, 2])
        rs = sb("rs", [128, 6])
        coef = sb("coef", [128, 3, 2, 2])
        wq = sb("wq", [128, 2, 3 * C])
        wo = sb("wo", [128, 2, C])
        bo2 = sb("bo2", [HALF, 2, C])
        gw = sb("gw", [128, 2, E])
        gb = sb("gb", [HALF, 4, E])
        ident = sb("ident", [128, 128])
        ones = sb("ones", [HALF, 128])
        upper = sb("upper", [HALF, HALF])
        heads = sb("heads", [128, 128])
        iotf = sb("iotf", [128, NONE])
        expert_id = sb("expert_id", [HALF, 4, E])
        expert_row = sb("expert_row", [HALF, 4, E])
        tokid_i = sb("tokid_i", [HALF, TILES], I32)
        tokid = sb("tokid", [HALF, TILES])
        xT = sb("xT", [128, 2, 2, HW])
        stt = sb("stt", [HALF, 2, 2, 2, 6])
        mv = sb("mv", [HALF, 2, 2, 2, 2])
        sm = sb("sm", [HALF, 2, 4, 2, 2])
        qr = sb("qr", [HALF, 2, 3, 2 * HEADS])
        kx = sb("kx", [128, 2, 4, 2])
        lg = sb("lg", [HALF, 2, 4, E])
        rt = sb("rt", [HALF, 12, 4, E])
        rv = sb("rv", [HALF, 2, 8, 4])
        top = sb("top", [HALF, 4, 8])
        topi = sb("topi", [HALF, 4, 8], U32)
        topf = sb("topf", [HALF, 4, 2])
        run = sb("run", [HALF, 2, 5, E])
        slot = sb("slot", [HALF, 3, 2, 4], I32)
        place = sb("place", [HALF, 2, 2, 2, 4])
        hot_row = sb("hot_row", [HALF, 4, 128], FR)
        hot_col = sb("hot_col", [HALF, 4, NONE], FR)
        table = sb("table", [128, NONE + 1])
        table_ids = sb("table_ids", [128, NONE + 1], U32)
        cnti = sb("cnti", [128, E], I32)
        ntl = sb("ntl", [128, 2, E])
        spare = sb("spare", [128, 1])
        lt = sb("lt", [128, E, E])
        big = sb("big", [128, 2, 64, E])
        iot = big[:, 0].rearrange("p a e -> p (a e)")[:, 0:NONE].bitcast(I32)
        tb = sb("tb", [128, 5, 64])
        tbi = sb("tbi", [128, 2, 64], I32)
        packed = sb("packed", [128, 2, SLOTS // 4])
        packedi = sb("packedi", [128, SLOTS // 4], I32)
        last_tile = sb("last_tile", [128, E], I32)
        is_expert = big[:, 1]
        wset = sb("wset", [128, 2 * WSET], FR)
        bset = sb("bset", [128, 2 * BSET])
        xr = sb("xr", [128, 2, ROW])
        ids = sb("ids", [128, 4, 1], U32)
        ids_add = sb("ids_add", [128, 2, 1], U32)
        wsel = sb("wsel", [128, E])
        meta = sb("meta", [128, 2])

        raw = [wset[:, a * 3 * UW:a * 3 * UW + UW].bitcast(F32) for a in range(2)]
        part_hi = [wset[:, a * 3 * UW + UW:a * 3 * UW + 2 * UW] for a in range(2)]
        part_lo = [wset[:, a * 3 * UW + 2 * UW:(a + 1) * 3 * UW] for a in range(2)]
        with ExitStack() as scope:
            def mem(name, shape, dt=F32):
                return scope.enter_context(nc.sbuf_tensor(name, shape, dt))
            pad = mem("pad", [128, B * 256], FR)
            mid2 = mem("mid2", [128, TOKENS], FR)
            relu = mem("relu", [128, 2, CW])
            w1s = mem("w1s", [128, 2, 128])
            w2s = mem("w2s", [128, 9, MID])
            w2h = mem("w2h", [128, 9, 2, MID], FR)
            w2l = mem("w2l", [128, 9, 2, MID], FR)
            w3s = mem("w3s", [128, C])
            w3h = mem("w3h", [128, C], FR)
            w3l = mem("w3l", [128, C], FR)
            padrow = scope.enter_context(nc.sbuf_tensor("padrow", [128, ROW], F32))
        with ExitStack() as scope:
            def mem(name, shape):
                return scope.enter_context(nc.sbuf_tensor(name, shape, F32))
            rows = mem("rows", [HALF, RING, 2, ROW])
            tc = mem("tc", [128, 2, 2, HW])
            xh = mem("xh", [HALF, 2, 2, C])
            qe = mem("qe", [HALF, 2, 2 * C])
            qn = mem("qn", [HALF, 2, 2 * C])
            ek = mem("ek", [128, 2, 2, HW])
            vT = mem("vT", [128, 3, 2, HW])
            ekt = mem("ekt", [HALF, 2, 2, C])
            cT = mem("cT", [128, 2, 2, 128])
            pr = mem("pr", [128, 2, 2, C])
            xT2 = mem("xT2", [128, 2, 2, HW])
        xrTh = sb("xrTh", [128, 2, C], FR)
        xrTl = sb("xrTl", [128, 2, C], FR)
        hb = sb("hb", [128, 2, FF])
        hTh = sb("hTh", [128, 2, FF], FR)
        hTl = sb("hTl", [128, 2, FF], FR)
        table_pad = sb("table_pad", [128, NONE + 1])
        yb = sb("yb", [128, 2, C])
        ys = sb("ys", [128, 2, C])

        ps = ctx.enter_context(nc.psum_tensor("ps", [128, 8, 512], F32))
        psT, psX, psQ, psK, psV = (ps[:, n, :] for n in range(5))
        psE, psC, psL = ps[:, 5, :], ps[:, 6, :], ps[:, 7, :]

        s_x = [sem(f"x_loaded{q}") for q in range(4)]
        s_w1 = sem("conv1_weights_loaded")
        s_wc = sem("conv_weights_loaded")
        s_wa = sem("attention_weights_loaded")
        s_const = sem("constants_built")
        s_conv = sem("conv_products")
        s_cst = sem("conv_stats")
        s_fin = sem("conv_coefficients")
        s_ca = sem("conv_applied")
        s_wh = sem("conv_weights_leading")
        s_wl = sem("conv_weights_rest")
        s_ph = sem("conv_input_leading")
        s_pl = sem("conv_input_rest")
        s_pp = sem("conv_input_rest_by_pool")
        s_sp = sem("softplus_steps")
        S = {st: {en: sem(f"{st}_steps_of_{en}") for en in STEPS[st]} for st in STEPS}
        s_rows = [sem(f"normalised_rows_written{a}") for a in range(RING // 2)]
        s_hrow = sem("one_hot_rows")
        s_hcol = sem("one_hot_columns")
        s_tmm = sem("table_products")
        s_tadd = sem("table_added")
        s_ids = sem("row_numbers_picked")
        s_kept = sem("row_numbers_kept")
        s_res = sem("residual_written")
        s_padw = sem("padding_written")
        s_cntp = sem("counts_summed")
        s_tab = sem("table_steps")
        s_raw = [sem(f"matrix_loaded{a}") for a in range(2)]
        s_hi = sem("leading_part_made")
        s_lo = sem("rest_made")
        s_split = [sem(f"matrix_split{a}") for a in range(2)]
        s_w = sem("expert_weights_loaded")
        s_xr = [sem(f"rows_loaded{p}") for p in range(2)]
        s_ws = sem("weight_picked")
        s_meta = sem("row_ends_kept")
        s_eT = sem("rows_turned")
        s_xhi = sem("turned_rows_leading")
        s_xlo = sem("turned_rows_rest")
        s_h = sem("hidden_products")
        s_hb = sem("hidden_biased")
        s_ge = sem("hidden_activated")
        s_hT = sem("hidden_turned")
        s_hhi = sem("turned_hidden_leading")
        s_hlo = sem("turned_hidden_rest")
        s_yp = sem("expert_products")
        s_y1 = sem("expert_biased")
        s_y = sem("expert_rows_ready")
        s_add = sem("rows_added")
        s_go = sem("adding_may_start")

        ps_chunk = lambda c, n=128: ps[0:n, c, 0:CW]
        block = ctx.enter_context(nc.Block())

        def wait_for(eng, stage, engine, name, i):
            if i >= 0:
                eng.wait_ge(S[stage][engine], after(stage, engine, name, i))


        def hot_rows(eng, q, between=None):
            g, k = q // 2, q % 2
            wait_for(eng, "route", "vec", "places", g)
            if q:
                eng.wait_ge(s_tmm, q)
            for t in range(4):
                eng.tensor_scalar(hot_row[:, t, :], iotf[0:HALF, 0:128], place[:, g % 2, 1, k, t:t + 1], None,
                                  ALU.is_equal).then_inc(s_hrow, 1)
                if between:
                    between()

        def hot_cols(eng, q, between=None):
            g, k = q // 2, q % 2
            wait_for(eng, "route", "vec", "places", g)
            if q:
                eng.wait_ge(s_tmm, q)
            for t in range(4):
                eng.tensor_scalar(hot_col[:, t, :], iotf[0:HALF, :], place[:, g % 2, 0, k, t:t + 1],
                                  tokid[:, 4 * g + t:4 * g + t + 1], ALU.is_equal, ALU.mult).then_inc(s_hcol, 1)
                if between:
                    between()

        @block.sync
        def _(sp):
            for q in range(4):
                for k in range(2):
                    sp.dma_start(img[:, 4 * q:4 * q + 4, k * HW:(k + 1) * HW],
                                 x[4 * q:4 * q + 4, k * 128:(k + 1) * 128, :].rearrange("b p n -> p b n")
                                 ).then_inc(s_x[q], 16)
                if q == 0:
                    for m in range(2):
                        sp.dma_start(w1s[:, :, m * MID:(m + 1) * MID],
                                     w1t.rearrange("(k p) m -> p k m", p=128)).then_inc(s_w1, 16)
            sp.dma_start(vecs[:, :, :, :], norms).then_inc(s_wc, 16)
            for h in range(2):
                part = slice(h * MID, (h + 1) * MID)
                sp.dma_start(w2s[part, :, :], w2t.rearrange("y x i o -> i (y x) o")).then_inc(s_wc, 16)
                sp.dma_start(w3s[part, :], w3t).then_inc(s_wc, 16)
            sp.dma_start(rs[:, 0:1], res_scale.rearrange("(a b) -> a b", a=1).to_broadcast([128, 1])).then_inc(s_wc, 16)

            def load_matrix(u):
                if u >= 2:
                    sp.wait_ge(s_lo, u - 1)
                src = ew1[u // 2] if u % 2 == 0 else ew2[u // 2]
                sp.dma_start(raw[u % 2].rearrange("p (k f) -> p k f", k=2 if u % 2 == 0 else 8),
                             src.rearrange("(k p) f -> p k f", p=128)).then_inc(s_raw[u % 2], 16)

            def store_parts(u):
                sp.wait_ge(s_hi, u + 1)
                sp.wait_ge(s_lo, u + 1)
                sp.dma_start(split_w[u // 2, :, u % 2, :],
                             wset[:, (u % 2) * 3 * UW + UW:(u % 2 + 1) * 3 * UW].bitcast(F32)).then_inc(s_split[u % 2], 16)

            load_matrix(0)
            load_matrix(1)
            sp.dma_start(wq[:, :, :], wqkv.rearrange("(k p) n -> p k n", p=128)).then_inc(s_wa, 16)
            sp.dma_start(wo[:, :, :], wout.rearrange("(k p) n -> p k n", p=128)).then_inc(s_wa, 16)
            sp.dma_start(gw[:, :, :], gate_w.rearrange("(k p) n -> p k n", p=128)).then_inc(s_wa, 16)
            for j in range(2):
                sp.dma_start(bo2[:, j, :], bout.rearrange("(a n) -> a n", a=1).to_broadcast([HALF, C])).then_inc(s_wa, 16)
            for j in range(4):
                sp.dma_start(gb[:, j, :], gate_b.rearrange("(a n) -> a n", a=1).to_broadcast([HALF, E])).then_inc(s_wa, 16)

            def load_part(e, n):
                p, w = e % 2, WSET // WPARTS
                if n or e:
                    sp.wait_ge(s_w, LOAD_E * e + 16 * n)
                if n < WPARTS:
                    sp.dma_start(wset[:, p * WSET + n * w:p * WSET + (n + 1) * w].bitcast(F32),
                                 split_w[e].rearrange("p m n -> p (m n)")[:, n * w:(n + 1) * w]).then_inc(s_w, 16)
                else:
                    sp.dma_start(bset[:, p * BSET:(p + 1) * BSET],
                                 eb[e:e + 1, :].to_broadcast([128, BSET])).then_inc(s_w, 16)

            def load_expert(e):
                for n in range(WPARTS + 1):
                    load_part(e, n)

            sp.wait_ge(s_const, NCONST)
            sp.dma_start(norm_rows[TOKENS:TOKENS + 128, :], padrow[:, :]).then_inc(s_padw, 16)
            sp.dma_start(out[TOKENS:TOKENS + 128, :], padrow[:, 0:C]).then_inc(s_padw, 16)

            def split_step(u):
                store_parts(u)
                if u + 2 < UNITS:
                    load_matrix(u + 2)

            for u in range(EARLY):
                split_step(u)
            for n in range(SLOTS_A):
                if n + EARLY < UNITS:
                    split_step(n + EARLY)
                i = n - LAG["out"]
                if 0 <= i < B:
                    wait_for(sp, "out", "vec", "add", i)
                    sp.dma_start(out[i * HW:(i + 1) * HW, :].rearrange("(j p) d -> p j d", p=HALF),
                                 img[0:HALF, i, 0:2 * C].rearrange("p (j d) -> p j d", j=2)).then_inc(s_res, 16)
                if n > ROUTE_LAG and n % 2:
                    g = (n - ROUTE_LAG) // 2
                    wait_for(sp, "route", "vec", "scale", g)
                    wait_for(sp, "norm2", "act", "norm1", 2 * g + 1)
                    at = (2 * g) % RING
                    sp.dma_start(norm_rows[2 * g * HW:(2 * g + 2) * HW, :].rearrange("(j p) d -> p j d", p=HALF),
                                 rows[:, at:at + 2, :, :].rearrange("p i j d -> p (i j) d")
                                 ).then_inc(s_rows[g % (RING // 2)], 16)
                if n == UNITS - EARLY:
                    for a in range(2):
                        sp.wait_ge(s_split[a], 16 * UNITS // 2)
                if UNITS - EARLY <= n <= UNITS - EARLY + WPARTS:
                    load_part(0, n - UNITS + EARLY)
            load_expert(1)
            sp.wait_ge(s_tab, TAB_STEPS)
            ends = [sp.value_load(last_tile[0:1, e - 2:e - 1], min_val=1, max_val=SLOTS) for e in range(2, E)]
            for e in range(2, E):
                sp.wait_ge(s_y1, ends[e - 2])
                load_expert(e)

        @block.gpsimd
        def _(pool):
            count = [0]

            def built(ins):
                ins.then_inc(s_const, 1)
                count[0] += 1
                pool.wait_ge(s_const, count[0])

            built(pool.memset(pad[:, :].bitcast(F32), 0.0))
            for t, v in ((ident, 0.0), (ones, 1.0), (upper, 1.0), (heads, 1.0), (padrow, 0.0)):
                built(pool.memset(t[:, :], v))
            built(pool.memset(run[:, :, :, :], 0.0))
            built(pool.memset(lt[:, :, :], 1.0))
            built(pool.iota(tokid_i[:, :], pattern=[[HALF, TILES]], base=1, channel_multiplier=1))
            built(pool.iota(iot, pattern=[[1, NONE]], base=0, channel_multiplier=0))
            built(pool.affine_select(out=ident[:, :], in_=ident[:, :], compare_op=ALU.not_equal, fill=1.0,
                                     base=0, pattern=[[-1, 128]], channel_multiplier=1))
            built(pool.affine_select(out=upper[:, :], in_=upper[:, :], compare_op=ALU.is_gt, fill=0.0,
                                     base=0, pattern=[[1, HALF]], channel_multiplier=-1))
            hv = heads[:, :].rearrange("p (h d) -> p h d", d=DH)
            built(pool.affine_select(out=hv, in_=hv, compare_op=ALU.is_ge, fill=0.0,
                                     base=0, pattern=[[-DH, 8], [0, DH]], channel_multiplier=1))
            built(pool.affine_select(out=hv, in_=hv, compare_op=ALU.is_ge, fill=0.0,
                                     base=DH - 1, pattern=[[DH, 8], [0, DH]], channel_multiplier=-1))
            built(pool.affine_select(out=lt[:, :, :], in_=lt[:, :, :], compare_op=ALU.is_ge, fill=0.0,
                                     base=0, pattern=[[1, E], [-1, E]], channel_multiplier=0))
            built(pool.iota(cnti[:, :], pattern=[[0, E]], base=TOKENS + 1, channel_multiplier=1))
            built(pool.tensor_copy(spare[:, :], cnti[:, 0:1]))
            built(pool.tensor_copy(tokid[:, :], tokid_i[:, :]))
            built(pool.tensor_copy(iotf[:, :], iot))
            built(pool.memset(table[:, :], 0.0))
            for j in range(4):
                built(pool.tensor_copy(expert_id[:, j, :], iot[0:HALF, 0:E]))
            for j in range(4):
                built(pool.tensor_scalar(expert_row[:, j, :], expert_id[:, j, :], float(128 * COLS), None, ALU.mult))
            assert count[0] == NCONST

            def split_rest(u):
                a = u % 2
                pool.wait_ge(s_hi, u + 1)
                pool.tensor_tensor(part_lo[a], raw[a], part_hi[a].bitcast(F32), ALU.subtract).then_inc(s_lo, 1)

            pool.wait_ge(s_wh, 2)
            pool.tensor_tensor(w2l[:, :, :, :], w2s[:, :, :].unsqueeze(2).to_broadcast([128, 9, 2, MID]),
                               w2h[:, :, :, :].bitcast(F32), ALU.subtract).then_inc(s_wl, 1)
            pool.tensor_tensor(w3l[:, :], w3s[:, :], w3h[:, :].bitcast(F32), ALU.subtract).then_inc(s_wl, 1)
            for u in range(2):
                split_rest(u)
            pool.wait_ge(s_lo, 2)
            for c in range(1, CHUNKS, 2):
                pool.wait_ge(s_ph, CHUNKS + c + 1)
                pool.wait_ge(s_ca, CHUNKS + c + 1)
                at = mid2[MID:128, c * CW:(c + 1) * CW]
                pool.tensor_tensor(at, relu[MID:128, c % 2, :], at.bitcast(F32), ALU.subtract).then_inc(s_pp, 1)
            pool.wait_ge(s_pp, CHUNKS // 2)
            for u in range(2, EARLY):
                split_rest(u)

            def norm_bias(i):
                wait_for(pool, "norm", "act", "norm1", i)
                t = img[0:HALF, i, 0:2 * C]
                pool.tensor_tensor(t, t, bo2[:, :, :].rearrange("p j d -> p (j d)"), ALU.add).then_inc(S["norm"]["pool"], 1)

            def soft_q(i):
                p = i % 2
                wait_for(pool, "soft", "vec", "qrec", i)
                wait_for(pool, "ctx", "pe", "ctx", i - 2)
                pool.tensor_tensor(qn[:, p, :].rearrange("p (g d) -> p g d", d=DH),
                                   qe[:, p, :].rearrange("p (g d) -> p g d", d=DH),
                                   qr[:, p, 2, :].unsqueeze(2).to_broadcast([HALF, 2 * HEADS, DH]),
                                   ALU.mult).then_inc(S["soft"]["pool"], 1)

            pool.wait_ge(s_wa, 9 * 16)
            for n in range(SLOTS_A):
                if 0 <= n - HOT_LAG < POOL_HALVES:
                    hot_cols(pool, n - HOT_LAG)
                if 0 <= n - LAG["norm"] < B:
                    norm_bias(n - LAG["norm"])
                if 0 <= n - LAG["soft"] < B:
                    soft_q(n - LAG["soft"])
                if n + EARLY < UNITS:
                    split_rest(n + EARLY)
            pool.wait_ge(s_res, 16 * B)
            for a in range(RING // 2):
                pool.wait_ge(s_rows[a], 16 * len(range(a, B // 2, RING // 2)))
            pool.wait_ge(s_padw, 32)

            def gather(i, r):
                pool.wait_ge(s_ids, i + 1)
                if not isinstance(i, int) or i >= 2:
                    pool.wait_ge(s_meta, i - 1)
                    pool.wait_ge(s_eT, i - 1)
                    pool.sem_inc(s_go, 1)
                pool.indirect_dma_start(xr[:, r % 2, :], None, norm_rows,
                                        bass.IndirectOffsetOnAxis(ids[:, r % 4, :], 0)).then_inc(s_xr[r % 2], 16)

            def add_rows(i, r):
                pool.wait_ge(s_y, i + 1)
                pool.wait_ge(s_kept, i + 1)
                if not isinstance(i, int) or i >= 1:
                    pool.wait_ge(s_add, i * 16)
                pool.sem_inc(s_go, 1)
                pool.indirect_dma_start(out, bass.IndirectOffsetOnAxis(ids_add[:, r % 2, :], 0), ys[:, r % 2, :], None,
                                        compute_op=ALU.add).then_inc(s_add, 16)

            def pool_slot(m, r):
                if not isinstance(m, int) or m + 1 < SLOTS:
                    gather(m + 1, r + 1)
                if not isinstance(m, int) or 0 <= m - 2 < SLOTS:
                    add_rows(m - 2, r + 2)

            gather(0, 0)
            for m in range(4):
                pool_slot(m, m)
            with pool.Fori(0, SLOTS // 8 - 1) as g:
                for r in range(8):
                    pool_slot(8 * g + 4 + r, r)
            for m in range(SLOTS - 4, SLOTS + 2):
                pool_slot(m, m % 4)
            pool.wait_ge(s_add, 16 * SLOTS)

        @block.scalar
        def _(act):
            def split_leading(u):
                a = u % 2
                act.wait_ge(s_raw[a], 16 * (u // 2 + 1))
                if u >= 2:
                    act.wait_ge(s_split[a], 16 * (u // 2))
                act.copy(part_hi[a], raw[a]).then_inc(s_hi, 1)

            act.wait_ge(s_wc, 16 * NCW)
            act.copy(w2h[:, :, :, :], w2s[:, :, :].unsqueeze(2).to_broadcast([128, 9, 2, MID])).then_inc(s_wh, 1)
            act.copy(w3h[:, :], w3s[:, :]).then_inc(s_wh, 1)
            for u in range(2):
                split_leading(u)

            def apply(layer, c):
                if layer == 0 and c >= 2:
                    act.wait_ge(s_pl, c - 1)
                elif layer == 1 and c < 2:
                    act.wait_ge(s_pl, CHUNKS - 1 + c)
                elif layer == 1 and c % 2:
                    act.wait_ge(s_pp, c // 2)
                elif layer == 1:
                    act.wait_ge(s_pl, CHUNKS + c // 2)
                act.activation(relu[:, c % 2, :], ps_chunk(c), ACT.Relu, bias=coef[:, layer, 1, 0:1],
                               scale=coef[:, layer, 0, 0:1]).then_inc(s_ca, 1)

            act.wait_ge(s_fin, 1)
            for c in range(CHUNKS):
                apply(0, c)
            act.wait_ge(s_sp, 1)
            act.activation(rs[:, 2:3], rs[:, 1:2], ACT.Exp, scale=-1.0).then_inc(s_sp, 1)
            act.wait_ge(s_sp, 3)
            act.activation(rs[:, 4:5], rs[:, 3:4], ACT.Ln).then_inc(s_sp, 1)
            for u in range(2, 4):
                split_leading(u)
            act.wait_ge(s_fin, 2)
            for c in range(CHUNKS):
                apply(1, c)
            for c in range(CHUNKS):
                for h in range(2):
                    act.wait_ge(s_conv, 2 * CHUNKS + 2 * c + h + 1)
                    act.copy(img[:, 2 * c:2 * c + 2, (2 + h) * HW:(3 + h) * HW],
                             ps_chunk((2 * c + h) % 8).rearrange("p (b n) -> p b n", b=2)).then_inc(s_ca, 1)

            def in_relu(i):
                p = i % 2
                for k in range(2):
                    wait_for(act, "in", "vec", f"mix{k}", i)
                    act.activation(tc[:, p, k, :], tc[:, p, k, :], ACT.Relu,
                                   bias=coef[:, 2, 1, k:k + 1]).then_inc(S["in"]["act"], 1)

            def in_keep(i):
                wait_for(act, "in", "pe", "turn", i)
                act.copy(img[0:HALF, i, 0:2 * C], psT[0:HALF, :]).then_inc(S["in"]["act"], 1)

            def normalise(stage, which, i, n, out):
                act.wait_ge(S["root"]["vec"], n * len(STEPS["root"]["vec"]))
                for j in range(2):
                    act.activation(out[j], img[0:HALF, i, j * C:(j + 1) * C], ACT.Identity,
                                   scale=sm[:, n % 2, 1, which, j:j + 1],
                                   bias=sm[:, n % 2, 3, which, j:j + 1]).then_inc(S[stage]["act"], 1)

            def norm_norm(i, n):
                wait_for(act, "norm", "pe", "xT", i - 2)
                normalise("norm", 0, i, n, [xh[:, i % 2, j, :] for j in range(2)])

            def norm2_norm(i, n):
                if i >= RING:
                    g = (i - RING) // 2
                    act.wait_ge(s_rows[g % (RING // 2)], 16 * (g // (RING // 2) + 1))
                normalise("norm2", 1, i, n, [rows[:, i % RING, j, 0:C] for j in range(2)])

            def norm_xT(i):
                wait_for(act, "norm", "pe", "xT", i)
                wait_for(act, "qkv", "pe", "k", i - 2)
                act.copy(xT[:, i % 2, :, :].rearrange("p k n -> p (k n)"), psX[:, 0:CW]).then_inc(S["norm"]["act"], 1)

            def soft_v(i):
                wait_for(act, "qkv", "pe", "v", i)
                wait_for(act, "out", "pe", "out", i - 3)
                act.copy(vT[:, i % 3, :, :].rearrange("p k n -> p (k n)"), psV[:, 0:CW]).then_inc(S["soft"]["act"], 1)

            def soft_exps(i):
                p = i % 2
                wait_for(act, "soft", "vec", "kneg", i)
                wait_for(act, "soft", "pe", "kT", i - 2)
                for h in range(2):
                    act.activation(ek[:, p, h, :], psK[:, h * HW:(h + 1) * HW], ACT.Exp, bias=kx[:, p, 1, h:h + 1],
                                   accum_out=kx[:, p, 2, h:h + 1]).then_inc(S["soft"]["act"], 1)
                wait_for(act, "soft", "vec", "qsub", i)
                act.activation(qe[:, p, :], qe[:, p, :], ACT.Exp, scale=float(DH) ** -0.5).then_inc(S["soft"]["act"], 1)

            def soft_kT(i):
                p = i % 2
                wait_for(act, "soft", "pe", "kT", i)
                wait_for(act, "ctx", "pe", "ctx", i - 2)
                act.copy(ekt[:, p, :, :].rearrange("p j d -> p (j d)"), psE[0:HALF, :]).then_inc(S["soft"]["act"], 1)

            def ctx_proj(i):
                wait_for(act, "ctx", "pe", "proj", i)
                wait_for(act, "out", "pe", "out", i - 2)
                act.copy(pr[:, i % 2, :, :].rearrange("p k d -> p (k d)"), psE[:, :]).then_inc(S["ctx"]["act"], 1)

            def norm2_xT(i):
                wait_for(act, "norm2", "pe", "xT", i)
                wait_for(act, "norm2", "pe", "logits", i - 2)
                act.copy(xT2[:, i % 2, :, :].rearrange("p k n -> p (k n)"), psL[:, 0:CW]).then_inc(S["norm2"]["act"], 1)

            def route_exp(g):
                wait_for(act, "route", "vec", "sub", g)
                act.activation(rt[:, 0], rt[:, 0], ACT.Exp).then_inc(S["route"]["act"], 1)

            for n in range(SLOTS_A):
                for stage, do in (("soft", soft_v), ("soft", soft_exps), ("in", in_relu),
                                  ("soft", soft_kT), ("norm2", lambda i: norm2_norm(i, n)),
                                  ("norm", lambda i: norm_norm(i, n)), ("in", in_keep), ("ctx", ctx_proj)):
                    if 0 <= n - LAG[stage] < B:
                        do(n - LAG[stage])
                if n >= ROUTE_LAG and n % 2 == 0 and (n - ROUTE_LAG) // 2 < B // 2:
                    route_exp((n - ROUTE_LAG) // 2)
                if n + EARLY < UNITS:
                    split_leading(n + EARLY)
                for stage, do in (("norm", norm_xT), ("norm2", norm2_xT)):
                    if 0 <= n - LAG[stage] < B:
                        do(n - LAG[stage])

            act.activation(rs[:, 2:3], rs[:, 1:2], ACT.Gelu)
            act.wait_ge(s_tab, TAB_STEPS)

            def pick_ids(i, r):
                column = act.value_load(tbi[0:1, 1, bass.ds(i, 1)], min_val=0, max_val=NONE)
                act.copy(ids[:, r % 4, :], table_ids[:, bass.ds(column, 1)]).then_inc(s_ids, 1)

            def keep_ids(i, r):
                act.wait_ge(s_ids, i + 1)
                if not isinstance(i, int) or i >= 2:
                    act.wait_ge(s_add, 16 * i - 16)
                act.copy(ids_add[:, r % 2, :], ids[:, r % 4, :]).then_inc(s_kept, 1)

            def turned(i, p):
                act.wait_ge(s_eT, i + 1)
                act.copy(xrTh[:, p, :], ps[:, 0, 0:C]).then_inc(s_xhi, 1)

            def gelu(i, p):
                for h in range(2):
                    act.wait_ge(s_hb, 2 * i + h + 1)
                    act.activation(hb[:, p, h * 512:(h + 1) * 512], hb[:, p, h * 512:(h + 1) * 512],
                                   ACT.Gelu).then_inc(s_ge, 1)

            def turned_hidden(i, p):
                for h in range(2):
                    act.wait_ge(s_hT, 2 * i + h + 1)
                    act.copy(hTh[:, p, h * 512:(h + 1) * 512], ps[:, 3 + h, :]).then_inc(s_hhi, 1)

            def act_slot(m, r):
                st = isinstance(m, int)
                p = r % 2
                if not st or 0 <= m - 2 < SLOTS:
                    turned_hidden(m - 2, p)
                if not st or m < SLOTS:
                    turned(m, p)
                if not st or m + 2 < SLOTS:
                    if not st or m >= 2:
                        act.wait_ge(s_kept, m - 1)
                    pick_ids(m + 2, r + 2)
                if not st or 0 <= m - 1 < SLOTS:
                    gelu(m - 1, 1 - p)
                    keep_ids(m - 1, r + 3)

            pick_ids(0, 0)
            pick_ids(1, 1)
            for m in range(4):
                act_slot(m, m)
            with act.Fori(0, SLOTS // 8 - 1) as g:
                for r in range(8):
                    act_slot(8 * g + 4 + r, r)
            for m in range(SLOTS - 4, SLOTS + 2):
                act_slot(m, m % 4)

        @block.tensor
        def _(pe):
            pe.wait_ge(s_w1, 32)
            for c in range(CHUNKS):
                if c % 2 == 0:
                    pe.wait_ge(s_x[c // 2], 32)
                for k in range(2):
                    last = pe.matmul(ps_chunk(c), w1s[:, k, :], img[:, 2 * c:2 * c + 2, k * HW:(k + 1) * HW],
                                     start=(k == 0), stop=(k == 1))
                last.then_inc(s_conv, 1)
            pv = pad[:, :].rearrange("p (b r c) -> p b r c", b=B, c=16)
            pe.wait_ge(s_wl, 2)
            for c in range(CHUNKS):
                pe.wait_ge(s_pl, c + 1)
                for t in range(9):
                    r, d = t // 3, t % 3
                    for n, w in enumerate((w2h, w2l)):
                        last = pe.matmul(ps_chunk(c), w[:, t, :, :].rearrange("p a o -> p (a o)"),
                                         pv[:, 2 * c:2 * c + 2, r:r + SIDE, d:d + SIDE],
                                         start=(t == 0 and n == 0), stop=(t == 8 and n == 1))
                last.then_inc(s_conv, 1)
            for c in range(CHUNKS):
                for h in range(2):
                    n = 2 * c + h
                    pe.wait_ge(s_ca, CHUNKS + n + 1 if n < 8 else 2 * CHUNKS + n - 7)
                    if c % 2:
                        pe.wait_ge(s_pp, c // 2 + 1)
                    else:
                        pe.wait_ge(s_pl, CHUNKS + c // 2 + 1)
                    for k, w in enumerate((w3h, w3l)):
                        last = pe.matmul(ps_chunk(n % 8), w[:, h * 128:(h + 1) * 128], mid2[:, c * CW:(c + 1) * CW],
                                         start=(k == 0), stop=(k == 1))
                    last.then_inc(s_conv, 1)
            pe.wait_ge(s_wa, 9 * 16)
            pe.wait_ge(s_const, NCONST)
            pe.wait_ge(s_ca, 4 * CHUNKS)

            def in_turn(i):
                p = i % 2
                wait_for(pe, "in", "act", "relu1", i)
                wait_for(pe, "in", "act", "keep", i - 1)
                if i > HOT_LAG:
                    pe.wait_ge(s_tadd, i - HOT_LAG)
                for j in range(2):
                    for k in range(2):
                        last = pe.transpose(psT[0:HALF, j * C + k * 128:j * C + (k + 1) * 128],
                                            tc[:, p, k, j * HALF:(j + 1) * HALF], ident[:, :])
                last.then_inc(S["in"]["pe"], 1)

            def norm_xT(i):
                p = i % 2
                wait_for(pe, "norm", "act", "norm1", i)
                wait_for(pe, "norm", "act", "xT", i - 1)
                for k in range(2):
                    for j in range(2):
                        last = pe.transpose(psX[:, k * HW + j * HALF:k * HW + (j + 1) * HALF],
                                            xh[:, p, j, k * 128:(k + 1) * 128], ident[0:HALF, 0:HALF])
                last.then_inc(S["norm"]["pe"], 1)

            def qkv_q(i):
                p = i % 2
                wait_for(pe, "norm", "act", "xT", i)
                wait_for(pe, "soft", "vec", "qsub", i - 1)
                for j in range(2):
                    for k in range(2):
                        last = pe.matmul(psQ[0:HALF, j * C:(j + 1) * C], xT[:, p, k, j * HALF:(j + 1) * HALF],
                                         wq[:, k, 0:C], start=(k == 0), stop=(k == 1))
                last.then_inc(S["qkv"]["pe"], 1)

            def qkv_kv(i, dst, off, free):
                p = i % 2
                wait_for(pe, "norm", "act", "xT", i)
                wait_for(pe, "soft", "act", free, i - 1)
                for h in range(2):
                    for k in range(2):
                        last = pe.matmul(dst[:, h * HW:(h + 1) * HW], wq[:, k, off + h * 128:off + (h + 1) * 128],
                                         xT[:, p, k, :], start=(k == 0), stop=(k == 1))
                last.then_inc(S["qkv"]["pe"], 1)

            def soft_kT(i):
                p = i % 2
                wait_for(pe, "soft", "act", "kexp1", i)
                wait_for(pe, "ctx", "act", "proj", i - 2)
                for j in range(2):
                    for h in range(2):
                        last = pe.transpose(psE[0:HALF, j * C + h * 128:j * C + (h + 1) * 128],
                                            ek[:, p, h, j * HALF:(j + 1) * HALF], ident[:, :])
                last.then_inc(S["soft"]["pe"], 1)

            def ctx_ctx(i):
                p = i % 2
                wait_for(pe, "soft", "act", "kT", i)
                wait_for(pe, "soft", "pool", "q", i)
                wait_for(pe, "out", "vec", "add", i - 1)
                for h in range(2):
                    for j in range(2):
                        last = pe.matmul(psC[:, h * 128:(h + 1) * 128], ekt[:, p, j, h * 128:(h + 1) * 128],
                                         qn[:, p, j * C + h * 128:j * C + (h + 1) * 128], start=(j == 0), stop=(j == 1))
                last.then_inc(S["ctx"]["pe"], 1)

            def ctx_proj(i):
                p = i % 2
                wait_for(pe, "ctx", "vec", "ctx1", i)
                wait_for(pe, "soft", "act", "kT", min(i + 1, B - 1))
                for h in range(2):
                    last = pe.matmul(psE[:, h * C:(h + 1) * C], cT[:, p, h, :], wo[:, h, :], start=True, stop=True)
                last.then_inc(S["ctx"]["pe"], 1)

            def out_out(i):
                wait_for(pe, "ctx", "act", "proj", i)
                for j in range(2):
                    for h in range(2):
                        last = pe.matmul(psC[0:HALF, j * C:(j + 1) * C], vT[:, i % 3, h, j * HALF:(j + 1) * HALF],
                                         pr[:, i % 2, h, :], start=(h == 0), stop=(h == 1))
                last.then_inc(S["out"]["pe"], 1)

            def norm2_xT(i):
                wait_for(pe, "norm2", "act", "norm1", i)
                wait_for(pe, "norm2", "act", "xT", i - 1)
                if i % 2 == 0:
                    wait_for(pe, "route", "vec", "bias", i // 2 - 1)
                for k in range(2):
                    for j in range(2):
                        last = pe.transpose(psL[:, k * HW + j * HALF:k * HW + (j + 1) * HALF],
                                            rows[:, i % RING, j, k * 128:(k + 1) * 128], ident[0:HALF, 0:HALF])
                last.then_inc(S["norm2"]["pe"], 1)

            def norm2_logits(i):
                wait_for(pe, "norm2", "act", "xT", i)
                wait_for(pe, "route", "vec", "bias", i // 2 - 1)
                for j in range(2):
                    at = CW + ((i % 2) * 2 + j) * E
                    for k in range(2):
                        last = pe.matmul(psL[0:HALF, at:at + E], xT2[:, i % 2, k, j * HALF:(j + 1) * HALF],
                                         gw[:, k, :], start=(k == 0), stop=(k == 1))
                last.then_inc(S["norm2"]["pe"], 1)

            def route_rank(g):
                wait_for(pe, "route", "vec", "run3", g)
                wait_for(pe, "norm2", "act", "xT", min(2 * g + 3, B - 1))
                pe.matmul(psL[0:HALF, CW + 32:CW + 64], upper[:, :], rt[:, 4].rearrange("p t e -> p (t e)"),
                          start=True, stop=False)
                pe.matmul(psL[0:HALF, CW + 32:CW + 64], ones[:, 0:HALF],
                          run[:, g % 2, 0:4, :].rearrange("p t e -> p (t e)"),
                          start=False, stop=True).then_inc(S["route"]["pe"], 1)

            def table_half(q):
                wait_for(pe, "in", "act", "keep", min(q + HOT_LAG, B - 1))
                if q:
                    pe.wait_ge(s_tadd, q)
                for t in range(4):
                    pe.wait_ge(s_hrow, 4 * q + t + 1)
                    pe.wait_ge(s_hcol, 4 * q + t + 1)
                    last = pe.matmul(psT[:, 0:NONE], hot_row[:, t, :], hot_col[:, t, :], start=(t == 0), stop=(t == 3))
                last.then_inc(s_tmm, 1)

            for n in range(SLOTS_A + 3):
                if n > HOT_LAG:
                    table_half(n - HOT_LAG - 1)
                if n == SLOTS_A - 1:
                    wait_for(pe, "route", "vec", "run3", B // 2 - 1)
                    pe.matmul(psX[:, 0:E], ones[:, :], run[:, (B // 2) % 2, 0, :], start=True, stop=True).then_inc(s_cntp, 1)
                for stage, do in (("out", out_out), ("qkv", lambda i: qkv_kv(i, psV, 2 * C, "v"))):
                    if 0 <= n - LAG[stage] < B:
                        do(n - LAG[stage])
                if n >= ROUTE_LAG + 2 and n % 2 == 0 and n < SLOTS_A:
                    route_rank((n - ROUTE_LAG - 2) // 2)
                for stage, lag, do in (("norm2", 1, norm2_logits), ("soft", 0, soft_kT), ("ctx", 0, ctx_ctx), ("qkv", 0, qkv_q),
                                       ("in", 0, in_turn), ("ctx", 0, ctx_proj), ("qkv", 0, lambda i: qkv_kv(i, psK, C, "kexp1")),
                                       ("norm", 0, norm_xT), ("norm2", 0, norm2_xT)):
                    if 0 <= n - LAG[stage] - lag < B:
                        do(n - LAG[stage] - lag)
            def x_turn(i, p, late):
                pe.wait_ge(s_xr[p], (i // 2 + 1) * 16 if isinstance(i, int) else late)
                if not isinstance(i, int) or i >= 1:
                    pe.wait_ge(s_xlo, i)
                for k in range(2):
                    last = pe.transpose(ps[:, 0, k * 128:(k + 1) * 128], xr[:, p, k * 128:(k + 1) * 128], ident[:, :])
                last.then_inc(s_eT, 1)

            def products(dst, hi, lo, parts, column, to_rest, width):
                for k in range(parts):
                    for n, (rows_k, rest) in enumerate(((hi, 0), (hi, to_rest), (lo, 0))):
                        last = pe.matmul(dst, rows_k[:, k * 128:(k + 1) * 128], wset[:, bass.ds(column(k) + rest, width)],
                                         start=(k == 0 and n == 0), stop=(k == parts - 1 and n == 2))
                return last

            def expert_of(i):
                return pe.value_load(tbi[0:1, 0, bass.ds(i, 1)], min_val=0, max_val=E - 1)

            def experts_of(g):
                six = pe.value_load(packedi[0:1, bass.ds(g, 1)], min_val=0, max_val=8 ** 6 - 1)
                return [(six >> (3 * n)) & (E - 1) for n in range(6)]

            def hidden(i, p, e):
                off = (e & 1) * WSET
                pe.wait_ge(s_xlo, i + 1)
                for h in range(2):
                    if not isinstance(i, int) or i >= 1:
                        pe.wait_ge(s_hb, 2 * i - 1 + h)
                    products(ps[:, 1 + h, :], xrTh[:, p, :], xrTl[:, p, :], 2,
                             lambda k: off + W1HI + k * FF + h * 512, W1LO - W1HI, 512).then_inc(s_h, 1)

            def h_turn(i, p):
                for h in range(2):
                    pe.wait_ge(s_ge, 2 * i + h + 1)
                    if not isinstance(i, int) or i >= 1:
                        pe.wait_ge(s_hlo, 2 * i - 1 + h)
                    for k in range(4):
                        last = pe.transpose(ps[:, 3 + h, k * 128:(k + 1) * 128],
                                            hb[:, p, h * 512 + k * 128:h * 512 + (k + 1) * 128], ident[:, :])
                    last.then_inc(s_hT, 1)

            def expert_out(i, p, e):
                off = (e & 1) * WSET
                pe.wait_ge(s_hlo, 2 * i + 2)
                if not isinstance(i, int) or i >= 1:
                    pe.wait_ge(s_y1, i)
                products(ps[:, 5, 0:C], hTh[:, p, :], hTl[:, p, :], 8,
                         lambda k: off + W2HI + k * C, W2LO - W2HI, C).then_inc(s_yp, 1)

            pe.wait_ge(s_tab, TAB_STEPS)

            def pe_slot(m, p, before=None, e=None, late=None):
                st = isinstance(m, int)
                if before is None:
                    e = expert_of(m - 1) if 0 <= m - 1 < SLOTS else None
                    before = expert_of(m - 2) if m >= 2 else None
                if not st or 0 <= m - 2 < SLOTS:
                    h_turn(m - 2, p)
                if not st or m < SLOTS:
                    x_turn(m, p, late)
                if e is not None:
                    hidden(m - 1, 1 - p, e)
                if not st or 0 <= m - 2 < SLOTS:
                    expert_out(m - 2, p, before)

            for m in range(4):
                pe_slot(m, m % 2)
            with pe.Fori(0, SLOTS // 8 - 1) as g:
                of = experts_of(2 * g + 1), experts_of(2 * g + 2)
                for q in range(8):
                    mine = of[q // 4]
                    pe_slot(8 * g + 4 + q, q % 2, mine[q % 4], mine[q % 4 + 1], g * 64 + (q // 2) * 16 + 48)
            of = experts_of(SLOTS // 4 - 1)
            for q in range(4):
                pe_slot(SLOTS - 4 + q, q % 2, of[q], of[q + 1])
            pe_slot(SLOTS, 0)
            pe_slot(SLOTS + 1, 1)

        @block.vector
        def _(dve):
            V, I = nc.vector, s_sp
            done = [0]

            def chain(ins):
                ins.then_inc(s_cst, 1)
                done[0] += 1
                dve.wait_ge(s_cst, done[0])

            def stat(ins):
                ins.then_inc(s_cst, 1)
                done[0] += 1

            def coefficients(m, parts, halves, mult=None):
                P, H = slice(0, parts), slice(0, halves)
                dve.wait_ge(s_cst, done[0])
                for h in range(halves):
                    chain(V.bn_aggr(bmv[P, h, :], bst[P, h, :, :].rearrange("p c s -> p (c s)")))
                mean, var = bmv[P, H, 0], bmv[P, H, 1]
                v, y, t, d = (bn[P, n, H] for n in range(4))
                chain(V.tensor_scalar(v, var, BN_EPS, None, ALU.add))
                chain(V.tensor_scalar(y.bitcast(I32), v.bitcast(I32), 1, -1, ALU.logical_shift_right, ALU.bitwise_xor))
                chain(V.tensor_tensor(d, mean, vecs[P, m, 0, H], ALU.add))
                chain(V.tensor_scalar(y.bitcast(I32), y.bitcast(I32), MAGIC, None, ALU.add))
                for n in range(3):
                    chain(V.tensor_tensor(t, y, y, ALU.mult))
                    chain(V.scalar_tensor_tensor(out=t, in0=t, scalar=-0.5, in1=v, op0=ALU.mult, op1=ALU.mult))
                    chain(V.scalar_tensor_tensor(out=y, in0=t, scalar=1.5, in1=y, op0=ALU.add, op1=ALU.mult))
                V.tensor_tensor(d, vecs[P, m, 0, H], d, ALU.subtract)
                chain(V.tensor_tensor(coef[P, m, 0, H], y, vecs[P, m, 1, H], ALU.mult))
                chain(V.tensor_tensor(d, d, coef[P, m, 0, H], ALU.mult))
                last = V.tensor_tensor(coef[P, m, 1, H], d, vecs[P, m, 2, H], ALU.add)
                if mult is not None:
                    chain(last)
                    last = V.tensor_scalar(coef[P, m, :, :], coef[P, m, :, :], mult, None, ALU.mult)
                last.then_inc(s_fin, 1)

            for c in range(CHUNKS):
                dve.wait_ge(s_conv, c + 1)
                stat(V.bn_stats(bst[:, 0, c, :], ps_chunk(c)))
            dve.wait_ge(s_wc, 16 * NCW)
            coefficients(0, 128, 1)
            pv = pad[:, :].rearrange("p (b r c) -> p b r c", b=B, c=16)
            dve.wait_ge(s_const, 1)
            for c in range(CHUNKS):
                dve.wait_ge(s_ca, c + 1)
                inside = pv[:, 2 * c:2 * c + 2, 1:15, 1:15]
                src = relu[:, c % 2, :].rearrange("p (b r c) -> p b r c", b=2, c=SIDE)
                V.tensor_copy(inside, src).then_inc(s_ph, 1)
                dve.wait_ge(s_ph, c + 1)
                V.tensor_tensor(inside[MID:128], src[MID:128], inside[MID:128].bitcast(F32),
                                ALU.subtract).then_inc(s_pl, 1)
            V.scalar_tensor_tensor(out=rs[:, 1:2], in0=rs[:, 0:1], scalar=-1.0, in1=rs[:, 0:1], op0=ALU.mult,
                                   op1=ALU.max).then_inc(s_sp, 1)
            for c in range(CHUNKS):
                dve.wait_ge(s_conv, CHUNKS + c + 1)
                stat(V.bn_stats(bst[:, 0, c, :], ps_chunk(c)))
                if c == 0:
                    dve.wait_ge(s_sp, 2)
                    V.tensor_scalar(rs[:, 3:4], rs[:, 2:3], 1.0, None, ALU.add).then_inc(s_sp, 1)
            coefficients(1, 128, 1)
            for c in range(CHUNKS):
                dve.wait_ge(s_ca, CHUNKS + c + 1)
                V.tensor_copy(mid2[:, c * CW:(c + 1) * CW], relu[:, c % 2, :]).then_inc(s_ph, 1)
                if c % 2 == 0:
                    dve.wait_ge(s_ph, CHUNKS + c + 1)
                    at = mid2[MID:128, c * CW:(c + 1) * CW]
                    V.tensor_tensor(at, relu[MID:128, c % 2, :], at.bitcast(F32), ALU.subtract).then_inc(s_pl, 1)
            for c in range(CHUNKS):
                for h in range(2):
                    dve.wait_ge(s_ca, 2 * CHUNKS + 2 * c + h + 1)
                    stat(V.bn_stats(bst[:, h, c, :], img[:, 2 * c:2 * c + 2, (2 + h) * HW:(3 + h) * HW]))
            dve.wait_ge(s_sp, 4)
            V.scalar_tensor_tensor(out=rs[:, 5:6], in0=rs[:, 0:1], scalar=0.0, in1=rs[:, 4:5], op0=ALU.max,
                                   op1=ALU.add).then_inc(s_sp, 1)
            dve.wait_ge(s_sp, 5)
            coefficients(2, 128, 2, rs[:, 5:6])
            dve.wait_ge(s_fin, 3)
            dve.wait_ge(s_const, NCONST)

            chains = [iter(()), iter(())]

            def fill():
                for one in chains:
                    next(one, None)

            def in_mix(i):
                p = i % 2
                wait_for(dve, "in", "pe", "turn", i - 2)
                for k in range(2):
                    V.scalar_tensor_tensor(out=tc[:, p, k, :], in0=img[:, i, (2 + k) * HW:(3 + k) * HW],
                                           scalar=coef[:, 2, 0, k:k + 1], in1=img[:, i, k * HW:(k + 1) * HW],
                                           op0=ALU.mult, op1=ALU.add).then_inc(S["in"]["vec"], 1)
                    fill()

            def stats(stage, which, i, n):
                p = n % 2
                for j in range(2):
                    V.bn_stats(stt[:, which, p, j, :], img[0:HALF, i, j * C:(j + 1) * C]).then_inc(S[stage]["vec"], 1)
                    fill()
                for j in range(2):
                    wait_for(dve, stage, "vec", f"stat{j}", i)
                    V.bn_aggr(mv[:, which, p, j, :], stt[:, which, p, j, :]).then_inc(S[stage]["vec"], 1)
                fill()
                wait_for(dve, stage, "vec", "agg1", i)

            def inverse_roots(n, lo, hi):
                def root(ins):
                    ins.then_inc(S["root"]["vec"], 1)
                    r[0] += 1
                W, q = slice(lo, hi), n % 2
                v, y, t, m = (sm[:, q, a, W, :] for a in range(4))
                if n >= 3:
                    wait_for(dve, "norm", "act", "norm1", min(n - 3, B - 1))
                    wait_for(dve, "norm2", "act", "norm1", n - 2 - LAG["norm2"])
                root(V.tensor_scalar(v, mv[:, W, q, :, 1], LN_EPS, None, ALU.add))
                yield
                dve.wait_ge(S["root"]["vec"], r[0])
                root(V.tensor_scalar(y.bitcast(I32), v.bitcast(I32), 1, -1, ALU.logical_shift_right, ALU.bitwise_xor))
                yield
                dve.wait_ge(S["root"]["vec"], r[0])
                root(V.tensor_scalar(y.bitcast(I32), y.bitcast(I32), MAGIC, None, ALU.add))
                for _ in range(3):
                    yield
                    dve.wait_ge(S["root"]["vec"], r[0])
                    root(V.tensor_tensor(t, y, y, ALU.mult))
                    yield
                    dve.wait_ge(S["root"]["vec"], r[0])
                    root(V.scalar_tensor_tensor(out=t, in0=t, scalar=-0.5, in1=v, op0=ALU.mult, op1=ALU.mult))
                    yield
                    dve.wait_ge(S["root"]["vec"], r[0])
                    root(V.scalar_tensor_tensor(out=y, in0=t, scalar=1.5, in1=y, op0=ALU.add, op1=ALU.mult))
                yield
                dve.wait_ge(S["root"]["vec"], r[0])
                root(V.scalar_tensor_tensor(out=m, in0=mv[:, W, q, :, 0], scalar=-1.0, in1=y,
                                            op0=ALU.mult, op1=ALU.mult))

            def soft_maxes(i):
                p = i % 2
                wait_for(dve, "qkv", "pe", "k", i)
                V.tensor_reduce(kx[:, p, 0, :], psK[:, 0:CW].rearrange("p (h n) -> p h n", h=2), X,
                                ALU.max).then_inc(S["soft"]["vec"], 1)
                fill()
                wait_for(dve, "soft", "vec", "kmax", i)
                V.tensor_scalar(kx[:, p, 1, :], kx[:, p, 0, :], -1.0, None, ALU.mult).then_inc(S["soft"]["vec"], 1)
                fill()
                q = psQ[0:HALF, :].rearrange("p (g d) -> p g d", d=DH)
                V.tensor_reduce(qr[:, p, 0, :], q, X, ALU.max).then_inc(S["soft"]["vec"], 1)
                fill()
                wait_for(dve, "soft", "vec", "qmax", i)
                wait_for(dve, "soft", "pool", "q", i - 2)
                V.tensor_tensor(qe[:, p, :].rearrange("p (g d) -> p g d", d=DH), q,
                                qr[:, p, 0, :].unsqueeze(2).to_broadcast([HALF, 2 * HEADS, DH]),
                                ALU.subtract).then_inc(S["soft"]["vec"], 1)
                fill()

            def soft_sums(i):
                p = i % 2
                wait_for(dve, "soft", "act", "qexp", i)
                V.tensor_reduce(qr[:, p, 1, :], qe[:, p, :].rearrange("p (g d) -> p g d", d=DH), X,
                                ALU.add).then_inc(S["soft"]["vec"], 1)
                fill()
                wait_for(dve, "soft", "vec", "qsum", i)
                V.reciprocal(qr[:, p, 2, :], qr[:, p, 1, :]).then_inc(S["soft"]["vec"], 1)
                fill()
                V.reciprocal(kx[:, p, 3, :], kx[:, p, 2, :]).then_inc(S["soft"]["vec"], 1)

            def ctx_ctx(i):
                p = i % 2
                wait_for(dve, "soft", "vec", "krec", i)
                wait_for(dve, "ctx", "pe", "ctx", i)
                for h in range(2):
                    V.scalar_tensor_tensor(out=cT[:, p, h, :], in0=psC[:, h * 128:(h + 1) * 128],
                                           scalar=kx[:, p, 3, h:h + 1], in1=heads[:, :],
                                           op0=ALU.mult, op1=ALU.mult).then_inc(S["ctx"]["vec"], 1)

            def out_add(i):
                wait_for(dve, "out", "pe", "out", i)
                wait_for(dve, "norm", "pool", "bias", i)
                V.tensor_tensor(img[0:HALF, i, 0:2 * C], psC[0:HALF, :], img[0:HALF, i, 0:2 * C],
                                ALU.add).then_inc(S["out"]["vec"], 1)

            r = [0]

            def over(v, k=E):
                return v.unsqueeze(2).to_broadcast([HALF, 4, k])

            L, one1, one2, both, comb, pos = (rt[:, n] for n in (0, 2, 3, 4, 5, 6))

            def step(name, g, reads=None):
                if reads is not None:
                    wait_for(dve, "route", "vec", reads, g)
                assert after("route", "vec", name, g) == done_r[0] + 1
                done_r[0] += 1
                return S["route"]["vec"], 1

            done_r = [0]

            def route_choose(g):
                v = rv[:, g % 2]
                wait_for(dve, "norm2", "pe", "logits", 2 * g + 1)
                sig = step("bias", g)
                V.tensor_tensor(L, psL[0:HALF, CW:CW + 32].rearrange("p (t e) -> p t e", e=E), gb[:, :, :],
                                ALU.add).then_inc(*sig)
                yield
                sig = step("max", g, "bias")
                V.tensor_reduce(v[:, 0, :], L, X, ALU.max).then_inc(*sig)
                yield
                sig = step("sub", g, "max")
                V.tensor_tensor(L, L, over(v[:, 0, :]), ALU.subtract).then_inc(*sig)

            def route_top(g):
                v = rv[:, g % 2]
                wait_for(dve, "route", "act", "exp", g)
                sig = step("sum", g)
                V.tensor_reduce(v[:, 1, :], L, X, ALU.add).then_inc(*sig)
                yield
                sig = step("rec", g, "sum")
                V.reciprocal(v[:, 2, :], v[:, 1, :]).then_inc(*sig)
                yield
                sig = step("prob", g, "rec")
                V.tensor_tensor(L, L, over(v[:, 2, :]), ALU.mult).then_inc(*sig)
                yield
                for t in range(4):
                    sig = step(f"top{t}", g, "prob" if t == 0 else None)
                    V.max(top[:, t, :], L[:, t, :]).then_inc(*sig)
                yield
                for t in range(4):
                    sig = step(f"at{t}", g, "top3" if t == 0 else None)
                    V.max_index(topi[:, t, :], top[:, t, :], L[:, t, :]).then_inc(*sig)
                sig = step("den", g)
                V.scalar_tensor_tensor(out=v[:, 3, :], in0=top[:, :, 0], scalar=1e-9, in1=top[:, :, 1],
                                       op0=ALU.add, op1=ALU.add).then_inc(*sig)
                yield
                sig = step("atf", g, "at3")
                V.tensor_copy(topf[:, :, :], topi[:, :, 0:2]).then_inc(*sig)
                sig = step("denr", g, "den")
                V.reciprocal(v[:, 4, :], v[:, 3, :]).then_inc(*sig)
                yield
                sig = step("one1", g, "atf")
                V.tensor_tensor(one1, expert_id[:, :, :], over(topf[:, :, 0]), ALU.is_equal).then_inc(*sig)
                sig = step("one2", g)
                V.tensor_tensor(one2, expert_id[:, :, :], over(topf[:, :, 1]), ALU.is_equal).then_inc(*sig)
                yield
                wait_for(dve, "route", "pe", "rank", g - 1)
                sig = step("both", g, "one2")
                V.tensor_tensor(both, one1, one2, ALU.add).then_inc(*sig)
                yield

                def run_step(t, reads):
                    sig = step(f"run{t}", g, reads)
                    dst = run[:, g % 2, t + 1, :] if t < 3 else run[:, (g + 1) % 2, 0, :]
                    V.tensor_tensor(dst, run[:, g % 2, t, :], both[:, t, :], ALU.add).then_inc(*sig)

                run_step(0, "both")
                sig = step("comb", g)
                V.tensor_tensor(comb, L, both, ALU.mult).then_inc(*sig)
                yield
                run_step(1, "run0")
                rw = rows[:, (2 * g) % RING:(2 * g) % RING + 2, :, :].rearrange("p i j r -> p (i j) r")
                sig = step("scale", g, "comb")
                V.tensor_tensor(rw[:, :, C:ROW], comb, over(v[:, 4, :]), ALU.mult).then_inc(*sig)
                yield
                run_step(2, "run1")
                yield
                run_step(3, "run2")

            def route_slots(g):
                v = rv[:, g % 2]
                wait_for(dve, "route", "pe", "rank", g)
                wait_for(dve, "norm2", "pe", "logits", min(2 * g + 3, B - 1))
                sig = step("pos", g)
                V.tensor_tensor(pos, psL[0:HALF, CW + 32:CW + 64].rearrange("p (t e) -> p t e", e=E),
                                expert_row[:, :, :], ALU.add).then_inc(*sig)
                yield
                for k, one in enumerate((one1, one2)):
                    sig = step(f"pos{k + 1}", g, "pos")
                    V.tensor_tensor(rt[:, 7 + k], pos, one, ALU.mult).then_inc(*sig)
                yield
                for k in range(2):
                    sig = step(f"slot{k + 1}", g, f"pos{k + 1}")
                    V.tensor_reduce(v[:, 5 + k, :], rt[:, 7 + k], X, ALU.add).then_inc(*sig)
                yield
                sig = step("slots", g, "slot2")
                V.tensor_copy(slot[:, 0], v[:, 5:7, :]).then_inc(*sig)
                yield
                sig = step("column", g, "slots")
                V.tensor_scalar(slot[:, 1], slot[:, 0], 7, None, ALU.logical_shift_right).then_inc(*sig)
                sig = step("row", g)
                V.tensor_scalar(slot[:, 2], slot[:, 0], 127, None, ALU.bitwise_and).then_inc(*sig)
                yield
                if g >= 2:
                    dve.wait_ge(s_tmm, 2 * (g - 1))
                sig = step("places", g, "row")
                V.tensor_copy(place[:, g % 2], slot[:, 1:3]).then_inc(*sig)

            def add_table(q):
                dve.wait_ge(s_tmm, q + 1)
                if q:
                    dve.wait_ge(s_tadd, q)
                V.tensor_tensor(table[:, 0:NONE], psT[:, 0:NONE], table[:, 0:NONE], ALU.add).then_inc(s_tadd, 1)

            tab = [0]

            def link(ins):
                ins.then_inc(s_tab, 1)
                tab[0] += 1

            def tile_table():
                dve.wait_ge(s_cntp, 1)
                link(V.tensor_scalar(cnti[:, :], psX[:, 0:E], 127.0, None, ALU.add))
                yield
                dve.wait_ge(s_tab, tab[0])
                link(V.tensor_scalar(cnti[:, :], cnti[:, :], 7, None, ALU.logical_shift_right))
                yield
                dve.wait_ge(s_tab, tab[0])
                link(V.tensor_scalar(ntl[:, 0, :], cnti[:, :], 1.0, None, ALU.max))
                yield
                dve.wait_ge(s_tab, tab[0])
                link(V.tensor_tensor(big[:, 0, 0:E, :], lt[:, :, :], ntl[:, 0, :].unsqueeze(1).to_broadcast([128, E, E]), ALU.mult))
                yield
                dve.wait_ge(s_tab, tab[0])
                link(V.tensor_reduce(ntl[:, 1, :], big[:, 0, 0:E, :], X, ALU.add))
                yield
                dve.wait_ge(s_tab, tab[0])
                link(V.tensor_copy(last_tile[:, :], ntl[:, 1, :]))
                yield
                dve.wait_ge(s_tab, tab[0])
                link(V.tensor_tensor(big[:, 0], iotf[:, 0:64].unsqueeze(2).to_broadcast([128, 64, E]),
                                     ntl[:, 1, :].unsqueeze(1).to_broadcast([128, 64, E]), ALU.is_ge))
                yield
                dve.wait_ge(s_tab, tab[0])
                link(V.tensor_reduce(tb[:, 1, :], big[:, 0], X, ALU.add))
                yield
                dve.wait_ge(s_tab, tab[0])
                link(V.tensor_tensor(big[:, 1], big[:, 0], ntl[:, 0, :].unsqueeze(1).to_broadcast([128, 64, E]), ALU.mult))
                yield
                dve.wait_ge(s_tab, tab[0])
                link(V.tensor_reduce(tb[:, 2, :], big[:, 1], X, ALU.add))
                yield
                dve.wait_ge(s_tab, tab[0])
                link(V.tensor_tensor(tb[:, 3, :], iotf[:, 0:64], tb[:, 2, :], ALU.subtract))
                yield
                dve.wait_ge(s_tab, tab[0])
                link(V.scalar_tensor_tensor(out=tb[:, 3, :], in0=tb[:, 1, :], scalar=float(COLS), in1=tb[:, 3, :],
                                            op0=ALU.mult, op1=ALU.add))
                yield
                dve.wait_ge(s_tab, tab[0])
                link(V.tensor_scalar(tbi[:, 1, :], tb[:, 3, :], float(NONE), None, ALU.min))
                yield
                dve.wait_ge(s_tab, tab[0])
                link(V.tensor_scalar(tb[:, 4, :], tb[:, 1, :], float(E - 1), None, ALU.min))
                yield
                dve.wait_ge(s_tab, tab[0])
                link(V.tensor_copy(tbi[:, 0, :], tb[:, 4, :]))
                yield
                dve.wait_ge(s_tab, tab[0])
                link(V.tensor_copy(tb[:, 0, 2:SLOTS + 2], tb[:, 4, 0:SLOTS]))
                yield
                dve.wait_ge(s_tab, tab[0])
                t5 = tb[:, 0, 0:SLOTS + 4].rearrange("p (g t) -> p g t", t=4)
                N4 = SLOTS // 4
                link(V.tensor_copy(packed[:, 0, 1:N4], t5[:, 1:N4, 0]))
                yield
                dve.wait_ge(s_tab, tab[0])
                for n in range(1, 6):
                    src = t5[:, 1:N4, n] if n < 4 else t5[:, 2:N4 + 1, n - 4]
                    link(V.scalar_tensor_tensor(out=packed[:, n % 2, 1:N4], in0=src, scalar=float(8 ** n),
                                                in1=packed[:, (n + 1) % 2, 1:N4], op0=ALU.mult, op1=ALU.add))
                    yield
                    dve.wait_ge(s_tab, tab[0])
                link(V.tensor_copy(packedi[:, 1:N4], packed[:, 1, 1:N4]))
                yield
                dve.wait_ge(s_tab, tab[0])
                link(V.tensor_tensor(is_expert, tb[:, 4, :].unsqueeze(2).to_broadcast([128, 64, E]),
                                     iotf[:, 0:E].unsqueeze(1).to_broadcast([128, 64, E]), ALU.is_equal))
                yield
                dve.wait_ge(s_tab, tab[0])

            for n in range(SLOTS_A):
                i = {stage: n - LAG[stage] for stage in LAG}
                on = {stage: 0 <= i[stage] < B for stage in LAG}
                g = (n - ROUTE_LAG) // 2
                pair = 0 <= g < B // 2
                if n % 2 == 1 and pair:
                    chains[1] = route_top(g)
                if on["norm"]:
                    wait_for(dve, "in", "act", "keep", i["norm"])
                    stats("norm", 0, i["norm"], n)
                if on["norm2"]:
                    wait_for(dve, "out", "vec", "add", i["norm2"])
                    stats("norm2", 1, i["norm2"], n)
                if on["norm"] or on["norm2"]:
                    chains[0] = inverse_roots(n, 0 if on["norm"] else 1, 2 if on["norm2"] else 1)
                    fill()
                if on["soft"]:
                    soft_maxes(i["soft"])
                if n > HOT_LAG:
                    add_table(n - HOT_LAG - 1)
                    fill()
                if on["out"]:
                    out_add(i["out"])
                    fill()
                if on["in"]:
                    in_mix(i["in"])
                if n % 2 == 0 and g >= 1:
                    chains[1] = route_slots(g - 1)
                for _ in chains[0]:
                    next(chains[1], None)
                if on["ctx"]:
                    ctx_ctx(i["ctx"])
                    fill()
                if n % 2 == 0 and pair:
                    for _ in chains[1]:
                        pass
                    chains[1] = route_choose(g)
                    fill()
                if on["soft"]:
                    soft_sums(i["soft"])
                if n == SLOTS_A - 1:
                    chains[0] = tile_table()
                for _ in chains[1]:
                    next(chains[0], None)
                if 0 <= n - HOT_LAG < B:
                    hot_rows(dve, n - HOT_LAG, fill)
                    if n - HOT_LAG >= POOL_HALVES:
                        hot_cols(dve, n - HOT_LAG, fill)

            for q in range(SLOTS_A - HOT_LAG - 1, B):
                if q > SLOTS_A - HOT_LAG - 1:
                    hot_rows(dve, q, fill)
                    hot_cols(dve, q, fill)
                add_table(q)
            for _ in chains[0]:
                pass

            dve.wait_ge(s_tadd, B)
            link(V.tensor_scalar(table_pad[:, :], table[:, :], 0.0, spare[:, 0:1], ALU.is_equal, ALU.mult))
            dve.wait_ge(s_tab, tab[0])
            link(V.scalar_tensor_tensor(out=table_ids[:, :], in0=table_pad[:, :], scalar=-1.0, in1=table[:, :],
                                        op0=ALU.add, op1=ALU.add))
            assert tab[0] == TAB_STEPS, tab[0]

            def turned_hidden(i, p):
                for h in range(2):
                    dve.wait_ge(s_hhi, 2 * i + h + 1)
                    part = slice(h * 512, (h + 1) * 512)
                    V.tensor_tensor(hTl[:, p, part], ps[:, 3 + h, :], hTh[:, p, part].bitcast(F32),
                                    ALU.subtract).then_inc(s_hlo, 1)

            def turned(i, p, e):
                dve.wait_ge(s_w, e * LOAD_E + LOAD_E)
                dve.wait_ge(s_xhi, i + 1)
                V.tensor_tensor(xrTl[:, p, :], ps[:, 0, 0:C], xrTh[:, p, :].bitcast(F32), ALU.subtract).then_inc(s_xlo, 1)

            def expert_of(i):
                return dve.value_load(tbi[0:1, 0, bass.ds(i, 1)], min_val=0, max_val=E - 1)

            def experts_of(g):
                six = dve.value_load(packedi[0:1, bass.ds(g, 1)], min_val=0, max_val=8 ** 6 - 1)
                return [(six >> (3 * n)) & (E - 1) for n in range(6)]

            def bias_hidden(i, p, e):
                off = (e & 1) * BSET
                for h in range(2):
                    dve.wait_ge(s_h, 2 * i + h + 1)
                    V.tensor_tensor(hb[:, p, h * 512:(h + 1) * 512], ps[:, 1 + h, :],
                                    bset[:, bass.ds(off + h * 512, 512)], ALU.add).then_inc(s_hb, 1)

            def finish(i, p, e):
                off = (e & 1) * BSET
                dve.wait_ge(s_yp, i + 1)
                V.tensor_tensor(yb[:, p, :], ps[:, 5, 0:C], bset[:, bass.ds(off + FF, C)], ALU.add).then_inc(s_y1, 1)
                if not isinstance(i, int) or i >= 2:
                    dve.wait_ge(s_add, i * 16 - 16)
                dve.wait_ge(s_y1, i + 1)
                dve.wait_ge(s_meta, i + 1)
                V.tensor_scalar(ys[:, p, :], yb[:, p, :], meta[:, p:p + 1], None, ALU.mult).then_inc(s_y, 1)

            def keep_row_ends(i, p, late):
                dve.wait_ge(s_xr[p], (i // 2 + 1) * 16 if isinstance(i, int) else late)
                if not isinstance(i, int) or i >= 2:
                    dve.wait_ge(s_y, i - 1)
                if not isinstance(i, int) or i >= 1:
                    dve.wait_ge(s_meta, i)
                V.tensor_tensor(wsel[:, :], xr[:, p, C:ROW],
                                is_expert[:, bass.ds(i, 1), :].rearrange("p a e -> p (a e)"), ALU.mult).then_inc(s_ws, 1)
                dve.wait_ge(s_ws, i + 1)
                V.tensor_reduce(meta[:, p:p + 1], wsel[:, :], X, ALU.add).then_inc(s_meta, 1)

            def vec_slot(m, p, before=None, e=None, now=None, late=None):
                st = isinstance(m, int)
                if before is None:
                    e = expert_of(m - 1) if 0 <= m - 1 < SLOTS else None
                    before = expert_of(m - 2) if m >= 2 else None
                    now = expert_of(m) if m < SLOTS else None
                if not st or 0 <= m - 2 < SLOTS:
                    turned_hidden(m - 2, p)
                if not st or m < SLOTS:
                    turned(m, p, now)
                if e is not None:
                    bias_hidden(m - 1, 1 - p, e)
                if not st or 0 <= m - 2 < SLOTS:
                    finish(m - 2, p, before)
                if not st or m < SLOTS:
                    keep_row_ends(m, p, late)

            for m in range(4):
                vec_slot(m, m % 2)
            with dve.Fori(0, SLOTS // 8 - 1) as g:
                of = experts_of(2 * g + 1), experts_of(2 * g + 2)
                for q in range(8):
                    mine = of[q // 4]
                    vec_slot(8 * g + 4 + q, q % 2, mine[q % 4], mine[q % 4 + 1], mine[q % 4 + 2],
                             g * 64 + (q // 2) * 16 + 48)
            of = experts_of(SLOTS // 4 - 1)
            for q in range(4):
                vec_slot(SLOTS - 4 + q, q % 2, of[q], of[q + 1], of[q + 2])
            vec_slot(SLOTS, 0)
            vec_slot(SLOTS + 1, 1)


NCONST = 28
WPARTS = 4
LOAD_E = 16 * (WPARTS + 1)
NCW = 6
MAGIC = 0x5F3759DF + 1
TAB_STEPS = 26


_NAMES = ["x", "w1t", "w2t", "w3t", "norms", "res_scale", "wqkv", "wout", "bout", "gate_w", "gate_b", "ew1", "ew2", "eb"]


def kernel(x, L0_conv_w1, L0_conv_b1, L0_conv_g1, L0_conv_be1, L0_conv_w2, L0_conv_b2, L0_conv_g2, L0_conv_be2,
           L0_conv_w3, L0_conv_b3, L0_conv_g3, L0_conv_be3, L0_conv_residual_scale, L1_attn_w_qkv, L1_attn_w_out,
           L1_attn_b_out, L1_ffn_gate_w, L1_ffn_gate_b, L1_ffn_w1, L1_ffn_b1, L1_ffn_w2, L1_ffn_b2):
    import numpy as np
    import concourse.bacc as bacc
    from concourse.bass_utils import run_bass_kernel_spmd

    vectors = [[L0_conv_b1, L0_conv_g1, L0_conv_be1], [L0_conv_b2, L0_conv_g2, L0_conv_be2],
               [L0_conv_b3, L0_conv_g3, L0_conv_be3]]
    norms = np.zeros((128, 3, 3, 2), np.float32)
    for n, v in enumerate(vectors[0]):
        norms[0:MID, 0, n, 0] = norms[MID:128, 0, n, 0] = np.asarray(v)
        norms[0:MID, 1, n, 0] = norms[MID:128, 1, n, 0] = np.asarray(vectors[1][n])
    for n, v in enumerate(vectors[2]):
        norms[:, 2, n, :] = np.asarray(v).reshape(2, 128).T
    values = [
        np.asarray(x).reshape(B, C, HW),
        np.asarray(L0_conv_w1).reshape(MID, C).T,
        np.asarray(L0_conv_w2).transpose(2, 3, 1, 0),
        np.asarray(L0_conv_w3).reshape(C, MID).T, norms,
        L0_conv_residual_scale, L1_attn_w_qkv, L1_attn_w_out, L1_attn_b_out,
        L1_ffn_gate_w, L1_ffn_gate_b, L1_ffn_w1, L1_ffn_w2,
        np.concatenate([np.asarray(L1_ffn_b1), np.asarray(L1_ffn_b2)], axis=1),
    ]
    nc = bacc.Bacc("TRN2", target_bir_lowering=False, num_devices=1)
    arrays, args = {}, []
    for name, value in zip(_NAMES, values):
        a = np.ascontiguousarray(value)
        arrays[f"in_{name}"] = a
        args.append(nc.dram_tensor(f"in_{name}", a.shape, mybir.dt.from_np(a.dtype), kind="ExternalInput").ap())
    args.append(nc.dram_tensor("out_0", (TOKENS + 128, C), F32, kind="ExternalOutput").ap())
    moe_block(nc, *args)
    r = run_bass_kernel_spmd(nc, [arrays], core_ids=[0])
    tokens = np.asarray(r.results[0]["out_0"])[:TOKENS]
    return np.ascontiguousarray(tokens.reshape(B, HW, C).transpose(0, 2, 1)).reshape(B, C, SIDE, SIDE)
```
